# Optimizing a Trainium2 kernel written in Bass

```python
import numpy as np
import jax
import jax.numpy as jnp

def _softmax(x, axis=-1):
    return jax.nn.softmax(x, axis=axis)

def _gelu(x):
    return jax.nn.gelu(x, approximate=True)

def _silu(x):
    return jax.nn.silu(x)

def _sigmoid(x):
    return jax.nn.sigmoid(x)

def _layernorm(x, axis=-1, eps=1e-05):
    m = jnp.mean(x, axis=axis, keepdims=True)
    v = jnp.var(x, axis=axis, keepdims=True)
    return (x - m) / jnp.sqrt(v + eps)

def _scatter_add(tgt, idx, src, axis=0):
    return tgt.at[idx].add(src)

def _segment_sum(src, seg, n):
    return jax.ops.segment_sum(src, seg, n)
kernel_name = 'mk_macaron_d1_jaxref_r8_e040f0'

def setup_inputs(seed: int=0):
    np.random.seed(seed)
    _w = jnp.asarray

    def _L0_attn_setup():
        import jax, jax.numpy as jnp
        from jax import lax
        import numpy as np
        DIM = 128
        HEADS = 16
        B, N = (2, 256)

        def sn_dense(x, W, u, sigma_param):
            v = lax.stop_gradient(W @ u)
            v = lax.stop_gradient(v / jnp.linalg.norm(v, ord=2))
            u2 = lax.stop_gradient(W.T @ v)
            u2 = lax.stop_gradient(u2 / jnp.linalg.norm(u2, ord=2))
            sigma = jnp.einsum('c,cd,d->', v, W, u2)
            return x @ (sigma_param[0] / sigma * W)
        key = jax.random.key(seed)
        ks = jax.random.split(key, 5)
        std = 0.1
        batch = jax.random.normal(ks[0], (B, N, DIM), dtype=jnp.float32)
        W_qkv = jax.random.normal(ks[1], (DIM, 3 * DIM), dtype=jnp.float32) * std
        W_proj = jax.random.normal(ks[2], (DIM, DIM), dtype=jnp.float32) * std
        u_qkv = jax.random.normal(ks[3], (3 * DIM,), dtype=jnp.float32)
        u_qkv = u_qkv / jnp.linalg.norm(u_qkv)
        u_proj = jax.random.normal(ks[4], (DIM,), dtype=jnp.float32)
        u_proj = u_proj / jnp.linalg.norm(u_proj)
        sigma_qkv = jnp.ones((1,), dtype=jnp.float32)
        sigma_proj = jnp.ones((1,), dtype=jnp.float32)
        return {'batch': batch, 'W_qkv': W_qkv, 'u_qkv': u_qkv, 'sigma_qkv': sigma_qkv, 'W_proj': W_proj, 'u_proj': u_proj, 'sigma_proj': sigma_proj}
    _L0_attn_in = _L0_attn_setup()

    def _L0_ffn_setup():
        import jax, jax.numpy as jnp
        import numpy as np
        B, S, D, E, F = (4, 256, 128, 8, 512)
        MIN_CAPACITY = 4

        def _make_waff():
            g = D // E
            scale = E / D
            w = np.zeros((E, D), np.float32)
            for i in range(E):
                w[i, i * g:(i + 1) * g] = scale
            return jnp.asarray(w)
        key = jax.random.key(seed)
        ks = jax.random.split(key, 6)
        inputs = jax.random.normal(ks[0], (B, S, D), dtype=jnp.float32)
        W1 = jax.random.normal(ks[1], (E, D, F), dtype=jnp.float32) * (1.0 / np.sqrt(D))
        b1 = jnp.zeros((E, F), dtype=jnp.float32)
        W2 = jax.random.normal(ks[2], (E, F, D), dtype=jnp.float32) * (1.0 / np.sqrt(F))
        b2 = jnp.zeros((E, D), dtype=jnp.float32)
        return {'inputs': inputs, 'waff': _make_waff(), 'W1': W1, 'b1': b1, 'W2': W2, 'b2': b2, 'affinity_threshold': jnp.float32(0.5)}
    _L0_ffn_in = _L0_ffn_setup()
    _d = {'L0_attn_batch': _L0_attn_in['batch'], 'L0_attn_W_qkv': _L0_attn_in['W_qkv'], 'L0_attn_u_qkv': _L0_attn_in['u_qkv'], 'L0_attn_sigma_qkv': _L0_attn_in['sigma_qkv'], 'L0_attn_W_proj': _L0_attn_in['W_proj'], 'L0_attn_u_proj': _L0_attn_in['u_proj'], 'L0_attn_sigma_proj': _L0_attn_in['sigma_proj'], 'L0_ffn_waff': _L0_ffn_in['waff'], 'L0_ffn_W1': _L0_ffn_in['W1'], 'L0_ffn_b1': _L0_ffn_in['b1'], 'L0_ffn_W2': _L0_ffn_in['W2'], 'L0_ffn_b2': _L0_ffn_in['b2'], 'L0_ffn_affinity_threshold': _L0_ffn_in['affinity_threshold']}
    _x0 = _d['L0_attn_batch']
    _d['L0_attn_batch'] = jax.random.normal(jax.random.fold_in(jax.random.key(seed), 1), (32, 256, 128), dtype=_x0.dtype)
    del _x0
    return _d

def reference(L0_attn_batch, L0_attn_W_qkv, L0_attn_u_qkv, L0_attn_sigma_qkv, L0_attn_W_proj, L0_attn_u_proj, L0_attn_sigma_proj, L0_ffn_waff, L0_ffn_W1, L0_ffn_b1, L0_ffn_W2, L0_ffn_b2, L0_ffn_affinity_threshold):

    def _L0_attn_ref(batch, W_qkv, u_qkv, sigma_qkv, W_proj, u_proj, sigma_proj):
        import jax, jax.numpy as jnp
        from jax import lax
        import numpy as np
        DIM = 128
        HEADS = 16
        B, N = (2, 256)

        def sn_dense(x, W, u, sigma_param):
            v = lax.stop_gradient(W @ u)
            v = lax.stop_gradient(v / jnp.linalg.norm(v, ord=2))
            u2 = lax.stop_gradient(W.T @ v)
            u2 = lax.stop_gradient(u2 / jnp.linalg.norm(u2, ord=2))
            sigma = jnp.einsum('c,cd,d->', v, W, u2)
            return x @ (sigma_param[0] / sigma * W)
        b, n, d = batch.shape
        h = HEADS
        hd = d // h
        qkv = sn_dense(batch, W_qkv, u_qkv, sigma_qkv)
        q, k, v = jnp.split(qkv, 3, axis=-1)
        split_heads = lambda t: t.reshape(b, n, h, hd).transpose(0, 2, 1, 3)
        q, k, v = (split_heads(q), split_heads(k), split_heads(v))
        scale = hd ** (-0.5)
        att = jnp.einsum('bhqd,bhkd->bhqk', q, k) * scale
        causal = jnp.tril(jnp.ones((n, n), dtype=jnp.float32))
        big_neg = jnp.finfo(att.dtype).min
        att = jnp.where(causal[None, None] == 0, big_neg, att)
        att = jax.nn.softmax(att, axis=-1)
        x = jnp.einsum('bhqk,bhkd->bhqd', att, v)
        x = x.transpose(0, 2, 1, 3).reshape(b, n, d)
        x = sn_dense(x, W_proj, u_proj, sigma_proj)
        return x

    def _L0_ffn_ref(inputs, waff, W1, b1, W2, b2, affinity_threshold):
        import jax, jax.numpy as jnp
        import numpy as np
        B, S, D, E, F = (4, 256, 128, 8, 512)
        MIN_CAPACITY = 4

        def _make_waff():
            g = D // E
            scale = E / D
            w = np.zeros((E, D), np.float32)
            for i in range(E):
                w[i, i * g:(i + 1) * g] = scale
            return jnp.asarray(w)
        num = jnp.einsum('bsd,ed->bse', inputs, waff)
        x_norm = jnp.linalg.norm(inputs, axis=-1, keepdims=True)
        w_norm = jnp.linalg.norm(waff, axis=-1)
        aff = num / (x_norm * w_norm[None, None, :] + 1e-09)
        router_probs = jax.nn.softmax(aff, axis=-1)
        cap = jnp.floor(S * jax.nn.sigmoid(aff.mean() - affinity_threshold)).astype(jnp.int32)
        cap = jnp.minimum(jnp.maximum(cap, MIN_CAPACITY), S)
        tcr = jax.nn.one_hot(jnp.argmax(router_probs, axis=-1), E, dtype=inputs.dtype)
        order = jnp.argsort(-aff, axis=1)
        ranks = jnp.argsort(order, axis=1)
        ecr = (ranks < cap).astype(inputs.dtype)
        dispatch = tcr * ecr
        masks = jnp.moveaxis(dispatch, -1, 0)

        def body(acc, expert):
            W1e, b1e, W2e, b2e, me = expert
            xi = inputs * me[..., None]
            h = jax.nn.gelu(xi @ W1e + b1e, approximate=False)
            return (acc + (h @ W2e + b2e), None)
        out, _ = jax.lax.scan(body, jnp.zeros_like(inputs), (W1, b1, W2, b2, masks))
        return out
    x = L0_attn_batch
    x = x + 0.5 * _L0_ffn_ref(_layernorm(x, axis=-1), L0_ffn_waff, L0_ffn_W1, L0_ffn_b1, L0_ffn_W2, L0_ffn_b2, L0_ffn_affinity_threshold)
    x = x + _L0_attn_ref(_layernorm(x, axis=-1), L0_attn_W_qkv, L0_attn_u_qkv, L0_attn_sigma_qkv, L0_attn_W_proj, L0_attn_u_proj, L0_attn_sigma_proj)
    x = x + 0.5 * _L0_ffn_ref(_layernorm(x, axis=-1), L0_ffn_waff, L0_ffn_W1, L0_ffn_b1, L0_ffn_W2, L0_ffn_b2, L0_ffn_affinity_threshold)
    return x

_drawn_inputs = setup_inputs


def setup_inputs(seed=0):
    import zlib

    import numpy as np

    out = dict(_drawn_inputs(seed))
    spreads = {'L0_ffn_b1': (0.0, 0.1), 'L0_ffn_b2': (0.0, 0.1)}
    factors = {}
    for name, (base, spread) in spreads.items():
        noise = np.random.default_rng([zlib.crc32(name.encode()), seed]).standard_normal(out[name].shape)
        drawn = base * np.exp(spread * noise) if base else spread * noise
        out[name] = jnp.asarray(drawn.astype(out[name].dtype))
    for name, factor in factors.items():
        out[name] = (out[name] * factor).astype(out[name].dtype)
    return out
```

```python
import numpy as np
import concourse.bass as bass
from concourse import mybir
from contextlib import ExitStack

F32 = mybir.dt.float32
BF16 = mybir.dt.bfloat16
I32 = mybir.dt.int32
ALU = mybir.AluOpType
ACT = mybir.ActivationFunctionType
AX = mybir.AxisListType

P = 128
D = 128
E, F = 8, 512
FC = F // P
B, S = 32, 256
TPB = S // P
T = B * S
NT = T // P
G = E + 1
NS = NT + G - 1
U = 8
BANK = 512
NSX = NS + U
XW = D + 4
H, HD = 16, 8
MAGIC = 1.5 * 2 ** 23
LN_EPS = 1e-5
TIE = -1e-37


def ds(start, n):
    return bass.ds(start, n)


class Mem:

    def __init__(self, nc, ctx):
        self.nc, self.ctx, self.sems = nc, ctx, []
        ctx.callback(self.clear)

    def clear(self):
        if self.sems:
            for n in range(min(self.sems), max(self.sems) + 1):
                if n in self.sems and n - 1 not in self.sems:
                    end = n
                    while end in self.sems:
                        end += 1
                    self.nc.gpsimd.sem_clear(range(n, end))
            self.nc.all_engine_barrier()

    def sb(self, name, shape, dt=F32):
        return self.ctx.enter_context(self.nc.sbuf_tensor(name, shape, dt))

    def ps(self, name, shape, dt=F32):
        size = int(np.prod(shape[1:]))
        whole = self.ctx.enter_context(self.nc.psum_tensor(name, [P, -(-size // BANK) * BANK], dt))
        out = whole[:, 0:size]
        return out if len(shape) == 2 else out.rearrange("p (a b) -> p a b", a=shape[1])

    def sem(self, name):
        sem = self.ctx.enter_context(self.nc.semaphore(name))
        self.sems.append(sem.num)
        return sem


class Steps:

    def __init__(self, engine, sem):
        self.engine, self.sem, self.n = engine, sem, 0

    def step(self, ins):
        self.n += 1
        ins.then_inc(self.sem, 1)
        self.engine.wait_ge(self.sem, self.n)


def preamble(nc, m, io, c):
    ctx = ExitStack()
    with ctx:
        t = Mem(nc, ctx)
        waff_n = t.sb("waff_n", [E, D])
        b1_chunks = t.sb("b1_chunks", [E * FC, P])
        b1_rows = t.sb("b1_rows", [E, F])
        b1_rest = t.sb("b1_rest", [E, F])
        b1_parts = t.sb("b1_parts", [E, 3, F], BF16)
        gelu_b1 = t.sb("gelu_b1", [P, E * FC])
        const_row = t.sb("const_row", [1, G, D])
        b2_row = t.sb("b2_row", [1, E, D])
        sum_row = t.sb("sum_row", [1, D])
        rest_row = t.sb("rest_row", [1, G, D])
        const_parts = t.sb("const_parts", [1, 3, G * D], BF16)
        w_raw = [t.sb("wqkv_raw", [P, 3 * D]), t.sb("wproj_raw", [P, D])]
        u_row = [t.sb("uqkv_row", [P, 3 * D]), t.sb("uproj_row", [P, D])]
        sig = t.sb("sig", [P, 2])
        prod = t.sb("prod", [P, 3 * D])
        u2 = t.sb("u2", [P, 3 * D])
        v_bc = t.sb("v_bc", [P, P])
        col = t.sb("col", [P, 16])
        sq = t.sb("sq", [P, E])
        half = t.sb("half", [P, E])
        mhalf = t.sb("mhalf", [P, 1])
        iota_i = t.sb("iota_i", [P, P], I32)
        part_i = t.sb("part_i", [P, 1], I32)
        tile_i = t.sb("tile_i", [P, NT], I32)
        down_i = t.sb("down_i", [P, E], I32)
        pm = [t.ps(f"pre{i}", [P, 512]) for i in range(8)]

        w_in, w_ffn, parts_out = t.sem("w_in"), t.sem("w_ffn"), t.sem("parts_out")
        made, ints = t.sem("made"), t.sem("ints")
        small_t, small_e = t.sem("small_t"), t.sem("small_e")
        b1_t, b1_g, k_done = t.sem("b1_t"), t.sem("b1_g"), t.sem("k_done")
        b1_split, const_split = t.sem("b1_split"), t.sem("const_split")
        wn_sum, wn_sq, pows = t.sem("wn_sum"), t.sem("wn_sq"), t.sem("pows")
        ask, told, vstep = t.sem("ask"), t.sem("told"), t.sem("vstep")
        powask = t.sem("powask")
        pstep = t.sem("pstep")
        blk = ctx.enter_context(nc.Block())
        N_SMALL = 11

        @blk.sync
        def _(sp):
            for dst, src in [
                (waff_n[:, :], io["waff"]),
                (b1_chunks[:, :], io["b1"].rearrange("e (c p) -> (e c) p", p=P)),
                (b1_rows[:, :], io["b1"]),
                (b2_row[:, :, :], io["b2"].rearrange("(a e) d -> a e d", a=1)),
                (w_raw[0][:, :], io["wqkv"]),
                (w_raw[1][:, :], io["wproj"]),
                (u_row[0][:, :], io["uqkv"].partition_broadcast(P)),
                (u_row[1][:, :], io["uproj"].partition_broadcast(P)),
                (sig[:, 0:1], io["sqkv"].partition_broadcast(P)),
                (sig[:, 1:2], io["sproj"].partition_broadcast(P)),
                (c.thr[:, :], io["thr"].partition_broadcast(P)),
            ]:
                sp.dma_start(dst, src).then_inc(w_in, 16)
            sp.dma_start(c.w2[:, 0:E, :, :], io["w2"].rearrange("e (c p) d -> p e c d", p=P)).then_inc(w_ffn, 16)
            sp.dma_start(c.w1[:, 0:E, :], io["w1"].rearrange("e d f -> d e f")).then_inc(w_ffn, 16)
            sp.wait_ge(made, 18)
            sp.wait_ge(b1_split, 3)
            for r in range(3):
                for e in range(E):
                    sp.dma_start(c.b1s[r:r + 1, e, :], b1_parts[e:e + 1, r, :]).then_inc(parts_out, 16)
            sp.wait_ge(const_split, 3)
            for r in range(3):
                sp.dma_start(c.cst[r:r + 1, :, :].rearrange("a g d -> a (g d)"), const_parts[0:1, r, :]).then_inc(parts_out, 16)
            sp.wait_ge(parts_out, 16 * 3 * (E + 1))
            sp.wait_ge(w_ffn, 32)

        @blk.gpsimd
        def _(pool):
            g = nc.gpsimd
            st = Steps(pool, made)
            g.memset(half[:, :], 0.5).then_inc(made, 1)
            g.memset(mhalf[:, :], -0.5).then_inc(made, 1)
            g.memset(c.ident[:, :], 0.0).then_inc(made, 1)
            g.memset(c.identb[:, :], 0.0).then_inc(made, 1)
            g.memset(c.ones[:, :], 1.0).then_inc(made, 1)
            g.memset(c.onesb[:, :], 1.0).then_inc(made, 1)
            g.memset(c.tri[:, :], 1.0).then_inc(made, 1)
            g.memset(c.tie[:, :, :], 0.0).then_inc(made, 1)
            g.memset(c.mask[:, :, :], 0.0).then_inc(made, 1)
            g.memset(c.b1s[:, :, :], 0.0).then_inc(made, 1)
            g.memset(c.cst[:, :, :], 0.0).then_inc(made, 1)
            g.memset(c.w1[:, E, :], 0.0).then_inc(made, 1)
            g.memset(c.w2[:, E, :, :], 0.0).then_inc(made, 1)
            pool.wait_ge(made, 13)
            for eye in (c.ident, c.identb):
                g.affine_select(out=eye[:, :], in_=eye[:, :], compare_op=ALU.not_equal, fill=1.0,
                                base=0, pattern=[[-1, P]], channel_multiplier=1).then_inc(made, 1)
            g.affine_select(out=c.tri[:, :], in_=c.tri[:, :], compare_op=ALU.is_gt, fill=0.0,
                            base=0, pattern=[[1, P]], channel_multiplier=-1).then_inc(made, 1)
            g.affine_select(out=c.tie[:, :, :], in_=c.tie[:, :, :], compare_op=ALU.is_ge, fill=TIE,
                            base=0, pattern=[[-P, TPB], [1, S]], channel_multiplier=-1).then_inc(made, 1)
            g.affine_select(out=c.mask[:, :, :], in_=c.mask[:, :, :], compare_op=ALU.is_ge, fill=-3e38,
                            base=0, pattern=[[0, 4], [-1, P]], channel_multiplier=1).then_inc(made, 1)
            g.iota(iota_i[:, :], pattern=[[1, P]], base=0, channel_multiplier=0).then_inc(ints, 1)
            g.iota(part_i[:, :], pattern=[[0, 1]], base=0, channel_multiplier=1).then_inc(ints, 1)
            g.iota(tile_i[:, :], pattern=[[1, NT]], base=1, channel_multiplier=0).then_inc(ints, 1)
            g.iota(down_i[:, :], pattern=[[-1, E]], base=E, channel_multiplier=0).then_inc(ints, 1)
            pool.wait_ge(powask, 1)
            g.tensor_tensor(c.wnorm[:, :], sq[:, :], half[:, :], ALU.pow).then_inc(pows, 1)
            for k in range(4):
                pool.wait_ge(powask, k + 2)
                g.tensor_tensor(col[:, 8 + k:9 + k], col[:, 4 + k:5 + k], mhalf[:, :], ALU.pow).then_inc(pows, 1)

        @blk.scalar
        def _(act):
            act.wait_ge(b1_t, 1)
            nc.scalar.activation(gelu_b1[:, :], pm[0][:, 0:E * FC], ACT.Gelu).then_inc(b1_g, 1)

        @blk.tensor
        def _(pe):
            pe.wait_ge(w_in, 16 * N_SMALL)
            pe.wait_ge(made, 18)
            nc.tensor.transpose(pm[0][:, 0:E * FC], b1_chunks[:, :], c.ident[0:E * FC, 0:E * FC]).then_inc(b1_t, 1)
            nc.tensor.transpose(pm[1][:, 0:E], waff_n[:, :], c.ident[0:E, 0:E]).then_inc(small_t, 1)
            pe.wait_ge(b1_g, 1)
            pe.wait_ge(w_ffn, 32)
            for e in range(E):
                for k in range(FC):
                    last = nc.tensor.matmul(pm[2 + e // 4][0:1, (e % 4) * D:(e % 4 + 1) * D],
                                            gelu_b1[:, e * FC + k:e * FC + k + 1], c.w2[:, e, k, :],
                                            start=(k == 0), stop=(k == FC - 1))
            last.then_inc(k_done, 1)
            pe.wait_ge(ask, 1)
            nc.tensor.matmul(pm[1][:, 16:16 + E], c.ones[:, :], sq[:, :], start=True, stop=True).then_inc(told, 1)
            for w, n in enumerate((3 * D, D)):
                pe.wait_ge(ask, 2 + 3 * w)
                nc.tensor.matmul(pm[4][:, 0:1], c.ones[:, :], col[:, 2:3], start=True, stop=True).then_inc(told, 1)
                pe.wait_ge(ask, 3 + 3 * w)
                nc.tensor.matmul(pm[5][:, 0:n], v_bc[:, :], w_raw[w][:, :], start=True, stop=True).then_inc(told, 1)
                pe.wait_ge(ask, 4 + 3 * w)
                nc.tensor.matmul(pm[4][:, 0:1], c.ones[:, :], col[:, 2:3], start=True, stop=True).then_inc(told, 1)

        @blk.vector
        def _(dve):
            v = nc.vector
            s = Steps(dve, vstep)
            dve.wait_ge(ints, 4)
            for dst, src in ((c.iota[:, :], iota_i[:, :]), (c.part[:, :], part_i[:, :]),
                             (c.tile1[:, :], tile_i[:, :]), (c.down[:, :], down_i[:, :])):
                s.step(v.tensor_copy(dst, src))
            dve.wait_ge(w_in, 16 * N_SMALL)
            for r in range(3):
                s.step(v.tensor_copy(b1_parts[:, r, :], b1_rows[:, :] if r == 0 else b1_rest[:, :]))
                b1_split_now = v.tensor_tensor(b1_rest[:, :], b1_rows[:, :] if r == 0 else b1_rest[:, :],
                                               b1_parts[:, r, :], ALU.subtract)
                b1_split_now.then_inc(b1_split, 1)
                dve.wait_ge(b1_split, r + 1)
            dve.wait_ge(small_t, 1)
            s.step(v.tensor_copy(c.waff_t[:, :], pm[1][:, 0:E]))
            v.tensor_tensor(sq[:, :], c.waff_t[:, :], c.waff_t[:, :], ALU.mult).then_inc(ask, 1)
            dve.wait_ge(told, 1)
            v.tensor_copy(sq[:, :], pm[1][:, 16:16 + E]).then_inc(powask, 1)
            dve.wait_ge(pows, 1)
            for w, n in enumerate((3 * D, D)):
                s.step(v.tensor_tensor(prod[:, 0:n], w_raw[w][:, :], u_row[w][:, :], ALU.mult))
                s.step(v.tensor_reduce(col[:, 0:1], prod[:, 0:n], axis=AX.X, op=ALU.add))
                v.tensor_tensor(col[:, 2:3], col[:, 0:1], col[:, 0:1], ALU.mult).then_inc(ask, 1)
                dve.wait_ge(told, 2 + 3 * w)
                v.tensor_copy(col[:, 4 + 2 * w:5 + 2 * w], pm[4][:, 0:1]).then_inc(powask, 1)
                dve.wait_ge(pows, 2 + 2 * w)
                s.step(v.tensor_tensor(col[:, 1:2], col[:, 0:1], col[:, 8 + 2 * w:9 + 2 * w], ALU.mult))
                v.tensor_scalar(v_bc[:, :], c.ones[:, :], col[:, 1:2], None, ALU.mult).then_inc(ask, 1)
                dve.wait_ge(told, 3 + 3 * w)
                s.step(v.tensor_copy(u2[:, 0:n], pm[5][:, 0:n]))
                s.step(v.tensor_tensor(prod[:, 0:n], u2[:, 0:n], u2[:, 0:n], ALU.mult))
                v.tensor_reduce(col[:, 5 + 2 * w:6 + 2 * w], prod[:, 0:n], axis=AX.X, op=ALU.add).then_inc(powask, 1)
                dve.wait_ge(pows, 3 + 2 * w)
                s.step(v.tensor_scalar(u2[:, 0:n], u2[:, 0:n], col[:, 9 + 2 * w:10 + 2 * w], None, ALU.mult))
                s.step(v.tensor_tensor(prod[:, 0:n], w_raw[w][:, :], u2[:, 0:n], ALU.mult))
                s.step(v.tensor_reduce(col[:, 3:4], prod[:, 0:n], axis=AX.X, op=ALU.add))
                v.tensor_tensor(col[:, 2:3], col[:, 3:4], col[:, 1:2], ALU.mult).then_inc(ask, 1)
                dve.wait_ge(told, 4 + 3 * w)
                s.step(v.reciprocal(col[:, 12:13], pm[4][:, 0:1]))
                s.step(v.tensor_tensor(col[:, 13:14], col[:, 12:13], sig[:, w:w + 1], ALU.mult))
                if w == 0:
                    for i, out in enumerate((c.wq, c.wk)):
                        s.step(v.tensor_scalar(out[:, :].rearrange("p (r d g) -> p r d g", r=2, d=HD),
                                               w_raw[0][:, i * D:(i + 1) * D].rearrange("p (g r d) -> p r d g", r=2, d=HD),
                                               col[:, 13:14], None, ALU.mult))
                    s.step(v.tensor_scalar(c.wv[:, :], w_raw[0][:, 2 * D:3 * D], col[:, 13:14], None, ALU.mult))
                else:
                    s.step(v.tensor_scalar(c.wproj[:, :], w_raw[1][:, :], col[:, 13:14], None, ALU.mult))
            dve.wait_ge(k_done, 1)
            k_row = const_row[:, 0:E, :]
            for h in range(2):
                s.step(v.tensor_copy(const_row[:, 4 * h:4 * h + 4, :].rearrange("a e d -> a (e d)"), pm[2 + h][0:1, :]))
            s.step(v.tensor_tensor(b2_row[:, :, :], b2_row[:, :, :], k_row, ALU.add))
            s.step(v.tensor_reduce(sum_row[:, :], b2_row[:, :, :].rearrange("a e d -> a d e"), axis=AX.X, op=ALU.add))
            s.step(v.tensor_scalar(k_row, k_row, -1.0, None, ALU.mult))
            s.step(v.memset(const_row[:, E, :], 0.0))
            s.step(v.tensor_tensor(const_row[:, :, :], const_row[:, :, :],
                                   sum_row[:, :].unsqueeze(1).to_broadcast([1, G, D]), ALU.add))
            flat = const_row[:, :, :].rearrange("a g d -> a (g d)")
            rest = rest_row[:, :, :].rearrange("a g d -> a (g d)")
            for r in range(3):
                s.step(v.tensor_copy(const_parts[:, r, :], flat if r == 0 else rest))
                v.tensor_tensor(rest, flat if r == 0 else rest, const_parts[:, r, :], ALU.subtract).then_inc(const_split, 1)
                dve.wait_ge(const_split, r + 1)


def token_stats(nc, m, io, c, x_dram):
    ctx = ExitStack()
    with ctx:
        t = Mem(nc, ctx)
        NX = 4
        XCREDIT = NX * TPB
        CREDIT = 2 * TPB
        x_row = [t.sb(f"ts_x{k}", [P, TPB, XW]) for k in range(NX)]
        bn = t.sb("ts_bn", [P, 2, TPB, 6])
        vare = t.sb("ts_vare", [P, 2, TPB])
        xn = [t.sb(f"ts_xn{k}", [P, TPB, D]) for k in range(2)]
        xn_t = [t.sb(f"ts_xnt{k}", [P, S]) for k in range(2)]
        mhalf = t.sb("ts_mhalf", [P, TPB])
        p_t = [t.ps(f"ts_pt{k}", [P, S]) for k in range(2)]
        p_n = [t.ps(f"ts_pn{k}", [P, TPB, E]) for k in range(2)]
        x_in = [t.sem(f"ts_in{k}") for k in range(NX)]
        x_out = [t.sem(f"ts_out{k}") for k in range(NX)]
        pad, bn_done, mv_done, var_done, rstd = t.sem("ts_pad"), t.sem("ts_bnd"), t.sem("ts_mv"), t.sem("ts_var"), t.sem("ts_rstd")
        xn_done, tr, tr_out, num, num_out = t.sem("ts_xnd"), t.sem("ts_tr"), t.sem("ts_tro"), t.sem("ts_num"), t.sem("ts_numo")
        passed = t.sem("ts_passed")
        blk = ctx.enter_context(nc.Block())
        x_v = x_dram.rearrange("(b k p) d -> p b k d", k=TPB, p=P)
        row_v = io["rows"].rearrange("(b k p) w -> p b k w", k=TPB, p=P)

        @blk.sync
        def _(sp):
            with sp.Fori(0, B // NX) as i:
                for k in range(NX):
                    b = i * NX + k
                    sp.wait_ge(x_out[k], i * 16)
                    sp.wait_ge(xn_done, b * TPB + TPB)
                    sp.dma_start(x_row[k][:, :, 0:D], x_v[:, ds(b, 1), :, :]).then_inc(x_in[k], 16)

        @blk.gpsimd
        def _(pool):
            nc.gpsimd.memset(mhalf[:, :], -0.5).then_inc(pad, 1)
            for k in range(NX):
                nc.gpsimd.memset(x_row[k][:, :, D + 2:XW], 0.0).then_inc(pad, 1)
            pool.wait_ge(pad, NX + 1)
            with pool.Fori(0, B // NX) as i:
                for k in range(NX):
                    b = i * NX + k
                    pool.wait_ge(var_done, b + 1)
                    nc.gpsimd.tensor_tensor(x_row[k][:, :, D + 1], vare[:, k % 2, :], mhalf[:, :], ALU.pow).then_inc(rstd, 1)

        @blk.scalar
        def _(act):
            act.wait_ge(pad, NX + 1)
            with act.Fori(0, B // NX) as i:
                for k in range(NX):
                    b = i * NX + k
                    act.wait_ge(rstd, b + 1)
                    act.dma_start(row_v[:, ds(b, 1), :, :], x_row[k][:, :, :]).then_inc(x_out[k], 16)
                    act.wait_ge(tr, b * TPB + TPB + CREDIT)
                    nc.scalar.activation(xn_t[k % 2][:, :], p_t[k % 2][:, :], ACT.Copy).then_inc(tr_out, 1)
                    act.wait_ge(num, b + 1)
                    nc.scalar.activation(c.num[:, ds(b * TPB, TPB), :], p_n[k % 2][:, :, :], ACT.Copy).then_inc(num_out, 1)
            for k in range(NX):
                act.wait_ge(x_out[k], 16 * (B // NX))

        @blk.vector
        def _(dve):
            v = nc.vector

            def stats(b, k):
                q = k % 2
                dve.wait_ge(x_in[k], b * (16 // NX) + (16 - k * (16 // NX)))
                dve.wait_ge(mv_done, b * TPB)
                for j in range(TPB):
                    v.bn_stats(bn[:, q, j, :], x_row[k][:, j, 0:D]).then_inc(bn_done, 1)
                for j in range(TPB):
                    dve.wait_ge(bn_done, b * TPB + (j + 1))
                    dve.sem_inc(passed, 1)
                    v.bn_aggr(x_row[k][:, j, D:D + 2], bn[:, q, j, :]).then_inc(mv_done, 1)
                dve.wait_ge(mv_done, b * TPB + TPB)
                v.tensor_copy(c.var[:, ds(b * TPB, TPB)], x_row[k][:, :, D + 1])
                v.tensor_scalar(vare[:, q, :], x_row[k][:, :, D + 1], LN_EPS, None, ALU.add).then_inc(var_done, 1)

            def norm(b, k):
                dve.wait_ge(rstd, b + 1)
                dve.wait_ge(tr, b * TPB + TPB)
                for j in range(TPB):
                    v.tensor_scalar(xn[k % 2][:, j, :], x_row[k][:, j, 0:D], x_row[k][:, j, D:D + 1],
                                    x_row[k][:, j, D + 1:D + 2], ALU.subtract, ALU.mult).then_inc(xn_done, 1)

            dve.sem_inc(xn_done, XCREDIT)
            stats(0, 0)
            with dve.Fori(0, B // NX - 1) as i:
                for k in range(NX):
                    stats(i * NX + (k + 1), (k + 1) % NX)
                    norm(i * NX + k, k)
            for k in range(NX):
                if k + 1 < NX:
                    stats(B - NX + k + 1, k + 1)
                norm(B - NX + k, k)

        @blk.tensor
        def _(pe):
            pe.sem_inc(tr, CREDIT)
            with pe.Fori(0, B // NX) as i:
                for k in range(NX):
                    b = i * NX + k
                    q = k % 2
                    for j in range(TPB):
                        pe.wait_ge(xn_done, b * TPB + (j + 1 + XCREDIT))
                        nc.tensor.transpose(p_t[q][:, j * P:(j + 1) * P], xn[q][:, j, :], c.ident[:, :]).then_inc(tr, 1)
                    pe.wait_ge(tr_out, b + 1)
                    for j in range(TPB):
                        last = nc.tensor.matmul(p_n[q][:, j, :], xn_t[q][:, j * P:(j + 1) * P], c.waff_t[:, :],
                                                start=True, stop=True)
                    last.then_inc(num, 1)


def consts(nc, m):
    class C:
        pass
    c = C()
    c.ident, c.ones = m.sb("ident", [P, P]), m.sb("ones", [P, P])
    c.identb, c.onesb, c.tri = (m.sb(n, [P, P], BF16) for n in ("identb", "onesb", "tri"))
    c.tie = m.sb("tie", [P, TPB, S])
    c.mask = m.sb("mask", [P, 4, P], BF16)
    c.iota, c.part, c.tile1, c.down = m.sb("iota", [P, P]), m.sb("part", [P, 1]), m.sb("tile1", [P, NT]), m.sb("down", [P, E])
    c.w1, c.w2 = m.sb("w1", [P, G, F]), m.sb("w2", [P, G, FC, D])
    c.b1s, c.cst = m.sb("b1s", [P, G, F], BF16), m.sb("cst", [P, G, D], BF16)
    c.waff_t, c.wnorm, c.thr = m.sb("waff_t", [P, E]), m.sb("wnorm", [P, E]), m.sb("thr", [P, 1])
    c.wq, c.wk, c.wv, c.wproj = (m.sb(n, [P, D]) for n in ("wq", "wk", "wv", "wproj"))
    c.num, c.var = m.sb("num", [P, NT, E]), m.sb("var", [P, NT])
    c.gidx, c.sidx = m.sb("gidx", [P, NSX], I32), m.sb("sidx", [P, NSX], I32)
    c.eid = m.sb("eid", [1, NSX], I32)
    return c


def route(nc, m, c, tag):
    ctx = ExitStack()
    with ctx:
        t = Mem(nc, ctx)

        def sb(name, shape, dt=F32):
            return t.sb(f"{tag}_{name}", shape, dt)

        def sem(name):
            return t.sem(f"{tag}_{name}")

        GT = G * NT
        xnorm2, xnorm, half = sb("xnorm2", [P, NT]), sb("xnorm", [P, NT]), sb("half", [P, NT])
        rec, den = sb("rec", [P, NT]), sb("den", [P, NT, E])
        both = sb("both", [P, NT, 2 * E])
        aff, hot = both[:, :, 0:E], both[:, :, E:2 * E]
        amax, wmax, weight = sb("amax", [P, NT]), sb("wmax", [P, NT]), sb("weight", [P, NT, E])
        cell = sb("cell", [P, 8])
        batch_s = [sb(f"batch{k}", [P, TPB, 2 * E]) for k in range(2)]
        batch_t = [sb(f"batcht{k}", [P, 2 * S]) for k in range(2)]
        beats = [sb(f"beats{k}", [P, S]) for k in range(2)]
        rank, kept = sb("rank", [P, NT]), sb("kept", [P, NT])
        taken = sb("taken", [P, G, NT], BF16)
        total, upto = sb("total", [P, GT]), sb("upto", [P, GT])
        one_row = sb("one_row", [P, GT])
        ends, count, tiles, tile_end, start, shift = (sb(n, [P, G]) for n in ("ends", "count", "tiles", "tend", "start", "shift"))
        place, slot, row, colp = sb("place", [P, GT]), sb("slot", [P, NT]), sb("row", [P, NT]), sb("colp", [P, NT])
        eid_f = [sb(f"eidf{k}", [P, NSX]) for k in range(2)]
        NR = 4
        at_p = [sb(f"atp{k}", [P, P], BF16) for k in range(NR)]
        at_t = [sb(f"att{k}", [P, 2, NS], BF16) for k in range(NR)]
        zero = sb("zero", [P, 2 * NS], BF16)
        lo, src, gsrc, away = sb("lo", [P, NS]), sb("src", [P, NS]), sb("gsrc", [P, NS]), sb("away", [P, NS])
        ps_sum = t.ps(f"{tag}_ps_sum", [P, 1])
        ps_t = [t.ps(f"{tag}_ps_t{k}", [P, 2 * S]) for k in range(2)]
        ps_b = [t.ps(f"{tag}_ps_b{k}", [P, TPB, S]) for k in range(2)]
        ps_pre = [t.ps(f"{tag}_ps_pre{k}", [P, 512]) for k in range(2)]
        ps_inv = t.ps(f"{tag}_ps_inv", [P, 2 * NS])

        sq_ask, sq_got = sem("sq_ask"), sem("sq_got")
        vs, made = sem("vs"), sem("made")
        sum_ask, sum_got, e_ask, e_got = sem("sum_ask"), sem("sum_got"), sem("e_ask"), sem("e_got")
        hot_done, cut, tr, tr_out, row_b, ranked = (sem(n) for n in ("hot", "cut", "tr", "tro", "rowb", "ranked"))
        taken_done, counted, copied = sem("taken_done"), sem("counted"), sem("copied")
        onehot, put, inv = sem("onehot"), sem("put"), sem("inv")
        blk = ctx.enter_context(nc.Block())
        TR_CREDIT = 4
        ROW_CREDIT = 2
        HB = GT // 2

        @blk.gpsimd
        def _(pool):
            nc.gpsimd.memset(half[:, :], 0.5).then_inc(made, 1)
            for k in range(2):
                nc.gpsimd.memset(batch_t[k][:, :], 0.0).then_inc(made, 1)
            nc.gpsimd.memset(zero[:, :], 0.0).then_inc(made, 1)
            nc.gpsimd.memset(one_row[:, :], 1.0).then_inc(made, 1)
            nc.gpsimd.memset(c.gidx[:, NS:NSX], 0).then_inc(made, 1)
            nc.gpsimd.memset(c.sidx[:, NS:NSX], 0).then_inc(made, 1)
            pool.wait_ge(made, 7)
            pool.wait_ge(sq_ask, 1)
            nc.gpsimd.tensor_tensor(xnorm[:, :], xnorm2[:, :], half[:, :], ALU.pow).then_inc(sq_got, 1)

        @blk.scalar
        def _(act):
            act.wait_ge(e_ask, 1)
            nc.scalar.activation(cell[:, 2:3], cell[:, 1:2], ACT.Exp, scale=-1.0).then_inc(e_got, 1)
            act.wait_ge(hot_done, 1)
            act.wait_ge(made, 7)
            with act.Fori(0, B // 2) as i:
                for k in range(2):
                    b = i * 2 + k
                    act.wait_ge(tr, b * 4)
                    nc.scalar.activation(batch_s[k][:, :, :], both[:, ds(b * TPB, TPB), :], ACT.Copy).then_inc(cut, 1)
                    act.wait_ge(tr, b * 4 + 4 + TR_CREDIT)
                    act.wait_ge(row_b, b + 1)
                    nc.scalar.activation(batch_t[k][0:E, :], ps_t[k][0:E, :], ACT.Copy).then_inc(tr_out, 1)

        @blk.tensor
        def _(pe):
            pe.wait_ge(sum_ask, 1)
            nc.tensor.matmul(ps_sum[:, :], c.ones[:, :], cell[:, 0:1], start=True, stop=True).then_inc(sum_got, 1)
            pe.sem_inc(tr, TR_CREDIT)
            pe.sem_inc(row_b, ROW_CREDIT)
            with pe.Fori(0, B // 2) as i:
                for k in range(2):
                    b = i * 2 + k
                    pe.wait_ge(cut, b + 1)
                    for w in range(2):
                        for j in range(TPB):
                            nc.tensor.transpose(ps_t[k][0:E, w * S + j * P:w * S + (j + 1) * P],
                                                batch_s[k][:, j, w * E:(w + 1) * E], c.ident[:, :]).then_inc(tr, 1)
                    pe.wait_ge(tr_out, b + 1)
                    pe.wait_ge(ranked, b * TPB + TPB)
                    for j in range(TPB):
                        last = nc.tensor.matmul(ps_b[k][:, j, :], batch_t[k][:, S + j * P:S + (j + 1) * P],
                                                batch_t[k][:, 0:S], start=True, stop=True)
                    last.then_inc(row_b, 1)
            pe.wait_ge(taken_done, 2)
            flat = taken[:, :, :].rearrange("p g t -> p (g t)")
            for h in range(2):
                nc.tensor.matmul(ps_pre[h][:, 0:HB], c.onesb[:, :], flat[:, h * HB:(h + 1) * HB], start=True, stop=True).then_inc(counted, 1)
            for h in range(2):
                pe.wait_ge(copied, h + 1)
                nc.tensor.matmul(ps_pre[h][:, 0:HB], c.tri[:, :], flat[:, h * HB:(h + 1) * HB], start=True, stop=True).then_inc(counted, 1)
            nc.tensor.matmul(ps_inv[:, :], zero[:, 0:P], zero[:, :], start=True, stop=False, skip_group_check=True)
            pe.sem_inc(put, NR)
            with pe.Fori(0, NT // NR) as i:
                for k in range(NR):
                    pe.wait_ge(onehot, i * NR + (k + 1))
                    nc.tensor.matmul(ps_inv[:, :], at_p[k][:, :], at_t[k][:, :, :].rearrange("p a s -> p (a s)"),
                                     start=False, stop=False, skip_group_check=True).then_inc(put, 1)
            nc.tensor.matmul(ps_inv[:, :], zero[:, 0:P], zero[:, :], start=False, stop=True, skip_group_check=True).then_inc(inv, 1)

        @blk.vector
        def _(dve):
            v = nc.vector
            s = Steps(dve, vs)

            def bc(col, shape, axis):
                return col.unsqueeze(axis).to_broadcast(shape)

            full = [P, NT, E]
            s.step(v.tensor_scalar(rec[:, :], c.var[:, :], LN_EPS, None, ALU.add))
            s.step(v.reciprocal(rec[:, :], rec[:, :]))
            s.step(v.tensor_tensor(xnorm2[:, :], c.var[:, :], rec[:, :], ALU.mult))
            v.tensor_scalar(xnorm2[:, :], xnorm2[:, :], float(D), None, ALU.mult).then_inc(sq_ask, 1)
            dve.wait_ge(sq_got, 1)
            s.step(v.tensor_tensor(den[:, :, :], bc(xnorm[:, :], full, 2), bc(c.wnorm[:, :], full, 1), ALU.mult))
            s.step(v.tensor_scalar(den[:, :, :], den[:, :, :], 1e-9, None, ALU.add))
            s.step(v.reciprocal(den[:, :, :], den[:, :, :]))
            s.step(v.tensor_tensor(aff, c.num[:, :, :], den[:, :, :], ALU.mult))
            v.tensor_reduce(cell[:, 0:1], aff, axis=AX.XY, op=ALU.add).then_inc(sum_ask, 1)
            s.step(v.tensor_reduce(amax[:, :], aff, axis=AX.X, op=ALU.max))
            s.step(v.tensor_tensor(weight[:, :, :], aff, bc(amax[:, :], full, 2), ALU.is_equal))
            s.step(v.tensor_tensor(weight[:, :, :], weight[:, :, :], bc(c.down[:, :], full, 1), ALU.mult))
            s.step(v.tensor_reduce(wmax[:, :], weight[:, :, :], axis=AX.X, op=ALU.max))
            v.tensor_tensor(hot, weight[:, :, :], bc(wmax[:, :], full, 2), ALU.is_equal).then_inc(hot_done, 1)
            dve.wait_ge(sum_got, 1)
            v.scalar_tensor_tensor(cell[:, 1:2], ps_sum[:, :], 1.0 / (T * E), c.thr[:, :], ALU.mult, ALU.subtract).then_inc(e_ask, 1)
            dve.wait_ge(e_got, 1)
            s.step(v.tensor_scalar(cell[:, 3:4], cell[:, 2:3], 1.0, None, ALU.add))
            s.step(v.reciprocal(cell[:, 4:5], cell[:, 3:4]))
            s.step(v.tensor_scalar(cell[:, 5:6], cell[:, 4:5], float(S), 4.0, ALU.mult, ALU.max))
            dve.sem_inc(ranked, 2 * TPB)
            with dve.Fori(0, B // 2) as i:
                for k in range(2):
                    b = i * 2 + k
                    dve.wait_ge(row_b, b + (1 + ROW_CREDIT))
                    for j in range(TPB):
                        dve.wait_ge(ranked, b * TPB + (j + 2 * TPB - 1))
                        v.scalar_tensor_tensor(beats[j][:, :], ps_b[k][:, j, :], amax[:, ds(b * TPB + j, 1)],
                                               c.tie[:, j, :], ALU.subtract, ALU.is_gt,
                                               accum_out=rank[:, ds(b * TPB + j, 1)]).then_inc(ranked, 1)
            dve.wait_ge(ranked, NT + 2 * TPB)
            s.step(v.tensor_scalar(kept[:, :], rank[:, :], 1.0, cell[:, 5:6], ALU.add, ALU.is_le))
            v.tensor_tensor(taken[:, 0:E, :].rearrange("p e t -> p t e"), hot, bc(kept[:, :], full, 2), ALU.mult).then_inc(taken_done, 1)
            v.tensor_scalar(taken[:, E, :], kept[:, :], -1.0, 1.0, ALU.mult, ALU.add).then_inc(taken_done, 1)
            dve.wait_ge(made, 7)
            for h in range(2):
                dve.wait_ge(counted, h + 1)
                v.tensor_copy(total[:, h * HB:(h + 1) * HB], ps_pre[h][:, 0:HB]).then_inc(copied, 1)
            dve.wait_ge(copied, 2)
            s.step(v.tensor_tensor_scan(upto[:, :], one_row[:, :], total[:, :], 0.0, ALU.mult, ALU.add))
            s.step(v.tensor_copy(ends[:, :], upto[:, :].rearrange("p (g t) -> p g t", g=G)[:, :, NT - 1]))
            s.step(v.tensor_copy(count[:, :], ends[:, :]))
            s.step(v.tensor_tensor(count[:, 1:G], ends[:, 1:G], ends[:, 0:G - 1], ALU.subtract))
            s.step(v.tensor_scalar(tiles[:, :], count[:, :], 1.0 / P, (P - 1) / P - 0.49609375, ALU.mult, ALU.add))
            s.step(v.tensor_scalar(tiles[:, :], tiles[:, :], MAGIC, None, ALU.add))
            s.step(v.tensor_scalar(tiles[:, :], tiles[:, :], MAGIC, None, ALU.subtract))
            s.step(v.tensor_tensor_scan(tile_end[:, :], one_row[:, 0:G], tiles[:, :], 0.0, ALU.mult, ALU.add))
            s.step(v.tensor_tensor(start[:, :], tile_end[:, :], tiles[:, :], ALU.subtract))
            s.step(v.tensor_tensor(shift[:, :], count[:, :], ends[:, :], ALU.subtract))
            s.step(v.scalar_tensor_tensor(shift[:, :], start[:, :], float(P), shift[:, :], ALU.mult, ALU.add))
            grid = "p (g t) -> p g t"
            s.step(v.tensor_tensor(upto[:, :], upto[:, :], total[:, :], ALU.subtract))
            s.step(v.tensor_tensor(upto[:, :].rearrange(grid, g=G), upto[:, :].rearrange(grid, g=G),
                                   bc(shift[:, :], [P, G, NT], 2), ALU.add))
            for h in range(2):
                dve.wait_ge(counted, h + 3)
                s.step(v.tensor_tensor(place[:, h * HB:(h + 1) * HB], ps_pre[h][:, 0:HB], upto[:, h * HB:(h + 1) * HB], ALU.add))
            s.step(v.tensor_tensor(place[:, :].rearrange(grid, g=G), place[:, :].rearrange(grid, g=G), taken[:, :, :], ALU.mult))
            s.step(v.tensor_reduce(slot[:, :], place[:, :].rearrange("p (g t) -> p t g", g=G), axis=AX.X, op=ALU.add))
            s.step(v.tensor_scalar(row[:, :], slot[:, :], 1.0 / P, -0.49609375, ALU.mult, ALU.add))
            s.step(v.tensor_scalar(row[:, :], row[:, :], MAGIC, None, ALU.add))
            s.step(v.tensor_scalar(row[:, :], row[:, :], MAGIC, None, ALU.subtract))
            s.step(v.scalar_tensor_tensor(colp[:, :], row[:, :], float(-P), slot[:, :], ALU.mult, ALU.add))
            with dve.Fori(0, NT // NR) as i:
                for k in range(NR):
                    j = i * NR + k
                    dve.wait_ge(put, j + 1)
                    v.tensor_scalar(at_p[k][:, :], c.iota[:, :], colp[:, ds(j, 1)], None, ALU.is_equal)
                    v.tensor_scalar(at_t[k][:, 0, :], c.iota[:, 0:NS], row[:, ds(j, 1)], c.tile1[:, ds(j, 1)], ALU.is_equal, ALU.mult)
                    v.tensor_scalar(at_t[k][:, 1, :], c.iota[:, 0:NS], row[:, ds(j, 1)], c.part[:, :], ALU.is_equal, ALU.mult).then_inc(onehot, 1)
            s.step(v.tensor_scalar(eid_f[0][:, :], c.iota[:, 0:NSX], tile_end[:, 0:1], None, ALU.is_ge))
            for g in range(1, E):
                s.step(v.scalar_tensor_tensor(eid_f[g % 2][:, :], c.iota[:, 0:NSX], tile_end[:, g:g + 1],
                                              eid_f[(g - 1) % 2][:, :], ALU.is_ge, ALU.add))
            s.step(v.tensor_copy(c.eid[:, :], eid_f[(E - 1) % 2][0:1, :]))
            dve.wait_ge(inv, 1)
            s.step(v.tensor_scalar(lo[:, :], ps_inv[:, NS:2 * NS], float(-P), None, ALU.add))
            s.step(v.scalar_tensor_tensor(src[:, :], ps_inv[:, 0:NS], float(P), lo[:, :], ALU.mult, ALU.add))
            s.step(v.tensor_scalar(gsrc[:, :], src[:, :], 0.0, None, ALU.max))
            s.step(v.tensor_copy(c.gidx[:, 0:NS], gsrc[:, :]))
            s.step(v.tensor_scalar(away[:, :], src[:, :], 0.0, float(4 * T), ALU.is_lt, ALU.mult))
            s.step(v.tensor_tensor(away[:, :], away[:, :], src[:, :], ALU.add))
            s.step(v.tensor_copy(c.sidx[:, 0:NS], away[:, :]))


def experts(nc, m, io, c, tag, y_dram):
    ctx = ExitStack()
    with ctx:
        t = Mem(nc, ctx)

        def sem(name):
            return t.sem(f"{tag}_{name}")

        x_row = [t.sb(f"{tag}_x{k}", [P, XW]) for k in range(U)]
        y_row = [t.sb(f"{tag}_y{k}", [P, D]) for k in range(U)]
        gi, si = t.sb(f"{tag}_gi", [P, U], I32), t.sb(f"{tag}_si", [P, U], I32)
        xn = [t.sb(f"{tag}_xn{k}", [P, D]) for k in range(2)]
        xn_t = [t.sb(f"{tag}_xnt{k}", [P, P]) for k in range(2)]
        hid = [t.sb(f"{tag}_h{k}", [P, F]) for k in range(2)]
        hid_t = [t.sb(f"{tag}_ht{k}", [P, FC, P]) for k in range(2)]
        ps_x = t.ps(f"{tag}_ps_x", [P, P])
        ps_h = [t.ps(f"{tag}_ps_h{k}", [P, F]) for k in range(2)]
        ps_t = [t.ps(f"{tag}_ps_t{k}", [P, FC, P]) for k in range(2)]
        ps_y = [t.ps(f"{tag}_ps_y{k}", [P, D]) for k in range(2)]
        x_in = [sem(f"xin{k}") for k in range(U)]
        y_out = [sem(f"yout{k}") for k in range(U)]
        cell = sem("cell")
        xn_done, x_tr, x_tr_out, up, gelu, h_tr, h_tr_out, down, y_done = (
            sem(n) for n in ("xn", "xtr", "xtro", "up", "gelu", "htr", "htro", "down", "y"))
        passed = sem("passed")
        BOTH = 2
        blk = ctx.enter_context(nc.Block())
        rows = io["rows"]

        @blk.sync
        def _(sp):
            for k in range(U):
                sp.wait_ge(y_out[k], 16 * (NS // U))

        @blk.gpsimd
        def _(pool):
            g = nc.gpsimd

            def gather(k):
                pool.indirect_dma_start(x_row[k][:, :], None, rows, bass.IndirectOffsetOnAxis(ap=gi[:, k:k + 1], axis=0)).then_inc(x_in[k], 16)

            g.tensor_copy(gi[:, :], c.gidx[:, 0:U]).then_inc(cell, 1)
            pool.wait_ge(cell, 1)
            for k in range(U):
                gather(k)
            with pool.Fori(0, NS // U) as i:
                for k in range(U):
                    pool.wait_ge(x_in[k], i * 16 + 16)
                    pool.wait_ge(y_out[k], i * 16)
                g.tensor_copy(gi[:, :], c.gidx[:, ds(i * U + U, U)]).then_inc(cell, 1)
                g.tensor_copy(si[:, :], c.sidx[:, ds(i * U, U)]).then_inc(cell, 1)
                pool.wait_ge(cell, i * 2 + 3)
                pool.sem_inc(passed, 1)
                for k in range(U):
                    pool.wait_ge(y_done, i * U + (k + 1))
                    pool.sem_inc(passed, 1)
                    pool.indirect_dma_start(y_dram, bass.IndirectOffsetOnAxis(ap=si[:, k:k + 1], axis=0), y_row[k][:, :], None,
                                            bounds_check=T - 1, oob_is_err=False).then_inc(y_out[k], 16)
                    gather(k)
            for k in range(U):
                pool.wait_ge(x_in[k], 16 * (NS // U + 1))

        @blk.scalar
        def _(act):
            a = nc.scalar

            def turn_x(j, k):
                act.wait_ge(x_tr, j + 1)
                act.wait_ge(up, j + 1)
                a.activation(xn_t[k][:, :], ps_x[:, :], ACT.Copy).then_inc(x_tr_out, 1)

            def bend(j, k):
                act.wait_ge(up, j + (1 + BOTH))
                act.wait_ge(h_tr, j + 1)
                a.activation(hid[k][:, :], ps_h[k][:, :], ACT.Gelu).then_inc(gelu, 1)

            act.sem_inc(gelu, BOTH)
            turn_x(0, 0)
            turn_x(1, 1)
            bend(0, 0)
            with act.Fori(0, NS // U) as i:
                for k in range(U):
                    j = i * U + k
                    turn_x(j + 2, k % 2)
                    bend(j + 1, (k + 1) % 2)

        @blk.tensor
        def _(pe):
            te = nc.tensor

            def turn_x(j, k):
                pe.wait_ge(xn_done, j + 1)
                pe.wait_ge(x_tr_out, j)
                te.transpose(ps_x[:, :], xn[k][:, :], c.ident[:, :]).then_inc(x_tr, 1)

            def expand(j, k):
                e = pe.value_load(c.eid[0:1, ds(j, 1)], min_val=0, max_val=E)
                pe.wait_ge(x_tr_out, j + 1)
                pe.wait_ge(gelu, j + 1)
                te.matmul(ps_h[k][:, :], c.onesb[:, :], c.b1s[:, ds(e, 1), :].rearrange("p a f -> p (a f)"), start=True, stop=False)
                te.matmul(ps_h[k][:, :], xn_t[k][:, :], c.w1[:, ds(e, 1), :].rearrange("p a f -> p (a f)"), start=False, stop=True).then_inc(up, 1)

            def turn_h(j, k):
                pe.wait_ge(gelu, j + (1 + BOTH))
                pe.wait_ge(h_tr_out, j + 1)
                for f in range(FC):
                    last = te.transpose(ps_t[k][:, f, :], hid[k][:, f * P:(f + 1) * P], c.ident[:, :])
                last.then_inc(h_tr, 1)

            def contract(j, k):
                e = pe.value_load(c.eid[0:1, ds(j, 1)], min_val=0, max_val=E)
                pe.wait_ge(h_tr_out, j + (1 + BOTH))
                pe.wait_ge(y_done, j)
                te.matmul(ps_y[k][:, :], c.onesb[:, :], c.cst[:, ds(e, 1), :].rearrange("p a d -> p (a d)"), start=True, stop=False)
                for f in range(FC):
                    last = te.matmul(ps_y[k][:, :], hid_t[k][:, f, :], c.w2[:, ds(e, 1), f, :].rearrange("p a d -> p (a d)"),
                                     start=False, stop=(f == FC - 1))
                last.then_inc(down, 1)

            pe.sem_inc(up, BOTH)
            pe.sem_inc(h_tr, BOTH)
            pe.sem_inc(down, BOTH)
            turn_x(0, 0)
            turn_x(1, 1)
            expand(0, 0)
            with pe.Fori(0, NS // U) as i:
                for k in range(U):
                    j = i * U + k
                    turn_h(j, k % 2)
                    turn_x(j + 2, k % 2)
                    expand(j + 1, (k + 1) % 2)
                    contract(j, k % 2)

        @blk.vector
        def _(dve):
            v = nc.vector

            def norm(j, s, turn):
                dve.wait_ge(x_in[s], turn * 16 + 16)
                v.tensor_scalar(xn[s % 2][:, :], x_row[s][:, 0:D], x_row[s][:, D:D + 1], x_row[s][:, D + 1:D + 2],
                                ALU.subtract, ALU.mult).then_inc(xn_done, 1)

            def copy_h(j, k):
                dve.wait_ge(h_tr, j + (1 + BOTH))
                dve.wait_ge(down, j + 1)
                v.tensor_copy(hid_t[k][:, :, :], ps_t[k][:, :, :]).then_inc(h_tr_out, 1)

            def finish(j, s, turn):
                dve.wait_ge(down, j + (1 + BOTH))
                dve.wait_ge(y_out[s], turn * 16)
                v.scalar_tensor_tensor(y_row[s][:, :], ps_y[s % 2][:, :], 0.5, x_row[s][:, 0:D], ALU.mult, ALU.add).then_inc(y_done, 1)

            dve.sem_inc(h_tr_out, BOTH)
            norm(0, 0, 0)
            norm(1, 1, 0)
            dve.wait_ge(x_tr, 1)
            norm(2, 2, 0)
            with dve.Fori(0, NS // U) as i:
                for k in range(U):
                    j = i * U + k
                    copy_h(j, k % 2)
                    dve.wait_ge(x_tr, j + 2)
                    norm(j + 3, (k + 3) % U, i if k + 3 < U else i + 1)
                    finish(j, k, i)


def attention(nc, m, io, c, x_dram):
    ctx = ExitStack()
    with ctx:
        t = Mem(nc, ctx)
        sb = lambda n, s, dt=F32: t.sb(f"at_{n}", s, dt)
        sem = lambda n: t.sem(f"at_{n}")
        two = lambda n, s, dt=F32: [sb(f"{n}{k}", s, dt) for k in range(2)]
        HP = H // 2
        QUADS = H // 4
        NP = 12
        NQ = 4
        RING = 6
        ROWS = 96
        SCALE = HD ** -0.5

        xa, xr, x2 = two("xa", [P, TPB, D + 2]), two("xr", [P, TPB, D]), two("x2", [P, TPB, XW])
        bn, vare = two("bn", [P, TPB, 6]), two("vare", [P, TPB])
        bn2, vare2 = two("bn2", [P, TPB, 6]), two("vare2", [P, TPB])
        xn, xt = two("xn", [P, TPB, D]), two("xt", [P, S])
        xn2, x2t = two("xn2", [P, TPB, D]), two("x2t", [P, S])
        part, rest = two("part", [P, 3, 2 * S], BF16), two("rest", [P, 2 * S])
        qs = [sb(f"qs{k}", [P, HP, S], BF16) for k in range(NQ)]
        kb = [sb(f"kb{k}", [P, HP, 2, S], BF16) for k in range(NQ)]
        kc = two("kc", [P, HP, S], BF16)
        vp = [sb(f"vp{k}", [P, TPB, H, 32]) for k in range(NQ)]
        pt = [sb(f"pt{k}", [P, 2 * S]) for k in range(RING)]
        ot, on, ont = two("ot", [P, QUADS, S]), two("on", [P, TPB, D]), two("ont", [P, S])
        rden = two("rden", [P, H])
        mx, nm, nr = two("mx", [P, TPB, H]), two("nm", [P, TPB, 2, HP]), two("nr", [P, TPB, H])
        mp, mt = two("mp", [P, TPB, 3, H], BF16), two("mt", [3 * H, S], BF16)
        mhalf, pick, sel = sb("mhalf", [P, TPB]), sb("pick", [P, 2, 9]), sb("sel", [P, 2])
        pp = [t.ps(f"at_pp{k}", [P, 2 * S]) for k in range(2)]
        pm = [t.ps(f"at_pm{k}", [P, 2 * S]) for k in range(2)]
        po = t.ps("at_po", [P, QUADS * S])
        mi = [t.ps(f"at_mi{k}", [P, 2 * S]) for k in range(2)]
        qkd = [nc.dram_tensor(f"at_qkd{k}", (3 * P, 2 * S), BF16, kind="Internal").ap() for k in range(2)]

        xa_in, xr_in, row_out = ([sem(f"{n}{k}") for k in range(2)] for n in ("xa_in", "xr_in", "row_out"))
        q_in, m_in = ([sem(f"{n}{k}") for k in range(NQ)] for n in ("q_in", "m_in"))
        k_in, part_out = ([sem(f"{n}{k}") for k in range(2)] for n in ("k_in", "part_out"))
        (zeroed, picked, selected, mv1, bnd1, var1, rstd1, xn_done, xt_tr, xt_out, qk_mm, a_done, r_done, b_done, part_done,
         kb_done, v_mm, v_out, pre_done, maxed, negs, mp_done, mt_tr, mt_out, main_done, exped, masked, pv_done, ot_out,
         otr, rd, on_done, ont_tr, ont_out, proj_mm, x2_done, bnd2, mv2, var2, rstd2, xn2_done, x2t_tr, x2t_out, num_mm,
         num_out) = (sem(n) for n in (
             "zeroed picked selected mv1 bnd1 var1 rstd1 xn_done xt_tr xt_out qk_mm a_done r_done b_done part_done "
             "kb_done v_mm v_out pre_done maxed negs mp_done mt_tr mt_out main_done exped masked pv_done ot_out "
             "otr rd on_done ont_tr ont_out proj_mm x2_done bnd2 mv2 var2 rstd2 xn2_done x2t_tr x2t_out num_mm "
             "num_out").split())
        passed = sem("passed")
        NZ = NQ * 3 + 2 + 1
        blk = ctx.enter_context(nc.Block())
        x_v = x_dram.rearrange("(b k p) d -> p b k d", k=TPB, p=P)
        row_v = io["rows"].rearrange("(b k p) w -> p b k w", k=TPB, p=P)

        def wait(eng, s, n, most=None):
            if isinstance(n, int):
                n = n if most is None else min(n, most)
                if n <= 0:
                    return
            eng.wait_ge(s, n)

        def dma_count(b, slots, each=1):
            return lambda k: b * (16 * each // slots) + (16 * each - (k % slots) * (16 * each // slots))

        def turns(turn):
            for b in range(-4, NQ):
                turn(b, b % NQ, lambda o, b=b: 0 <= b + o < B)
            yield
            for b in range(B - NQ, B + 2):
                turn(b, b % NQ, lambda o, b=b: 0 <= b + o < B)
            yield

        def run(eng, turn):
            emit = turns(turn)
            next(emit)
            with eng.Fori(1, B // NQ - 1) as i:
                for k in range(NQ):
                    turn(i * NQ + k, k, lambda o: True)
            next(emit)

        @blk.sync
        def _(sp):
            def turn(b, k, has):
                if has(4):
                    wait(sp, xn_done, (b + 3) * TPB)
                    sp.dma_start(xa[k % 2][:, :, 0:D], x_v[:, ds(b + 4, 1), :, :]).then_inc(xa_in[k % 2], 16)
                if has(0):
                    wait(sp, x2_done, b - 1)
                    sp.dma_start(xr[k % 2][:, :, :], x_v[:, ds(b, 1), :, :]).then_inc(xr_in[k % 2], 16)
                if has(2):
                    n, q = b + 2, (k + 2) % NQ
                    wait(sp, part_done, n + 1)
                    sp.sem_inc(passed, 1)
                    wait(sp, main_done, (n - NQ + 1) * NP)
                    sp.sem_inc(passed, 1)
                    wait(sp, kb_done, (n - 1) * 2)
                    sp.dma_start(qkd[k % 2].rearrange("(t p) n -> p t n", t=3), part[k % 2][:, :, :]).then_inc(part_out[k % 2], 16)
                    wait(sp, part_out[k % 2], dma_count(n, 2)(k))
                    src = qkd[k % 2].rearrange("(tq g) n -> tq g n", g=HP)
                    for row, lo, hi in ((0, 0, 48), (48, 0, 32), (80, 0, 16)):
                        sp.dma_start(kc[k % 2][row:row + hi - lo, :, :], src[lo:hi, :, S:2 * S]).then_inc(k_in[k % 2], 16)
                    for i, p in enumerate((0, 0, 0, 1, 1, 2)):
                        sp.dma_start(qs[q][16 * i:16 * i + 16, :, :], src[16 * p:16 * p + 16, :, 0:S]).then_inc(q_in[q], 16)
                if has(-1):
                    wait(sp, rstd2, b)
                    sp.dma_start(row_v[:, ds(b - 1, 1), :, :], x2[(k - 1) % 2][:, :, :]).then_inc(row_out[(k - 1) % 2], 16)

            run(sp, turn)
            for k in range(2):
                sp.wait_ge(row_out[k], 16 * (B // 2))

        @blk.gpsimd
        def _(pool):
            g = nc.gpsimd
            g.memset(mhalf[:, :], -0.5).then_inc(zeroed, 1)
            for k in range(2):
                g.memset(x2[k][:, :, D + 2:XW], 0.0).then_inc(zeroed, 1)
            for k in range(NQ):
                g.memset(vp[k][:, :, :, HD + 1:32], 0.0).then_inc(zeroed, 1)
                g.memset(vp[k][:, :, :, HD:HD + 1], 1.0).then_inc(zeroed, 1)
            g.memset(pick[:, :, 0:6], 1.0).then_inc(picked, 1)
            g.memset(pick[:, :, 6:9], 0.0).then_inc(picked, 1)
            pool.wait_ge(picked, 2)
            g.affine_select(out=pick[:, :, 0:6], in_=pick[:, :, 0:6], compare_op=ALU.is_ge, fill=0.0,
                            base=0, pattern=[[-8, 2], [-16, 6]], channel_multiplier=1).then_inc(picked, 1)
            g.affine_select(out=pick[:, :, 6:9], in_=pick[:, :, 6:9], compare_op=ALU.not_equal, fill=1.0,
                            base=-ROWS, pattern=[[-1, 2], [-2, 3]], channel_multiplier=1).then_inc(picked, 1)
            pool.wait_ge(picked, 4)
            g.affine_select(out=pick[:, :, 0:6], in_=pick[:, :, 0:6], compare_op=ALU.is_ge, fill=0.0,
                            base=HD - 1, pattern=[[8, 2], [16, 6]], channel_multiplier=-1).then_inc(picked, 1)

            def turn(b, k, has):
                def mask(u):
                    if not has(0):
                        return
                    wait(pool, exped, b * NP + (u + 1))
                    pool.sem_inc(passed, 1)
                    n = 4 if u % 3 == 2 else 2
                    tile = pt[u % RING][:, :].rearrange("p (h q) -> p h q", h=n)[:, :, 0:P]
                    g.affine_select(out=tile, in_=tile, compare_op=ALU.is_ge, fill=0.0, base=0,
                                    pattern=[[0, n], [1, P]], channel_multiplier=-1).then_inc(masked, 1)

                for u in range(4):
                    mask(u)
                if has(2):
                    n, q = b + 2, k % 2
                    wait(pool, r_done, n + 1)
                    pool.sem_inc(passed, 1)
                    g.tensor_copy(part[q][:, 1, :], rest[q][:, :]).then_inc(b_done, 1)
                    wait(pool, b_done, n + 1)
                    g.tensor_tensor(part[q][:, 2, :], rest[q][:, :], part[q][:, 1, :], ALU.subtract).then_inc(part_done, 1)
                for u in range(4, 7):
                    mask(u)
                if has(1):
                    n, q = b + 1, (k + 1) % 2
                    wait(pool, maxed, (n + 1) * NP)
                    pool.sem_inc(passed, 1)
                    for j in range(TPB):
                        g.tensor_scalar(nm[q][:, j, :, :], mx[q][:, j, :].rearrange("p (g r) -> p r g", r=2), -1.0, None, ALU.mult).then_inc(negs, 1)
                    flat = nm[q][:, :, :, :].rearrange("p j r g -> p j (r g)")
                    wait(pool, negs, n * 5 + 2)
                    pool.sem_inc(passed, 1)
                    g.tensor_copy(mp[q][:, :, 0, :], flat).then_inc(negs, 1)
                    wait(pool, negs, n * 5 + 3)
                    g.tensor_tensor(nr[q][:, :, :], flat, mp[q][:, :, 0, :], ALU.subtract).then_inc(negs, 1)
                    wait(pool, negs, n * 5 + 4)
                    pool.sem_inc(passed, 1)
                    g.tensor_copy(mp[q][:, :, 1, :], nr[q][:, :, :]).then_inc(negs, 1)
                    wait(pool, negs, n * 5 + 5)
                    g.tensor_tensor(mp[q][:, :, 2, :], nr[q][:, :, :], mp[q][:, :, 1, :], ALU.subtract).then_inc(mp_done, 1)
                for u in (7, 8):
                    mask(u)
                if has(3):
                    q = (k + 3) % 2
                    wait(pool, var1, b + 4)
                    g.tensor_tensor(xa[q][:, :, D + 1], vare[q][:, :], mhalf[:, :], ALU.pow).then_inc(rstd1, 1)
                for u in (9, 10):
                    mask(u)
                if has(-1):
                    q = (k - 1) % 2
                    wait(pool, var2, b)
                    g.tensor_tensor(x2[q][:, :, D + 1], vare2[q][:, :], mhalf[:, :], ALU.pow).then_inc(rstd2, 1)
                mask(11)

            run(pool, turn)

        @blk.scalar
        def _(act):
            a = nc.scalar
            act.wait_ge(zeroed, 3 + 3 * NQ)

            def turn(b, k, has):
                if has(-1):
                    wait(act, pv_done, b * NP)
                    wait(act, otr, (b - 2) * 2)
                    a.activation(ot[(k - 1) % 2][:, :, :].rearrange("p g q -> p (g q)"), po, ACT.Copy).then_inc(ot_out, 1)
                for u in range(NP):
                    if has(0):
                        wait(act, main_done, b * NP + (u + 1))
                        wait(act, pv_done, b * NP + (u + 1 - RING))
                        a.activation(pt[u % RING][:, :], pm[u % 2], ACT.Exp, scale=SCALE).then_inc(exped, 1)
                    if u == 0 and has(2):
                        wait(act, xt_tr, (b + 3) * TPB)
                        wait(act, v_mm, b + 1)
                        a.activation(xt[k % 2][:, :], mi[0][:, 0:S], ACT.Copy).then_inc(xt_out, 1)
                    if u == 1 and has(-2):
                        wait(act, x2t_tr, (b - 1) * TPB)
                        a.activation(x2t[k % 2][:, :], mi[1][:, 0:S], ACT.Copy).then_inc(x2t_out, 1)
                    if u == 2 and has(2):
                        wait(act, qk_mm, b + 3)
                        wait(act, part_out[k % 2], dma_count(b, 2)(k))
                        a.activation(part[k % 2][:, 0, :], mi[0], ACT.Copy).then_inc(a_done, 1)
                    if u == 3 and has(-2):
                        wait(act, num_mm, b - 1)
                        a.activation(c.num[:, ds((b - 2) * TPB, TPB), :], mi[1][:, 0:TPB * E].rearrange("p (j e) -> p j e", e=E),
                                     ACT.Copy).then_inc(num_out, 1)
                    if u == 4 and has(2):
                        wait(act, v_mm, b + 3)
                        wait(act, pv_done, (b - 1) * NP)
                        a.activation(vp[(k + 2) % NQ][:, :, :, 0:HD].rearrange("p j h d -> p (j h) d"),
                                     mi[0][:, 0:TPB * D].rearrange("p (h d) -> p h d", d=HD), ACT.Copy).then_inc(v_out, 1)
                    if u == 7 and has(-1):
                        wait(act, ont_tr, b)
                        a.activation(ont[(k - 1) % 2][:, :], mi[1][:, 0:S], ACT.Copy).then_inc(ont_out, 1)
                    if u == 8 and has(1):
                        q = (k + 1) % NQ
                        wait(act, mt_tr, b + 2)
                        wait(act, m_in[(q - 2) % NQ], dma_count(b - 1, NQ)(q - 2))
                        a.activation(mt[q % 2][:, :], mi[0].bitcast(BF16)[0:3 * H, 0:S], ACT.Copy).then_inc(mt_out, 1)
                        wait(act, mt_out, b + 2)
                        act.dma_start(qs[q][ROWS:ROWS + 6, :, :], mt[q % 2][:, :].unsqueeze(1)).then_inc(m_in[q], 16)

            run(act, turn)

        @blk.tensor
        def _(pe):
            te = nc.tensor
            pe.wait_ge(zeroed, 3 + 3 * NQ)

            def turn(b, k, has):
                def scores_by_query(v):
                    n, s, out = b + 1, (k + 1) % NQ, pp[v % 2]
                    if v == 0:
                        wait(pe, q_in[s], dma_count(n, NQ, 6)(s))
                        wait(pe, kb_done, (n + 1) * 2)
                    wait(pe, maxed, n * NP + (v - 1))
                    if v < 4:
                        for w in range(2):
                            te.matmul(out[:, w * S:(w + 1) * S], qs[s][0:ROWS, 2 * v + w, 0:P], kb[s][0:ROWS, 2 * v + w, :, 0:P],
                                      start=(w == 0), stop=False, skip_group_check=True)
                        te.matmul(out, c.identb[:, :], c.mask[:, :, :].rearrange("p a q -> p (a q)"),
                                  start=False, stop=True, skip_group_check=True).then_inc(pre_done, 1)
                    else:
                        te.matmul(out, qs[s][0:ROWS, v - 4, P:S], kb[s][0:ROWS, v - 4, :, :].rearrange("p r q -> p (r q)"),
                                  start=True, stop=False, skip_group_check=True)
                        te.matmul(out.rearrange("p (r q) -> p r q", r=2)[:, :, P:S], c.identb[:, :], c.mask[:, 0:2, :],
                                  start=False, stop=True, skip_group_check=True).then_inc(pre_done, 1)

                def scores_by_key(u):
                    s, out, quad, w = k, pm[u % 2], u // 3, u % 3
                    if u == 0:
                        wait(pe, m_in[s], dma_count(b, NQ)(s))
                    wait(pe, exped, b * NP + (u - 1))
                    if w < 2:
                        for r in range(2):
                            last = te.matmul(out[:, r * S:(r + 1) * S], kb[s][:, 2 * quad + w, r, 0:P], qs[s][:, 2 * quad + w, :],
                                             start=True, stop=True)
                    else:
                        for j in range(4):
                            last = te.matmul(out[:, j * P:(j + 1) * P], kb[s][:, 2 * quad + j // 2, j % 2, P:S],
                                             qs[s][:, 2 * quad + j // 2, P:S], start=True, stop=True)
                    last.then_inc(main_done, 1)

                def times_v(u):
                    s, quad, w, src = k, u // 3, u % 3, pt[u % RING]
                    if u == 0:
                        wait(pe, ot_out, b)
                        wait(pe, v_out, b + 1)
                    wait(pe, masked, b * NP + (u + 1))
                    for i in range(2 if w < 2 else 4):
                        j = 2 * w + i if w < 2 else i
                        n = S if w < 2 else P
                        last = te.matmul(po[32 * j:32 * j + 32, (quad + 1) * S - n:(quad + 1) * S],
                                         vp[s][:, w // 2, 4 * quad + j, :], src[:, i * n:(i + 1) * n],
                                         start=(w < 2), stop=(w == 2), skip_group_check=True)
                    last.then_inc(pv_done, 1)

                def small(u):
                    if u == 0 and has(2):
                        wait(pe, xn_done, (b + 3) * TPB)
                        wait(pe, mt_out, b + 1, B)
                        if isinstance(b, int):
                            wait(pe, v_out, b + 2)
                        for j in range(TPB):
                            te.transpose(mi[0][:, j * P:(j + 1) * P], xn[k % 2][:, j, :], c.ident[:, :]).then_inc(xt_tr, 1)
                    if u == 1 and has(-2):
                        wait(pe, xn2_done, (b - 1) * TPB)
                        for j in range(TPB):
                            te.transpose(mi[1][:, j * P:(j + 1) * P], xn2[k % 2][:, j, :], c.ident[:, :]).then_inc(x2t_tr, 1)
                    if u == 2 and has(2):
                        wait(pe, xt_out, b + 3)
                        te.matmul(mi[0][:, 0:S], c.wq[:, :], xt[k % 2][:, :], start=True, stop=True)
                        te.matmul(mi[0][:, S:2 * S], c.wk[:, :], xt[k % 2][:, :], start=True, stop=True).then_inc(qk_mm, 1)
                    if u == 3 and has(-2):
                        wait(pe, x2t_out, b - 1)
                        for j in range(TPB):
                            last = te.matmul(mi[1][:, j * E:(j + 1) * E], x2t[k % 2][:, j * P:(j + 1) * P], c.waff_t[:, :],
                                             start=True, stop=True)
                        last.then_inc(num_mm, 1)
                    if u == 4 and has(2):
                        wait(pe, r_done, b + 3)
                        for j in range(TPB):
                            last = te.matmul(mi[0][:, j * D:(j + 1) * D], xt[k % 2][:, j * P:(j + 1) * P], c.wv[:, :],
                                             start=True, stop=True)
                        last.then_inc(v_mm, 1)
                    if u in (5, 6) and has(-1):
                        j = u - 5
                        wait(pe, ot_out, b)
                        wait(pe, num_out, b - 1) if j == 0 else wait(pe, v_out, b + 3, B)
                        for quad in range(QUADS):
                            last = te.transpose(mi[1 - j][:, quad * P:(quad + 1) * P], ot[(k - 1) % 2][:, quad, j * P:(j + 1) * P],
                                                c.ident[:, :])
                        last.then_inc(otr, 1)
                    if u == 7 and has(-1):
                        wait(pe, on_done, b * TPB)
                        for j in range(TPB):
                            last = te.transpose(mi[1][:, j * P:(j + 1) * P], on[(k - 1) % 2][:, j, :], c.ident[:, :])
                        last.then_inc(ont_tr, 1)
                    if u == 8 and has(1):
                        wait(pe, mp_done, b + 2)
                        wait(pe, on_done, b * TPB)
                        wait(pe, v_out, b + 3, B)
                        pe.sem_inc(passed, 1)
                        for j in range(TPB):
                            last = te.transpose(mi[0].bitcast(BF16)[0:3 * H, j * P:(j + 1) * P],
                                                mp[(k + 1) % 2][:, j, :, :].rearrange("p t h -> p (t h)"), c.identb[:, :])
                        last.then_inc(mt_tr, 1)
                    if u == 9 and has(-1):
                        wait(pe, ont_out, b)
                        for j in range(TPB):
                            last = te.matmul(mi[1][:, j * D:(j + 1) * D], ont[(k - 1) % 2][:, j * P:(j + 1) * P], c.wproj[:, :],
                                             start=True, stop=True)
                        last.then_inc(proj_mm, 1)

                for u in range(NP):
                    if has(1) and u < NP // 2:
                        scores_by_query(2 * u)
                        scores_by_query(2 * u + 1)
                    if has(0):
                        scores_by_key(u)
                        if u >= 2:
                            times_v(u - 2)
                    small(u)
                if has(0):
                    times_v(NP - 2)
                    times_v(NP - 1)

            run(pe, turn)

        @blk.vector
        def _(dve):
            v = nc.vector
            for k in range(NQ):
                v.memset(qs[k][ROWS:P, :, :], 0.0).then_inc(zeroed, 1)
            dve.wait_ge(zeroed, 3 + 3 * NQ)
            dve.wait_ge(picked, 5)
            v.tensor_reduce(sel[:, :], pick[:, :, :], axis=AX.X, op=ALU.add).then_inc(selected, 1)
            for k in range(2):
                v.memset(kc[k][ROWS:P, :, :], 1.0).then_inc(selected, 1)
            dve.wait_ge(selected, 3)

            def statistics(n, x, bns, var, bnd, mv, done, keep):
                wait(dve, bnd, n * TPB)
                for j in range(TPB):
                    v.bn_stats(bns[:, j, :], x[:, j, 0:D]).then_inc(bnd, 1)
                for j in range(TPB):
                    wait(dve, bnd, n * TPB + (j + 1))
                    dve.sem_inc(passed, 1)
                    v.bn_aggr(x[:, j, D:D + 2], bns[:, j, :]).then_inc(mv, 1)
                wait(dve, mv, n * TPB + TPB)
                if keep:
                    v.tensor_copy(c.var[:, ds(n * TPB, TPB)], x[:, :, D + 1])
                v.tensor_scalar(var[:, :], x[:, :, D + 1], LN_EPS, None, ALU.add).then_inc(done, 1)

            def normalise(out, x, done):
                for j in range(TPB):
                    v.tensor_scalar(out[:, j, :], x[:, j, 0:D], x[:, j, D:D + 1], x[:, j, D + 1:D + 2],
                                    ALU.subtract, ALU.mult).then_inc(done, 1)

            def turn(b, k, has):
                for u in range(NP):
                    if has(1):
                        n, q = b + 1, (k + 1) % 2
                        wait(dve, pre_done, n * NP + (u + 1))
                        if u == 0:
                            wait(dve, mp_done, n - 1)
                        if u < 4:
                            v.tensor_reduce(mx[q][:, 0, 4 * u:4 * u + 4], pp[u % 2].rearrange("p (h q) -> p h q", h=4),
                                            axis=AX.X, op=ALU.max).then_inc(maxed, 1)
                        else:
                            v.tensor_reduce(mx[q][:, 1, 2 * u - 8:2 * u - 6], pp[u % 2].rearrange("p (h q) -> p h q", h=2),
                                            axis=AX.X, op=ALU.max).then_inc(maxed, 1)
                    if u == 5 and has(2):
                        wait(dve, a_done, b + 3)
                        v.tensor_tensor(rest[k % 2][:, :], mi[0], part[k % 2][:, 0, :], ALU.subtract).then_inc(r_done, 1)
                if has(-1):
                    q = (k - 1) % 2
                    for j in range(TPB):
                        wait(dve, otr, (b - 1) * TPB + (j + 1))
                        rows = mi[1 - j].rearrange("p (h w) -> p h w", w=32)
                        v.reciprocal(rden[j][:, :], rows[:, :, HD]).then_inc(rd, 1)
                        wait(dve, rd, (b - 1) * TPB + (j + 1))
                        v.tensor_tensor(on[q][:, j, :].rearrange("p (h d) -> p h d", d=HD), rows[:, :, 0:HD],
                                        rden[j][:, :].unsqueeze(2).to_broadcast([P, H, HD]), ALU.mult).then_inc(on_done, 1)
                if has(3):
                    q = (k + 3) % 2
                    wait(dve, xa_in[q], dma_count(b + 3, 2)(q))
                    statistics(b + 3, xa[q], bn[q], vare[q], bnd1, mv1, var1, False)
                if has(-1):
                    q = (k - 1) % 2
                    wait(dve, proj_mm, b)
                    wait(dve, xr_in[q], dma_count(b - 1, 2)(q))
                    wait(dve, row_out[q], dma_count(b - 3, 2)(q))
                    v.tensor_tensor(x2[q][:, :, 0:D], mi[1][:, 0:TPB * D].rearrange("p (j d) -> p j d", d=D), xr[q][:, :, :],
                                    ALU.add).then_inc(x2_done, 1)
                    wait(dve, x2_done, b)
                    statistics(b - 1, x2[q], bn2[q], vare2[q], bnd2, mv2, var2, True)
                if has(3):
                    q = (k + 3) % 2
                    wait(dve, rstd1, b + 4)
                    wait(dve, xt_tr, (b + 2) * TPB)
                    normalise(xn[q], xa[q], xn_done)
                if has(2):
                    wait(dve, k_in[k % 2], dma_count(b + 2, 2, 3)(k))
                    for r in range(2):
                        v.tensor_scalar(kb[(k + 2) % NQ][:, :, r, :], kc[k % 2][:, :, :], sel[:, r:r + 1], None,
                                        ALU.mult).then_inc(kb_done, 1)
                if has(-1):
                    q = (k - 1) % 2
                    wait(dve, rstd2, b)
                    wait(dve, x2t_tr, (b - 2) * TPB)
                    normalise(xn2[q], x2[q], xn2_done)

            run(dve, turn)


def macaron(nc, io, out):
    ctx = ExitStack()
    with ctx:
        m = Mem(nc, ctx)
        c = consts(nc, m)
        io["rows"] = nc.dram_tensor("rows", (T, XW), F32, kind="Internal").ap()
        x1 = nc.dram_tensor("x1", (T, D), F32, kind="Internal").ap()
        preamble(nc, m, io, c)
        token_stats(nc, m, io, c, io["x"])
        route(nc, m, c, "r1")
        experts(nc, m, io, c, "e1", x1)
        attention(nc, m, io, c, x1)
        route(nc, m, c, "r2")
        experts(nc, m, io, c, "e2", out)


_INS = {
    "x": ("L0_attn_batch", (T, D)),
    "wqkv": ("L0_attn_W_qkv", (D, 3 * D)),
    "uqkv": ("L0_attn_u_qkv", (3 * D,)),
    "sqkv": ("L0_attn_sigma_qkv", (1,)),
    "wproj": ("L0_attn_W_proj", (D, D)),
    "uproj": ("L0_attn_u_proj", (D,)),
    "sproj": ("L0_attn_sigma_proj", (1,)),
    "waff": ("L0_ffn_waff", (E, D)),
    "w1": ("L0_ffn_W1", (E, D, F)),
    "b1": ("L0_ffn_b1", (E, F)),
    "w2": ("L0_ffn_W2", (E, F, D)),
    "b2": ("L0_ffn_b2", (E, D)),
    "thr": ("L0_ffn_affinity_threshold", (1,)),
}


def kernel(**inputs):
    import concourse.bacc as _bacc
    from concourse.bass_utils import run_bass_kernel_spmd as _run

    nc = _bacc.Bacc("TRN2", target_bir_lowering=False, num_devices=1)
    arrays, io = {}, {}
    for short, (name, shape) in _INS.items():
        a = np.ascontiguousarray(inputs[name]).reshape(shape)
        arrays[f"in_{short}_dram"] = a
        io[short] = nc.dram_tensor(f"in_{short}_dram", shape, mybir.dt.from_np(a.dtype), kind="ExternalInput").ap()
    out = nc.dram_tensor("out_0_dram", (T, D), F32, kind="ExternalOutput").ap()
    macaron(nc, io, out)
    r = _run(nc, [arrays], core_ids=[0])
    return r.results[0]["out_0_dram"].reshape(B, S, D)
```

```python
import numpy as np
import concourse.bass as bass
from concourse import mybir
from contextlib import ExitStack

F32 = mybir.dt.float32
BF16 = mybir.dt.bfloat16
I32 = mybir.dt.int32
ALU = mybir.AluOpType
ACT = mybir.ActivationFunctionType
AX = mybir.AxisListType

P = 128
D = 128
E, F = 8, 512
FC = F // P
B, S = 32, 256
TPB = S // P
T = B * S
NT = T // P
G = E + 1
NS = NT + G - 1
U = 8
BANK = 512
NSX = NS + U
XW = D + 4
H, HD = 16, 8
MAGIC = 1.5 * 2 ** 23
LN_EPS = 1e-5
TIE = -1e-37


def ds(start, n):
    return bass.ds(start, n)


class Mem:

    def __init__(self, nc, ctx):
        self.nc, self.ctx, self.sems = nc, ctx, []
        ctx.callback(self.clear)

    def clear(self):
        if self.sems:
            for n in range(min(self.sems), max(self.sems) + 1):
                if n in self.sems and n - 1 not in self.sems:
                    end = n
                    while end in self.sems:
                        end += 1
                    self.nc.gpsimd.sem_clear(range(n, end))
            self.nc.all_engine_barrier()

    def sb(self, name, shape, dt=F32):
        return self.ctx.enter_context(self.nc.sbuf_tensor(name, shape, dt))

    def ps(self, name, shape, dt=F32):
        size = int(np.prod(shape[1:]))
        whole = self.ctx.enter_context(self.nc.psum_tensor(name, [P, -(-size // BANK) * BANK], dt))
        out = whole[:, 0:size]
        return out if len(shape) == 2 else out.rearrange("p (a b) -> p a b", a=shape[1])

    def sem(self, name):
        sem = self.ctx.enter_context(self.nc.semaphore(name))
        self.sems.append(sem.num)
        return sem


class Steps:

    def __init__(self, engine, sem):
        self.engine, self.sem, self.n = engine, sem, 0

    def step(self, ins):
        self.n += 1
        ins.then_inc(self.sem, 1)
        self.engine.wait_ge(self.sem, self.n)


def preamble(nc, m, io, c):
    ctx = ExitStack()
    with ctx:
        t = Mem(nc, ctx)
        waff_n = t.sb("waff_n", [E, D])
        b1_chunks = t.sb("b1_chunks", [E * FC, P])
        b1_rows = t.sb("b1_rows", [E, F])
        b1_rest = t.sb("b1_rest", [E, F])
        b1_parts = t.sb("b1_parts", [E, 3, F], BF16)
        gelu_b1 = t.sb("gelu_b1", [P, E * FC])
        const_row = t.sb("const_row", [1, G, D])
        b2_row = t.sb("b2_row", [1, E, D])
        sum_row = t.sb("sum_row", [1, D])
        rest_row = t.sb("rest_row", [1, G, D])
        const_parts = t.sb("const_parts", [1, 3, G * D], BF16)
        w_raw = [t.sb("wqkv_raw", [P, 3 * D]), t.sb("wproj_raw", [P, D])]
        u_row = [t.sb("uqkv_row", [P, 3 * D]), t.sb("uproj_row", [P, D])]
        sig = t.sb("sig", [P, 2])
        prod = t.sb("prod", [P, 3 * D])
        u2 = t.sb("u2", [P, 3 * D])
        v_bc = t.sb("v_bc", [P, P])
        col = t.sb("col", [P, 16])
        sq = t.sb("sq", [P, E])
        half = t.sb("half", [P, E])
        mhalf = t.sb("mhalf", [P, 1])
        iota_i = t.sb("iota_i", [P, P], I32)
        part_i = t.sb("part_i", [P, 1], I32)
        tile_i = t.sb("tile_i", [P, NT], I32)
        down_i = t.sb("down_i", [P, E], I32)
        pm = [t.ps(f"pre{i}", [P, 512]) for i in range(8)]

        w_in, w_ffn, parts_out = t.sem("w_in"), t.sem("w_ffn"), t.sem("parts_out")
        made, ints = t.sem("made"), t.sem("ints")
        small_t, small_e = t.sem("small_t"), t.sem("small_e")
        b1_t, b1_g, k_done = t.sem("b1_t"), t.sem("b1_g"), t.sem("k_done")
        b1_split, const_split = t.sem("b1_split"), t.sem("const_split")
        wn_sum, wn_sq, pows = t.sem("wn_sum"), t.sem("wn_sq"), t.sem("pows")
        ask, told, vstep = t.sem("ask"), t.sem("told"), t.sem("vstep")
        powask = t.sem("powask")
        pstep = t.sem("pstep")
        blk = ctx.enter_context(nc.Block())
        N_SMALL = 11

        @blk.sync
        def _(sp):
            for dst, src in [
                (waff_n[:, :], io["waff"]),
                (b1_chunks[:, :], io["b1"].rearrange("e (c p) -> (e c) p", p=P)),
                (b1_rows[:, :], io["b1"]),
                (b2_row[:, :, :], io["b2"].rearrange("(a e) d -> a e d", a=1)),
                (w_raw[0][:, :], io["wqkv"]),
                (w_raw[1][:, :], io["wproj"]),
                (u_row[0][:, :], io["uqkv"].partition_broadcast(P)),
                (u_row[1][:, :], io["uproj"].partition_broadcast(P)),
                (sig[:, 0:1], io["sqkv"].partition_broadcast(P)),
                (sig[:, 1:2], io["sproj"].partition_broadcast(P)),
                (c.thr[:, :], io["thr"].partition_broadcast(P)),
            ]:
                sp.dma_start(dst, src).then_inc(w_in, 16)
            sp.dma_start(c.w2[:, 0:E, :, :], io["w2"].rearrange("e (c p) d -> p e c d", p=P)).then_inc(w_ffn, 16)
            sp.dma_start(c.w1[:, 0:E, :], io["w1"].rearrange("e d f -> d e f")).then_inc(w_ffn, 16)
            sp.wait_ge(made, 18)
            sp.wait_ge(b1_split, 3)
            for r in range(3):
                for e in range(E):
                    sp.dma_start(c.b1s[r:r + 1, e, :], b1_parts[e:e + 1, r, :]).then_inc(parts_out, 16)
            sp.wait_ge(const_split, 3)
            for r in range(3):
                sp.dma_start(c.cst[r:r + 1, :, :].rearrange("a g d -> a (g d)"), const_parts[0:1, r, :]).then_inc(parts_out, 16)
            sp.wait_ge(parts_out, 16 * 3 * (E + 1))
            sp.wait_ge(w_ffn, 32)

        @blk.gpsimd
        def _(pool):
            g = nc.gpsimd
            st = Steps(pool, made)
            g.memset(half[:, :], 0.5).then_inc(made, 1)
            g.memset(mhalf[:, :], -0.5).then_inc(made, 1)
            g.memset(c.ident[:, :], 0.0).then_inc(made, 1)
            g.memset(c.identb[:, :], 0.0).then_inc(made, 1)
            g.memset(c.ones[:, :], 1.0).then_inc(made, 1)
            g.memset(c.onesb[:, :], 1.0).then_inc(made, 1)
            g.memset(c.tri[:, :], 1.0).then_inc(made, 1)
            g.memset(c.tie[:, :, :], 0.0).then_inc(made, 1)
            g.memset(c.mask[:, :, :], 0.0).then_inc(made, 1)
            g.memset(c.b1s[:, :, :], 0.0).then_inc(made, 1)
            g.memset(c.cst[:, :, :], 0.0).then_inc(made, 1)
            g.memset(c.w1[:, E, :], 0.0).then_inc(made, 1)
            g.memset(c.w2[:, E, :, :], 0.0).then_inc(made, 1)
            pool.wait_ge(made, 13)
            for eye in (c.ident, c.identb):
                g.affine_select(out=eye[:, :], in_=eye[:, :], compare_op=ALU.not_equal, fill=1.0,
                                base=0, pattern=[[-1, P]], channel_multiplier=1).then_inc(made, 1)
            g.affine_select(out=c.tri[:, :], in_=c.tri[:, :], compare_op=ALU.is_gt, fill=0.0,
                            base=0, pattern=[[1, P]], channel_multiplier=-1).then_inc(made, 1)
            g.affine_select(out=c.tie[:, :, :], in_=c.tie[:, :, :], compare_op=ALU.is_ge, fill=TIE,
                            base=0, pattern=[[-P, TPB], [1, S]], channel_multiplier=-1).then_inc(made, 1)
            g.affine_select(out=c.mask[:, :, :], in_=c.mask[:, :, :], compare_op=ALU.is_ge, fill=-3e38,
                            base=0, pattern=[[0, 4], [-1, P]], channel_multiplier=1).then_inc(made, 1)
            g.iota(iota_i[:, :], pattern=[[1, P]], base=0, channel_multiplier=0).then_inc(ints, 1)
            g.iota(part_i[:, :], pattern=[[0, 1]], base=0, channel_multiplier=1).then_inc(ints, 1)
            g.iota(tile_i[:, :], pattern=[[1, NT]], base=1, channel_multiplier=0).then_inc(ints, 1)
            g.iota(down_i[:, :], pattern=[[-1, E]], base=E, channel_multiplier=0).then_inc(ints, 1)
            pool.wait_ge(powask, 1)
            g.tensor_tensor(c.wnorm[:, :], sq[:, :], half[:, :], ALU.pow).then_inc(pows, 1)
            for k in range(4):
                pool.wait_ge(powask, k + 2)
                g.tensor_tensor(col[:, 8 + k:9 + k], col[:, 4 + k:5 + k], mhalf[:, :], ALU.pow).then_inc(pows, 1)

        @blk.scalar
        def _(act):
            act.wait_ge(b1_t, 1)
            nc.scalar.activation(gelu_b1[:, :], pm[0][:, 0:E * FC], ACT.Gelu).then_inc(b1_g, 1)

        @blk.tensor
        def _(pe):
            pe.wait_ge(w_in, 16 * N_SMALL)
            pe.wait_ge(made, 18)
            nc.tensor.transpose(pm[0][:, 0:E * FC], b1_chunks[:, :], c.ident[0:E * FC, 0:E * FC]).then_inc(b1_t, 1)
            nc.tensor.transpose(pm[1][:, 0:E], waff_n[:, :], c.ident[0:E, 0:E]).then_inc(small_t, 1)
            pe.wait_ge(b1_g, 1)
            pe.wait_ge(w_ffn, 32)
            for e in range(E):
                for k in range(FC):
                    last = nc.tensor.matmul(pm[2 + e // 4][0:1, (e % 4) * D:(e % 4 + 1) * D],
                                            gelu_b1[:, e * FC + k:e * FC + k + 1], c.w2[:, e, k, :],
                                            start=(k == 0), stop=(k == FC - 1))
            last.then_inc(k_done, 1)
            pe.wait_ge(ask, 1)
            nc.tensor.matmul(pm[1][:, 16:16 + E], c.ones[:, :], sq[:, :], start=True, stop=True).then_inc(told, 1)
            for w, n in enumerate((3 * D, D)):
                pe.wait_ge(ask, 2 + 3 * w)
                nc.tensor.matmul(pm[4][:, 0:1], c.ones[:, :], col[:, 2:3], start=True, stop=True).then_inc(told, 1)
                pe.wait_ge(ask, 3 + 3 * w)
                nc.tensor.matmul(pm[5][:, 0:n], v_bc[:, :], w_raw[w][:, :], start=True, stop=True).then_inc(told, 1)
                pe.wait_ge(ask, 4 + 3 * w)
                nc.tensor.matmul(pm[4][:, 0:1], c.ones[:, :], col[:, 2:3], start=True, stop=True).then_inc(told, 1)

        @blk.vector
        def _(dve):
            v = nc.vector
            s = Steps(dve, vstep)
            dve.wait_ge(ints, 4)
            for dst, src in ((c.iota[:, :], iota_i[:, :]), (c.part[:, :], part_i[:, :]),
                             (c.tile1[:, :], tile_i[:, :]), (c.down[:, :], down_i[:, :])):
                s.step(v.tensor_copy(dst, src))
            dve.wait_ge(w_in, 16 * N_SMALL)
            for r in range(3):
                s.step(v.tensor_copy(b1_parts[:, r, :], b1_rows[:, :] if r == 0 else b1_rest[:, :]))
                b1_split_now = v.tensor_tensor(b1_rest[:, :], b1_rows[:, :] if r == 0 else b1_rest[:, :],
                                               b1_parts[:, r, :], ALU.subtract)
                b1_split_now.then_inc(b1_split, 1)
                dve.wait_ge(b1_split, r + 1)
            dve.wait_ge(small_t, 1)
            s.step(v.tensor_copy(c.waff_t[:, :], pm[1][:, 0:E]))
            v.tensor_tensor(sq[:, :], c.waff_t[:, :], c.waff_t[:, :], ALU.mult).then_inc(ask, 1)
            dve.wait_ge(told, 1)
            v.tensor_copy(sq[:, :], pm[1][:, 16:16 + E]).then_inc(powask, 1)
            dve.wait_ge(pows, 1)
            for w, n in enumerate((3 * D, D)):
                s.step(v.tensor_tensor(prod[:, 0:n], w_raw[w][:, :], u_row[w][:, :], ALU.mult))
                s.step(v.tensor_reduce(col[:, 0:1], prod[:, 0:n], axis=AX.X, op=ALU.add))
                v.tensor_tensor(col[:, 2:3], col[:, 0:1], col[:, 0:1], ALU.mult).then_inc(ask, 1)
                dve.wait_ge(told, 2 + 3 * w)
                v.tensor_copy(col[:, 4 + 2 * w:5 + 2 * w], pm[4][:, 0:1]).then_inc(powask, 1)
                dve.wait_ge(pows, 2 + 2 * w)
                s.step(v.tensor_tensor(col[:, 1:2], col[:, 0:1], col[:, 8 + 2 * w:9 + 2 * w], ALU.mult))
                v.tensor_scalar(v_bc[:, :], c.ones[:, :], col[:, 1:2], None, ALU.mult).then_inc(ask, 1)
                dve.wait_ge(told, 3 + 3 * w)
                s.step(v.tensor_copy(u2[:, 0:n], pm[5][:, 0:n]))
                s.step(v.tensor_tensor(prod[:, 0:n], u2[:, 0:n], u2[:, 0:n], ALU.mult))
                v.tensor_reduce(col[:, 5 + 2 * w:6 + 2 * w], prod[:, 0:n], axis=AX.X, op=ALU.add).then_inc(powask, 1)
                dve.wait_ge(pows, 3 + 2 * w)
                s.step(v.tensor_scalar(u2[:, 0:n], u2[:, 0:n], col[:, 9 + 2 * w:10 + 2 * w], None, ALU.mult))
                s.step(v.tensor_tensor(prod[:, 0:n], w_raw[w][:, :], u2[:, 0:n], ALU.mult))
                s.step(v.tensor_reduce(col[:, 3:4], prod[:, 0:n], axis=AX.X, op=ALU.add))
                v.tensor_tensor(col[:, 2:3], col[:, 3:4], col[:, 1:2], ALU.mult).then_inc(ask, 1)
                dve.wait_ge(told, 4 + 3 * w)
                s.step(v.reciprocal(col[:, 12:13], pm[4][:, 0:1]))
                s.step(v.tensor_tensor(col[:, 13:14], col[:, 12:13], sig[:, w:w + 1], ALU.mult))
                if w == 0:
                    for i, out in enumerate((c.wq, c.wk)):
                        s.step(v.tensor_scalar(out[:, :].rearrange("p (r d g) -> p r d g", r=2, d=HD),
                                               w_raw[0][:, i * D:(i + 1) * D].rearrange("p (g r d) -> p r d g", r=2, d=HD),
                                               col[:, 13:14], None, ALU.mult))
                    s.step(v.tensor_scalar(c.wv[:, :], w_raw[0][:, 2 * D:3 * D], col[:, 13:14], None, ALU.mult))
                else:
                    s.step(v.tensor_scalar(c.wproj[:, :], w_raw[1][:, :], col[:, 13:14], None, ALU.mult))
            dve.wait_ge(k_done, 1)
            k_row = const_row[:, 0:E, :]
            for h in range(2):
                s.step(v.tensor_copy(const_row[:, 4 * h:4 * h + 4, :].rearrange("a e d -> a (e d)"), pm[2 + h][0:1, :]))
            s.step(v.tensor_tensor(b2_row[:, :, :], b2_row[:, :, :], k_row, ALU.add))
            s.step(v.tensor_reduce(sum_row[:, :], b2_row[:, :, :].rearrange("a e d -> a d e"), axis=AX.X, op=ALU.add))
            s.step(v.tensor_scalar(k_row, k_row, -1.0, None, ALU.mult))
            s.step(v.memset(const_row[:, E, :], 0.0))
            s.step(v.tensor_tensor(const_row[:, :, :], const_row[:, :, :],
                                   sum_row[:, :].unsqueeze(1).to_broadcast([1, G, D]), ALU.add))
            flat = const_row[:, :, :].rearrange("a g d -> a (g d)")
            rest = rest_row[:, :, :].rearrange("a g d -> a (g d)")
            for r in range(3):
                s.step(v.tensor_copy(const_parts[:, r, :], flat if r == 0 else rest))
                v.tensor_tensor(rest, flat if r == 0 else rest, const_parts[:, r, :], ALU.subtract).then_inc(const_split, 1)
                dve.wait_ge(const_split, r + 1)


def token_stats(nc, m, io, c, x_dram):
    ctx = ExitStack()
    with ctx:
        t = Mem(nc, ctx)
        NX = 4
        XCREDIT = NX * TPB
        CREDIT = 2 * TPB
        x_row = [t.sb(f"ts_x{k}", [P, TPB, XW]) for k in range(NX)]
        bn = t.sb("ts_bn", [P, 2, TPB, 6])
        vare = t.sb("ts_vare", [P, 2, TPB, 2])
        powers = t.sb("ts_powers", [P, TPB, 2])
        xn = [t.sb(f"ts_xn{k}", [P, TPB, D]) for k in range(2)]
        xn_t = [t.sb(f"ts_xnt{k}", [P, S]) for k in range(2)]
        p_t = [t.ps(f"ts_pt{k}", [P, S]) for k in range(2)]
        p_n = [t.ps(f"ts_pn{k}", [P, TPB, E]) for k in range(2)]
        x_in = [t.sem(f"ts_in{k}") for k in range(NX)]
        x_out = [t.sem(f"ts_out{k}") for k in range(NX)]
        pad, bn_done, mv_done, var_done, rstd = t.sem("ts_pad"), t.sem("ts_bnd"), t.sem("ts_mv"), t.sem("ts_var"), t.sem("ts_rstd")
        xn_done, tr, tr_out, num, num_out = t.sem("ts_xnd"), t.sem("ts_tr"), t.sem("ts_tro"), t.sem("ts_num"), t.sem("ts_numo")
        xnorm_done = t.sem("ts_xnorm")
        passed = t.sem("ts_passed")
        blk = ctx.enter_context(nc.Block())
        x_v = x_dram.rearrange("(b k p) d -> p b k d", k=TPB, p=P)
        row_v = io["rows"].rearrange("(b k p) w -> p b k w", k=TPB, p=P)

        @blk.sync
        def _(sp):
            with sp.Fori(0, B // NX) as i:
                for k in range(NX):
                    b = i * NX + k
                    sp.wait_ge(x_out[k], i * 16)
                    sp.wait_ge(xn_done, b * TPB + TPB)
                    sp.sem_inc(passed, 1)
                    sp.wait_ge(xnorm_done, b + 1)
                    sp.sem_inc(passed, 1)
                    sp.dma_start(x_row[k][:, :, 0:D], x_v[:, ds(b, 1), :, :]).then_inc(x_in[k], 16)

        @blk.gpsimd
        def _(pool):
            pool.sem_inc(xnorm_done, NX)
            nc.gpsimd.memset(powers[:, :, 0:1], -0.5).then_inc(pad, 1)
            nc.gpsimd.memset(powers[:, :, 1:2], 0.5).then_inc(pad, 1)
            for k in range(NX):
                nc.gpsimd.memset(x_row[k][:, :, D + 3:XW], 0.0).then_inc(pad, 1)
            pool.wait_ge(pad, NX + 2)
            with pool.Fori(0, B // NX) as i:
                for k in range(NX):
                    b = i * NX + k
                    pool.wait_ge(var_done, b + 1)
                    nc.gpsimd.tensor_tensor(x_row[k][:, :, D + 1:D + 3], vare[:, k % 2, :, :], powers[:, :, :], ALU.pow).then_inc(rstd, 1)
                    pool.wait_ge(rstd, b + 1)
                    nc.gpsimd.tensor_tensor(c.xnorm[:, ds(b * TPB, TPB)], x_row[k][:, :, D + 1], x_row[k][:, :, D + 2], ALU.mult).then_inc(xnorm_done, 1)

        @blk.scalar
        def _(act):
            act.wait_ge(pad, NX + 2)
            with act.Fori(0, B // NX) as i:
                for k in range(NX):
                    b = i * NX + k
                    act.wait_ge(rstd, b + 1)
                    act.dma_start(row_v[:, ds(b, 1), :, :], x_row[k][:, :, :]).then_inc(x_out[k], 16)
                    act.wait_ge(tr, b * TPB + TPB + CREDIT)
                    nc.scalar.activation(xn_t[k % 2][:, :], p_t[k % 2][:, :], ACT.Copy).then_inc(tr_out, 1)
                    act.wait_ge(num, b + 1)
                    nc.scalar.activation(c.num[:, ds(b * TPB, TPB), :], p_n[k % 2][:, :, :], ACT.Copy).then_inc(num_out, 1)
            for k in range(NX):
                act.wait_ge(x_out[k], 16 * (B // NX))

        @blk.vector
        def _(dve):
            v = nc.vector

            def stats(b, k):
                q = k % 2
                dve.wait_ge(x_in[k], b * (16 // NX) + (16 - k * (16 // NX)))
                dve.wait_ge(mv_done, b * TPB)
                for j in range(TPB):
                    v.bn_stats(bn[:, q, j, :], x_row[k][:, j, 0:D]).then_inc(bn_done, 1)
                for j in range(TPB):
                    dve.wait_ge(bn_done, b * TPB + (j + 1))
                    dve.sem_inc(passed, 1)
                    v.bn_aggr(x_row[k][:, j, D:D + 2], bn[:, q, j, :]).then_inc(mv_done, 1)
                dve.wait_ge(mv_done, b * TPB + TPB)
                v.tensor_copy(vare[:, q, :, 1], x_row[k][:, :, D + 1])
                v.tensor_scalar(vare[:, q, :, 0], x_row[k][:, :, D + 1], LN_EPS, None, ALU.add).then_inc(var_done, 1)

            def norm(b, k):
                dve.wait_ge(rstd, b + 1)
                dve.wait_ge(tr, b * TPB + TPB)
                for j in range(TPB):
                    v.tensor_scalar(xn[k % 2][:, j, :], x_row[k][:, j, 0:D], x_row[k][:, j, D:D + 1],
                                    x_row[k][:, j, D + 1:D + 2], ALU.subtract, ALU.mult).then_inc(xn_done, 1)

            dve.sem_inc(xn_done, XCREDIT)
            stats(0, 0)
            with dve.Fori(0, B // NX - 1) as i:
                for k in range(NX):
                    stats(i * NX + (k + 1), (k + 1) % NX)
                    norm(i * NX + k, k)
            for k in range(NX):
                if k + 1 < NX:
                    stats(B - NX + k + 1, k + 1)
                norm(B - NX + k, k)

        @blk.tensor
        def _(pe):
            pe.sem_inc(tr, CREDIT)
            with pe.Fori(0, B // NX) as i:
                for k in range(NX):
                    b = i * NX + k
                    q = k % 2
                    for j in range(TPB):
                        pe.wait_ge(xn_done, b * TPB + (j + 1 + XCREDIT))
                        nc.tensor.transpose(p_t[q][:, j * P:(j + 1) * P], xn[q][:, j, :], c.ident[:, :]).then_inc(tr, 1)
                    pe.wait_ge(tr_out, b + 1)
                    for j in range(TPB):
                        last = nc.tensor.matmul(p_n[q][:, j, :], xn_t[q][:, j * P:(j + 1) * P], c.waff_t[:, :],
                                                start=True, stop=True)
                    last.then_inc(num, 1)


def consts(nc, m):
    class C:
        pass
    c = C()
    c.ident, c.ones = m.sb("ident", [P, P]), m.sb("ones", [P, P])
    c.identb, c.onesb, c.tri = (m.sb(n, [P, P], BF16) for n in ("identb", "onesb", "tri"))
    c.tie = m.sb("tie", [P, TPB, S])
    c.mask = m.sb("mask", [P, 4, P], BF16)
    c.iota, c.part, c.tile1, c.down = m.sb("iota", [P, P]), m.sb("part", [P, 1]), m.sb("tile1", [P, NT]), m.sb("down", [P, E])
    c.w1, c.w2 = m.sb("w1", [P, G, F]), m.sb("w2", [P, G, FC, D])
    c.b1s, c.cst = m.sb("b1s", [P, G, F], BF16), m.sb("cst", [P, G, D], BF16)
    c.waff_t, c.wnorm, c.thr = m.sb("waff_t", [P, E]), m.sb("wnorm", [P, E]), m.sb("thr", [P, 1])
    c.wq, c.wk, c.wv, c.wproj = (m.sb(n, [P, D]) for n in ("wq", "wk", "wv", "wproj"))
    c.num, c.xnorm = m.sb("num", [P, NT, E]), m.sb("xnorm", [P, NT])
    c.gidx, c.sidx = m.sb("gidx", [P, NSX], I32), m.sb("sidx", [P, NSX], I32)
    c.eid = m.sb("eid", [1, NSX], I32)
    return c


def route(nc, m, c, tag):
    ctx = ExitStack()
    with ctx:
        t = Mem(nc, ctx)

        def sb(name, shape, dt=F32):
            return t.sb(f"{tag}_{name}", shape, dt)

        def sem(name):
            return t.sem(f"{tag}_{name}")

        GT = G * NT
        den = sb("den", [P, NT, E])
        AHEAD = 2 * TPB
        both = sb("both", [P, NT + AHEAD, 2 * E])
        aff, hot = both[:, 0:NT, 0:E], both[:, 0:NT, E:2 * E]
        amax, wmax, weight = sb("amax", [P, NT]), sb("wmax", [P, NT]), sb("weight", [P, NT, E])
        cell = sb("cell", [P, 8])
        batch_s = [sb(f"batch{k}", [P, TPB, 2 * E]) for k in range(2)]
        batch_t = [sb(f"batcht{k}", [P, 2 * S]) for k in range(2)]
        beats = [sb(f"beats{k}", [P, S]) for k in range(2)]
        rank, kept = sb("rank", [P, NT]), sb("kept", [P, NT])
        taken = sb("taken", [P, G, NT], BF16)
        total, upto = sb("total", [P, GT]), sb("upto", [P, GT])
        one_row = sb("one_row", [P, GT])
        ends, count, tiles, tile_end, start, shift = (sb(n, [P, G]) for n in ("ends", "count", "tiles", "tend", "start", "shift"))
        place, slot, row, colp = sb("place", [P, GT]), sb("slot", [P, NT]), sb("row", [P, NT]), sb("colp", [P, NT])
        eid_f = [sb(f"eidf{k}", [P, NSX]) for k in range(2)]
        NR = 4
        at_p = [sb(f"atp{k}", [P, NR, P], BF16) for k in range(2)]
        at_s = [sb(f"ats{k}", [P, NR, NS], BF16) for k in range(2)]
        at_t = [sb(f"att{k}", [P, NR, 2, NS], BF16) for k in range(2)]
        zero = sb("zero", [P, 2 * NS], BF16)
        lo, src, gsrc, away = sb("lo", [P, NS]), sb("src", [P, NS]), sb("gsrc", [P, NS]), sb("away", [P, NS])
        ps_sum = t.ps(f"{tag}_ps_sum", [P, 1])
        ps_t = [t.ps(f"{tag}_ps_t{k}", [P, 2 * S]) for k in range(2)]
        ps_b = [t.ps(f"{tag}_ps_b{k}", [P, TPB, S]) for k in range(2)]
        ps_pre = [t.ps(f"{tag}_ps_pre{k}", [P, 512]) for k in range(2)]
        ps_inv = t.ps(f"{tag}_ps_inv", [P, 2 * NS])

        vs, made = sem("vs"), sem("made")
        sum_ask, sum_got, e_ask, e_got = sem("sum_ask"), sem("sum_got"), sem("e_ask"), sem("e_got")
        hot_done, cut, tr, tr_out, row_b, ranked = (sem(n) for n in ("hot", "cut", "tr", "tro", "rowb", "ranked"))
        taken_done, counted, copied = sem("taken_done"), sem("counted"), sem("copied")
        s_done, onehot, put, inv = (sem(n) for n in ("s_done", "onehot", "put", "inv"))
        blk = ctx.enter_context(nc.Block())
        ROW_CREDIT = 2
        HB = GT // 2

        @blk.gpsimd
        def _(pool):
            nc.gpsimd.memset(both[:, NT:NT + AHEAD, :], 0.0).then_inc(made, 1)
            for k in range(2):
                nc.gpsimd.memset(batch_t[k][:, :], 0.0).then_inc(made, 1)
            nc.gpsimd.memset(zero[:, :], 0.0).then_inc(made, 1)
            nc.gpsimd.memset(one_row[:, :], 1.0).then_inc(made, 1)
            nc.gpsimd.memset(c.gidx[:, NS:NSX], 0).then_inc(made, 1)
            nc.gpsimd.memset(c.sidx[:, NS:NSX], 0).then_inc(made, 1)

        @blk.scalar
        def _(act):
            act.wait_ge(e_ask, 1)
            nc.scalar.activation(cell[:, 2:3], cell[:, 1:2], ACT.Exp, scale=-1.0).then_inc(e_got, 1)
            act.wait_ge(hot_done, 1)
            act.wait_ge(made, 7)
            for b in range(2):
                nc.scalar.activation(batch_s[b][:, :, :], both[:, b * TPB:(b + 1) * TPB, :], ACT.Copy).then_inc(cut, 1)
            with act.Fori(0, B // 2) as i:
                for k in range(2):
                    b = i * 2 + k
                    act.wait_ge(tr, b * 4 + 4)
                    act.wait_ge(row_b, b + 1)
                    nc.scalar.activation(batch_t[k][0:E, :], ps_t[k][0:E, :], ACT.Copy).then_inc(tr_out, 1)
                    nc.scalar.activation(batch_s[k][:, :, :], both[:, ds(b * TPB + 2 * TPB, TPB), :], ACT.Copy).then_inc(cut, 1)

        @blk.tensor
        def _(pe):
            pe.wait_ge(sum_ask, 1)
            nc.tensor.matmul(ps_sum[:, :], c.ones[:, :], cell[:, 0:1], start=True, stop=True).then_inc(sum_got, 1)
            pe.sem_inc(row_b, ROW_CREDIT)

            def as_rows(b, k):
                pe.wait_ge(cut, b + 1)
                for w in range(2):
                    for j in range(TPB):
                        nc.tensor.transpose(ps_t[k][0:E, w * S + j * P:w * S + (j + 1) * P],
                                            batch_s[k][:, j, w * E:(w + 1) * E], c.ident[:, :]).then_inc(tr, 1)

            as_rows(0, 0)
            with pe.Fori(0, B // 2) as i:
                for k in range(2):
                    b = i * 2 + k
                    as_rows(b + 1, (k + 1) % 2)
                    pe.wait_ge(tr_out, b + 1)
                    pe.wait_ge(ranked, b * TPB + TPB)
                    for j in range(TPB):
                        last = nc.tensor.matmul(ps_b[k][:, j, :], batch_t[k][:, S + j * P:S + (j + 1) * P],
                                                batch_t[k][:, 0:S], start=True, stop=True)
                    last.then_inc(row_b, 1)
            pe.wait_ge(taken_done, 2)
            flat = taken[:, :, :].rearrange("p g t -> p (g t)")
            for h in range(2):
                nc.tensor.matmul(ps_pre[h][:, 0:HB], c.onesb[:, :], flat[:, h * HB:(h + 1) * HB], start=True, stop=True).then_inc(counted, 1)
            for h in range(2):
                pe.wait_ge(copied, h + 1)
                nc.tensor.matmul(ps_pre[h][:, 0:HB], c.tri[:, :], flat[:, h * HB:(h + 1) * HB], start=True, stop=True).then_inc(counted, 1)
            nc.tensor.matmul(ps_inv[:, :], zero[:, 0:P], zero[:, :], start=True, stop=False, skip_group_check=True)
            pe.sem_inc(put, 2 * NR)
            with pe.Fori(0, NT // NR // 2) as i:
                for k in range(2):
                    pe.wait_ge(onehot, i * 2 + (k + 1))
                    for r in range(NR):
                        nc.tensor.matmul(ps_inv[:, :], at_p[k][:, r, :], at_t[k][:, r, :, :].rearrange("p a s -> p (a s)"),
                                         start=False, stop=False, skip_group_check=True).then_inc(put, 1)
            nc.tensor.matmul(ps_inv[:, :], zero[:, 0:P], zero[:, :], start=False, stop=True, skip_group_check=True).then_inc(inv, 1)

        @blk.vector
        def _(dve):
            v = nc.vector
            s = Steps(dve, vs)

            def bc(col, shape, axis):
                return col.unsqueeze(axis).to_broadcast(shape)

            full = [P, NT, E]
            s.step(v.tensor_tensor(den[:, :, :], bc(c.xnorm[:, :], full, 2), bc(c.wnorm[:, :], full, 1), ALU.mult))
            s.step(v.tensor_scalar(den[:, :, :], den[:, :, :], float(D) ** 0.5, 1e-9, ALU.mult, ALU.add))
            s.step(v.reciprocal(den[:, :, :], den[:, :, :]))
            s.step(v.tensor_tensor(aff, c.num[:, :, :], den[:, :, :], ALU.mult))
            v.tensor_reduce(cell[:, 0:1], aff, axis=AX.XY, op=ALU.add).then_inc(sum_ask, 1)
            s.step(v.tensor_reduce(amax[:, :], aff, axis=AX.X, op=ALU.max))
            s.step(v.tensor_tensor(weight[:, :, :], aff, bc(amax[:, :], full, 2), ALU.is_equal))
            s.step(v.tensor_tensor(weight[:, :, :], weight[:, :, :], bc(c.down[:, :], full, 1), ALU.mult))
            s.step(v.tensor_reduce(wmax[:, :], weight[:, :, :], axis=AX.X, op=ALU.max))
            v.tensor_tensor(hot, weight[:, :, :], bc(wmax[:, :], full, 2), ALU.is_equal).then_inc(hot_done, 1)
            dve.wait_ge(sum_got, 1)
            v.scalar_tensor_tensor(cell[:, 1:2], ps_sum[:, :], 1.0 / (T * E), c.thr[:, :], ALU.mult, ALU.subtract).then_inc(e_ask, 1)
            dve.wait_ge(e_got, 1)
            s.step(v.tensor_scalar(cell[:, 3:4], cell[:, 2:3], 1.0, None, ALU.add))
            s.step(v.reciprocal(cell[:, 4:5], cell[:, 3:4]))
            s.step(v.tensor_scalar(cell[:, 5:6], cell[:, 4:5], float(S), 4.0, ALU.mult, ALU.max))
            dve.sem_inc(ranked, 2 * TPB)
            with dve.Fori(0, B // 2) as i:
                for k in range(2):
                    b = i * 2 + k
                    dve.wait_ge(row_b, b + (1 + ROW_CREDIT))
                    for j in range(TPB):
                        dve.wait_ge(ranked, b * TPB + (j + 2 * TPB - 1))
                        v.scalar_tensor_tensor(beats[j][:, :], ps_b[k][:, j, :], amax[:, ds(b * TPB + j, 1)],
                                               c.tie[:, j, :], ALU.subtract, ALU.is_gt,
                                               accum_out=rank[:, ds(b * TPB + j, 1)]).then_inc(ranked, 1)
            dve.wait_ge(ranked, NT + 2 * TPB)
            s.step(v.tensor_scalar(kept[:, :], rank[:, :], 1.0, cell[:, 5:6], ALU.add, ALU.is_le))
            v.tensor_tensor(taken[:, 0:E, :].rearrange("p e t -> p t e"), hot, bc(kept[:, :], full, 2), ALU.mult).then_inc(taken_done, 1)
            v.tensor_scalar(taken[:, E, :], kept[:, :], -1.0, 1.0, ALU.mult, ALU.add).then_inc(taken_done, 1)
            dve.wait_ge(made, 7)
            for h in range(2):
                dve.wait_ge(counted, h + 1)
                v.tensor_copy(total[:, h * HB:(h + 1) * HB], ps_pre[h][:, 0:HB]).then_inc(copied, 1)
            dve.wait_ge(copied, 2)
            s.step(v.tensor_tensor_scan(upto[:, :], one_row[:, :], total[:, :], 0.0, ALU.mult, ALU.add))
            s.step(v.tensor_copy(ends[:, :], upto[:, :].rearrange("p (g t) -> p g t", g=G)[:, :, NT - 1]))
            s.step(v.tensor_copy(count[:, :], ends[:, :]))
            s.step(v.tensor_tensor(count[:, 1:G], ends[:, 1:G], ends[:, 0:G - 1], ALU.subtract))
            s.step(v.tensor_scalar(tiles[:, :], count[:, :], 1.0 / P, (P - 1) / P - 0.49609375, ALU.mult, ALU.add))
            s.step(v.tensor_scalar(tiles[:, :], tiles[:, :], MAGIC, None, ALU.add))
            s.step(v.tensor_scalar(tiles[:, :], tiles[:, :], MAGIC, None, ALU.subtract))
            s.step(v.tensor_tensor_scan(tile_end[:, :], one_row[:, 0:G], tiles[:, :], 0.0, ALU.mult, ALU.add))
            s.step(v.tensor_tensor(start[:, :], tile_end[:, :], tiles[:, :], ALU.subtract))
            s.step(v.tensor_tensor(shift[:, :], count[:, :], ends[:, :], ALU.subtract))
            s.step(v.scalar_tensor_tensor(shift[:, :], start[:, :], float(P), shift[:, :], ALU.mult, ALU.add))
            grid = "p (g t) -> p g t"
            s.step(v.tensor_tensor(upto[:, :], upto[:, :], total[:, :], ALU.subtract))
            s.step(v.tensor_tensor(upto[:, :].rearrange(grid, g=G), upto[:, :].rearrange(grid, g=G),
                                   bc(shift[:, :], [P, G, NT], 2), ALU.add))
            for h in range(2):
                dve.wait_ge(counted, h + 3)
                s.step(v.tensor_tensor(place[:, h * HB:(h + 1) * HB], ps_pre[h][:, 0:HB], upto[:, h * HB:(h + 1) * HB], ALU.add))
            s.step(v.tensor_tensor(place[:, :].rearrange(grid, g=G), place[:, :].rearrange(grid, g=G), taken[:, :, :], ALU.mult))
            s.step(v.tensor_reduce(slot[:, :], place[:, :].rearrange("p (g t) -> p t g", g=G), axis=AX.X, op=ALU.add))
            s.step(v.tensor_scalar(row[:, :], slot[:, :], 1.0 / P, -0.49609375, ALU.mult, ALU.add))
            s.step(v.tensor_scalar(row[:, :], row[:, :], MAGIC, None, ALU.add))
            s.step(v.tensor_scalar(row[:, :], row[:, :], MAGIC, None, ALU.subtract))
            s.step(v.scalar_tensor_tensor(colp[:, :], row[:, :], float(-P), slot[:, :], ALU.mult, ALU.add))
            grid = [P, NR, NS]
            with dve.Fori(0, NT // NR // 2) as i:
                for k in range(2):
                    n = i * 2 + k
                    v.tensor_tensor(at_s[k][:, :, :], bc(c.iota[:, 0:NS], grid, 1), bc(row[:, ds(n * NR, NR)], grid, 2),
                                    ALU.is_equal).then_inc(s_done, 1)
                    dve.wait_ge(put, n * NR + NR)
                    v.tensor_tensor(at_p[k][:, :, :], bc(c.iota[:, :], [P, NR, P], 1), bc(colp[:, ds(n * NR, NR)], [P, NR, P], 2),
                                    ALU.is_equal)
                    dve.wait_ge(s_done, n + 1)
                    v.tensor_scalar(at_t[k][:, :, 1, :], at_s[k][:, :, :], c.part[:, :], None, ALU.mult)
                    v.tensor_tensor(at_t[k][:, :, 0, :], at_s[k][:, :, :], bc(c.tile1[:, ds(n * NR, NR)], grid, 2),
                                    ALU.mult).then_inc(onehot, 1)
            s.step(v.tensor_scalar(eid_f[0][:, :], c.iota[:, 0:NSX], tile_end[:, 0:1], None, ALU.is_ge))
            for g in range(1, E):
                s.step(v.scalar_tensor_tensor(eid_f[g % 2][:, :], c.iota[:, 0:NSX], tile_end[:, g:g + 1],
                                              eid_f[(g - 1) % 2][:, :], ALU.is_ge, ALU.add))
            s.step(v.tensor_copy(c.eid[:, :], eid_f[(E - 1) % 2][0:1, :]))
            dve.wait_ge(inv, 1)
            s.step(v.tensor_scalar(lo[:, :], ps_inv[:, NS:2 * NS], float(-P), None, ALU.add))
            s.step(v.scalar_tensor_tensor(src[:, :], ps_inv[:, 0:NS], float(P), lo[:, :], ALU.mult, ALU.add))
            s.step(v.tensor_scalar(gsrc[:, :], src[:, :], 0.0, None, ALU.max))
            s.step(v.tensor_copy(c.gidx[:, 0:NS], gsrc[:, :]))
            s.step(v.tensor_scalar(away[:, :], src[:, :], 0.0, float(4 * T), ALU.is_lt, ALU.mult))
            s.step(v.tensor_tensor(away[:, :], away[:, :], src[:, :], ALU.add))
            s.step(v.tensor_copy(c.sidx[:, 0:NS], away[:, :]))


def experts(nc, m, io, c, tag, y_dram):
    ctx = ExitStack()
    with ctx:
        t = Mem(nc, ctx)

        def sem(name):
            return t.sem(f"{tag}_{name}")

        OWN = 4
        HU = U // 2
        x_row = [t.sb(f"{tag}_x{k}", [P, XW]) for k in range(U)]
        y_row = [t.sb(f"{tag}_y{k}", [P, D]) for k in range(U)]
        gi, si = ([t.sb(f"{tag}_{n}{h}", [P, HU], I32) for h in range(2)] for n in ("gi", "si"))
        xn = [t.sb(f"{tag}_xn{k}", [P, D]) for k in range(2)]
        xn_t = [t.sb(f"{tag}_xnt{k}", [P, P]) for k in range(2)]
        hid_t = [t.sb(f"{tag}_ht{k}", [P, FC, P]) for k in range(2)]
        w1_own = [t.sb(f"{tag}_w1own{k}", [P, F]) for k in range(OWN)]
        ps_x = [t.ps(f"{tag}_ps_x{k}", [P, P]) for k in range(2)]
        ps_h = [t.ps(f"{tag}_ps_h{k}", [P, FC, P]) for k in range(2)]
        ps_y = [t.ps(f"{tag}_ps_y{k}", [P, D]) for k in range(2)]
        x_in = [sem(f"xin{k}") for k in range(U)]
        y_out = [sem(f"yout{k}") for k in range(U)]
        cell = sem("cell")
        xn_done, x_tr, x_tr_out, up, gelu, down, y_done, w1_done = (
            sem(n) for n in ("xn", "xtr", "xtro", "up", "gelu", "down", "y", "w1"))
        passed = sem("passed")
        BOTH = 2
        blk = ctx.enter_context(nc.Block())
        rows = io["rows"]

        def experts_of(eng, j, n):
            _, e = nc.values_load_multi_w_load_instructions(c.eid[0:1, ds(j, n)], engines=[eng.engine], min_val=0, max_val=E)
            return e

        @blk.sync
        def _(sp):
            for k in range(U):
                sp.wait_ge(y_out[k], 16 * (NS // U))

        @blk.gpsimd
        def _(pool):
            g = nc.gpsimd

            def gather(k):
                pool.indirect_dma_start(x_row[k][:, :], None, rows,
                                        bass.IndirectOffsetOnAxis(ap=gi[k // HU][:, k % HU:k % HU + 1], axis=0)).then_inc(x_in[k], 16)

            for h in range(2):
                g.tensor_copy(gi[h][:, :], c.gidx[:, h * HU:(h + 1) * HU]).then_inc(cell, 1)
            pool.wait_ge(cell, 2)
            for k in range(U):
                gather(k)
            with pool.Fori(0, NS // U) as i:
                for h in range(2):
                    for k in range(h * HU, (h + 1) * HU):
                        pool.wait_ge(x_in[k], i * 16 + 16)
                        pool.wait_ge(y_out[k], i * 16)
                    pool.sem_inc(passed, 1)
                    g.tensor_copy(gi[h][:, :], c.gidx[:, ds(i * U + (U + h * HU), HU)]).then_inc(cell, 1)
                    g.tensor_copy(si[h][:, :], c.sidx[:, ds(i * U + h * HU, HU)]).then_inc(cell, 1)
                    pool.wait_ge(cell, i * 4 + (2 * h + 4))
                    pool.sem_inc(passed, 1)
                    for k in range(h * HU, (h + 1) * HU):
                        pool.wait_ge(y_done, i * U + (k + 1))
                        pool.sem_inc(passed, 1)
                        pool.indirect_dma_start(y_dram, bass.IndirectOffsetOnAxis(ap=si[h][:, k % HU:k % HU + 1], axis=0),
                                                y_row[k][:, :], None, bounds_check=T - 1, oob_is_err=False).then_inc(y_out[k], 16)
                        gather(k)
            for k in range(U):
                pool.wait_ge(x_in[k], 16 * (NS // U + 1))

        @blk.scalar
        def _(act):
            a = nc.scalar

            def turn_x(j, k):
                act.wait_ge(x_tr, j + 1)
                act.wait_ge(up, j + 1)
                a.activation(xn_t[k][:, :], ps_x[k][:, :], ACT.Copy).then_inc(x_tr_out, 1)

            def bend(j, k):
                act.wait_ge(up, j + (1 + BOTH))
                act.wait_ge(down, j + 1)
                a.activation(hid_t[k][:, :, :], ps_h[k][:, :, :], ACT.Gelu).then_inc(gelu, 1)

            act.sem_inc(gelu, BOTH)
            turn_x(0, 0)
            turn_x(1, 1)
            bend(0, 0)
            with act.Fori(0, NS // U) as i:
                for k in range(U):
                    j = i * U + k
                    turn_x(j + 2, k % 2)
                    bend(j + 1, (k + 1) % 2)

        @blk.tensor
        def _(pe):
            te = nc.tensor

            def turn_x(j, k):
                pe.wait_ge(xn_done, j + 1)
                if not isinstance(j, int):
                    pe.wait_ge(x_tr_out, j - 1)
                te.transpose(ps_x[k][:, :], xn[k][:, :], c.ident[:, :]).then_inc(x_tr, 1)

            def expand(j, k, s, e):
                pe.wait_ge(x_tr_out, j + 1)
                pe.wait_ge(gelu, j + 1)
                pe.wait_ge(w1_done, j + 1)
                for f in range(FC):
                    chunk = slice(f * P, (f + 1) * P)
                    te.matmul(ps_h[k][:, f, :], c.b1s[:, ds(e, 1), chunk].rearrange("p a f -> p (a f)"), c.onesb[:, :], start=True, stop=False)
                    last = te.matmul(ps_h[k][:, f, :], w1_own[s][:, chunk], xn_t[k][:, :],
                                     start=False, stop=True)
                last.then_inc(up, 1)

            def contract(j, k, e):
                pe.wait_ge(gelu, j + (1 + BOTH))
                pe.wait_ge(y_done, j)
                te.matmul(ps_y[k][:, :], c.onesb[:, :], c.cst[:, ds(e, 1), :].rearrange("p a d -> p (a d)"), start=True, stop=False)
                for f in range(FC):
                    last = te.matmul(ps_y[k][:, :], hid_t[k][:, f, :], c.w2[:, ds(e, 1), f, :].rearrange("p a d -> p (a d)"),
                                     start=False, stop=(f == FC - 1))
                last.then_inc(down, 1)

            pe.sem_inc(up, BOTH)
            pe.sem_inc(down, BOTH)
            turn_x(0, 0)
            turn_x(1, 1)
            expand(0, 0, 0, experts_of(pe, 0, 1)[0])
            with pe.Fori(0, NS // U) as i:
                for k in range(U):
                    j = i * U + k
                    if k % HU == 0:
                        e = experts_of(pe, j, HU + 1)
                    turn_x(j + 2, k % 2)
                    expand(j + 1, (k + 1) % 2, (k + 1) % OWN, e[k % HU + 1])
                    contract(j, k % 2, e[k % HU])

        @blk.vector
        def _(dve):
            v = nc.vector

            def norm(j, s, turn):
                dve.wait_ge(x_in[s], turn * 16 + 16)
                v.tensor_scalar(xn[s % 2][:, :], x_row[s][:, 0:D], x_row[s][:, D:D + 1], x_row[s][:, D + 1:D + 2],
                                ALU.subtract, ALU.mult).then_inc(xn_done, 1)

            def fetch(j, s, e):
                if not isinstance(j, int):
                    dve.wait_ge(up, j + (1 + BOTH - OWN))
                v.tensor_copy(w1_own[s][:, :], c.w1[:, ds(e, 1), :].rearrange("p a f -> p (a f)")).then_inc(w1_done, 1)

            def finish(j, s, turn):
                dve.wait_ge(down, j + (1 + BOTH))
                dve.wait_ge(y_out[s], turn * 16)
                v.scalar_tensor_tensor(y_row[s][:, :], ps_y[s % 2][:, :], 0.5, x_row[s][:, 0:D], ALU.mult, ALU.add).then_inc(y_done, 1)

            norm(0, 0, 0)
            norm(1, 1, 0)
            e = experts_of(dve, 0, 2)
            fetch(0, 0, e[0])
            fetch(1, 1, e[1])
            dve.wait_ge(x_tr, 1)
            norm(2, 2, 0)
            with dve.Fori(0, NS // U) as i:
                for k in range(U):
                    j = i * U + k
                    if k % HU == 0:
                        e = experts_of(dve, j + 2, HU)
                    dve.wait_ge(x_tr, j + 2)
                    norm(j + 3, (k + 3) % U, i if k + 3 < U else i + 1)
                    fetch(j + 2, (k + 2) % OWN, e[k % HU])
                    finish(j, k, i)


def attention(nc, m, io, c, x_dram):
    ctx = ExitStack()
    with ctx:
        t = Mem(nc, ctx)
        sb = lambda n, s, dt=F32: t.sb(f"at_{n}", s, dt)
        sem = lambda n: t.sem(f"at_{n}")
        two = lambda n, s, dt=F32: [sb(f"{n}{k}", s, dt) for k in range(2)]
        HP = H // 2
        QUADS = H // 4
        NP = 12
        NQ = 4
        RING = 6
        LAG = 4
        ROWS = 96
        QUERY_TILES = [(0, 1), (2, 3), (4,), (5, 6), (7, 8), (9,), (10, 11)] + [()] * 5
        SCALE = HD ** -0.5

        xa, xr, x2 = two("xa", [P, TPB, D + 2]), two("xr", [P, TPB, D]), two("x2", [P, TPB, XW])
        bn, vare = two("bn", [P, TPB, 6]), two("vare", [P, TPB])
        bn2, vare2 = two("bn2", [P, TPB, 6]), two("vare2", [P, TPB, 2])
        xn, xt = two("xn", [P, TPB, D]), two("xt", [P, S])
        xn2, x2t = two("xn2", [P, TPB, D]), two("x2t", [P, S])
        part, rest = two("part", [P, 3, 2 * S], BF16), two("rest", [P, 2 * S])
        qs = [sb(f"qs{k}", [P, HP, S], BF16) for k in range(NQ)]
        kb = [sb(f"kb{k}", [P, HP, 2, S], BF16) for k in range(NQ)]
        kc = two("kc", [P, HP, S], BF16)
        vp = [sb(f"vp{k}", [P, TPB, H, 32]) for k in range(NQ)]
        pt = [sb(f"pt{k}", [P, 2 * S]) for k in range(RING)]
        ot, on, ont = two("ot", [P, QUADS, S]), two("on", [P, TPB, D]), two("ont", [P, S])
        rden = two("rden", [P, H])
        mx, nm, nr = two("mx", [P, TPB, H]), two("nm", [P, TPB, 2, HP]), two("nr", [P, TPB, H])
        mp, mt = two("mp", [P, TPB, 3, H], BF16), two("mt", [3 * H, S], BF16)
        powers, mhalf, pick, sel = sb("powers", [P, TPB, 2]), sb("mhalf", [P, TPB]), sb("pick", [P, 2, 9]), sb("sel", [P, 2])
        pp = [t.ps(f"at_pp{k}", [P, 2 * S]) for k in range(2)]
        pm = [t.ps(f"at_pm{k}", [P, 2 * S]) for k in range(2)]
        po = t.ps("at_po", [P, QUADS * S])
        mi = [t.ps(f"at_mi{k}", [P, 2 * S]) for k in range(2)]
        qkd = [nc.dram_tensor(f"at_qkd{k}", (3 * P, 2 * S), BF16, kind="Internal").ap() for k in range(2)]

        xa_in, xr_in, row_out = ([sem(f"{n}{k}") for k in range(2)] for n in ("xa_in", "xr_in", "row_out"))
        q_in, m_in = ([sem(f"{n}{k}") for k in range(NQ)] for n in ("q_in", "m_in"))
        k_in, part_out = ([sem(f"{n}{k}") for k in range(2)] for n in ("k_in", "part_out"))
        (zeroed, picked, selected, mv1, bnd1, var1, rstd1, xn_done, xt_tr, xt_out, qk_mm, a_done, r_done, b_done, part_done,
         kb_done, v_mm, v_out, pre_done, maxed, negs, mp_done, mt_tr, mt_out, main_done, exped, masked, pv_done, ot_out,
         otr, rd, on_done, ont_tr, ont_out, proj_mm, x2_done, bnd2, mv2, var2, rstd2, xn2_done, x2t_tr, x2t_out, num_mm,
         num_out) = (sem(n) for n in (
             "zeroed picked selected mv1 bnd1 var1 rstd1 xn_done xt_tr xt_out qk_mm a_done r_done b_done part_done "
             "kb_done v_mm v_out pre_done maxed negs mp_done mt_tr mt_out main_done exped masked pv_done ot_out "
             "otr rd on_done ont_tr ont_out proj_mm x2_done bnd2 mv2 var2 rstd2 xn2_done x2t_tr x2t_out num_mm "
             "num_out").split())
        xnorm_done = sem("xnorm")
        passed = sem("passed")
        NZ = NQ * 3 + 2 + 3
        blk = ctx.enter_context(nc.Block())
        x_v = x_dram.rearrange("(b k p) d -> p b k d", k=TPB, p=P)
        row_v = io["rows"].rearrange("(b k p) w -> p b k w", k=TPB, p=P)

        def wait(eng, s, n, most=None):
            if isinstance(n, int):
                n = n if most is None else min(n, most)
                if n <= 0:
                    return
            eng.wait_ge(s, n)

        def dma_count(b, slots, each=1):
            return lambda k: b * (16 * each // slots) + (16 * each - (k % slots) * (16 * each // slots))

        def turns(turn):
            for b in range(-4, NQ):
                turn(b, b % NQ, lambda o, b=b: 0 <= b + o < B)
            yield
            for b in range(B - NQ, B + 2):
                turn(b, b % NQ, lambda o, b=b: 0 <= b + o < B)
            yield

        def run(eng, turn):
            emit = turns(turn)
            next(emit)
            with eng.Fori(1, B // NQ - 1) as i:
                for k in range(NQ):
                    turn(i * NQ + k, k, lambda o: True)
            next(emit)

        @blk.sync
        def _(sp):
            def turn(b, k, has):
                if has(4):
                    wait(sp, xn_done, (b + 3) * TPB)
                    sp.dma_start(xa[k % 2][:, :, 0:D], x_v[:, ds(b + 4, 1), :, :]).then_inc(xa_in[k % 2], 16)
                if has(0):
                    wait(sp, x2_done, b - 1)
                    sp.dma_start(xr[k % 2][:, :, :], x_v[:, ds(b, 1), :, :]).then_inc(xr_in[k % 2], 16)
                if has(3):
                    n, q, h = b + 3, (k + 3) % NQ, (k + 1) % 2
                    wait(sp, part_done, n + 1)
                    sp.sem_inc(passed, 1)
                    wait(sp, main_done, (n - NQ + 1) * NP)
                    sp.sem_inc(passed, 1)
                    wait(sp, kb_done, (n - 1) * 2)
                    sp.sem_inc(passed, 1)
                    wait(sp, q_in[(q + 2) % NQ], dma_count(n - 2, NQ, 6)(q + 2))
                    sp.dma_start(qkd[h].rearrange("(t p) n -> p t n", t=3), part[h][:, :, :]).then_inc(part_out[h], 16)
                    wait(sp, part_out[h], dma_count(n, 2)(h))
                    src = qkd[h].rearrange("(tq g) n -> tq g n", g=HP)
                    for row, lo, hi in ((0, 0, 48), (48, 0, 32), (80, 0, 16)):
                        sp.dma_start(kc[h][row:row + hi - lo, :, :], src[lo:hi, :, S:2 * S]).then_inc(k_in[h], 16)
                    for i, p in enumerate((0, 0, 0, 1, 1, 2)):
                        sp.dma_start(qs[q][16 * i:16 * i + 16, :, :], src[16 * p:16 * p + 16, :, 0:S]).then_inc(q_in[q], 16)
                if has(-1):
                    wait(sp, rstd2, b)
                    sp.dma_start(row_v[:, ds(b - 1, 1), :, :], x2[(k - 1) % 2][:, :, :]).then_inc(row_out[(k - 1) % 2], 16)

            run(sp, turn)
            for k in range(2):
                sp.wait_ge(row_out[k], 16 * (B // 2))

        @blk.gpsimd
        def _(pool):
            g = nc.gpsimd
            g.memset(mhalf[:, :], -0.5).then_inc(zeroed, 1)
            g.memset(powers[:, :, 0:1], -0.5).then_inc(zeroed, 1)
            g.memset(powers[:, :, 1:2], 0.5).then_inc(zeroed, 1)
            for k in range(2):
                g.memset(x2[k][:, :, D + 3:XW], 0.0).then_inc(zeroed, 1)
            for k in range(NQ):
                g.memset(vp[k][:, :, :, HD + 1:32], 0.0).then_inc(zeroed, 1)
                g.memset(vp[k][:, :, :, HD:HD + 1], 1.0).then_inc(zeroed, 1)
            g.memset(pick[:, :, 0:6], 1.0).then_inc(picked, 1)
            g.memset(pick[:, :, 6:9], 0.0).then_inc(picked, 1)
            pool.wait_ge(picked, 2)
            g.affine_select(out=pick[:, :, 0:6], in_=pick[:, :, 0:6], compare_op=ALU.is_ge, fill=0.0,
                            base=0, pattern=[[-8, 2], [-16, 6]], channel_multiplier=1).then_inc(picked, 1)
            g.affine_select(out=pick[:, :, 6:9], in_=pick[:, :, 6:9], compare_op=ALU.not_equal, fill=1.0,
                            base=-ROWS, pattern=[[-1, 2], [-2, 3]], channel_multiplier=1).then_inc(picked, 1)
            pool.wait_ge(picked, 4)
            g.affine_select(out=pick[:, :, 0:6], in_=pick[:, :, 0:6], compare_op=ALU.is_ge, fill=0.0,
                            base=HD - 1, pattern=[[8, 2], [16, 6]], channel_multiplier=-1).then_inc(picked, 1)

            def turn(b, k, has):
                for u in range(NP):
                    if has(0):
                        wait(pool, exped, b * NP + (u + 1))
                        pool.sem_inc(passed, 1)
                        n = 4 if u % 3 == 2 else 2
                        tile = pt[u % RING][:, :].rearrange("p (h q) -> p h q", h=n)[:, :, 0:P]
                        g.affine_select(out=tile, in_=tile, compare_op=ALU.is_ge, fill=0.0, base=0,
                                        pattern=[[0, n], [1, P]], channel_multiplier=-1).then_inc(masked, 1)
                    if u == 5 and has(3):
                        q = (k + 1) % 2
                        wait(pool, b_done, b + 4)
                        g.tensor_tensor(part[q][:, 2, :], rest[q][:, :], part[q][:, 1, :], ALU.subtract).then_inc(part_done, 1)
                    if u == 7 and has(1):
                        n, q = b + 1, (k + 1) % 2
                        wait(pool, maxed, (n + 1) * NP)
                        pool.sem_inc(passed, 1)
                        for j in range(TPB):
                            g.tensor_scalar(nm[q][:, j, :, :], mx[q][:, j, :].rearrange("p (g r) -> p r g", r=2), -1.0, None,
                                            ALU.mult).then_inc(negs, 1)
                        flat = nm[q][:, :, :, :].rearrange("p j r g -> p j (r g)")
                        wait(pool, negs, n * 5 + 2)
                        pool.sem_inc(passed, 1)
                        g.tensor_copy(mp[q][:, :, 0, :], flat).then_inc(negs, 1)
                        wait(pool, negs, n * 5 + 3)
                        g.tensor_tensor(nr[q][:, :, :], flat, mp[q][:, :, 0, :], ALU.subtract).then_inc(negs, 1)
                        wait(pool, negs, n * 5 + 4)
                        pool.sem_inc(passed, 1)
                        g.tensor_copy(mp[q][:, :, 1, :], nr[q][:, :, :]).then_inc(negs, 1)
                        wait(pool, negs, n * 5 + 5)
                        g.tensor_tensor(mp[q][:, :, 2, :], nr[q][:, :, :], mp[q][:, :, 1, :], ALU.subtract).then_inc(mp_done, 1)
                    if u == 8 and has(4):
                        wait(pool, var1, b + 5)
                        g.tensor_tensor(xa[k % 2][:, :, D + 1], vare[k % 2][:, :], mhalf[:, :], ALU.pow).then_inc(rstd1, 1)
                if has(-1):
                    q = (k - 1) % 2
                    wait(pool, var2, b)
                    g.tensor_tensor(x2[q][:, :, D + 1:D + 3], vare2[q][:, :, :], powers[:, :, :], ALU.pow).then_inc(rstd2, 1)
                    wait(pool, rstd2, b)
                    g.tensor_tensor(c.xnorm[:, ds((b - 1) * TPB, TPB)], x2[q][:, :, D + 1], x2[q][:, :, D + 2], ALU.mult).then_inc(xnorm_done, 1)

            run(pool, turn)

        @blk.scalar
        def _(act):
            a = nc.scalar
            act.wait_ge(zeroed, NZ)

            def turn(b, k, has):
                for u in range(NP):
                    if has(0):
                        wait(act, main_done, b * NP + (u + 1))
                        wait(act, pv_done, b * NP + (u + 1 - RING))
                        a.activation(pt[u % RING][:, :], pm[u % 2], ACT.Exp, scale=SCALE).then_inc(exped, 1)
                    if u == 0 and has(3):
                        wait(act, xt_tr, (b + 4) * TPB)
                        a.activation(xt[(k + 1) % 2][:, :], mi[0][:, 0:S], ACT.Copy).then_inc(xt_out, 1)
                    if u == 1 and has(-2):
                        wait(act, x2t_tr, (b - 1) * TPB)
                        a.activation(x2t[k % 2][:, :], mi[1][:, 0:S], ACT.Copy).then_inc(x2t_out, 1)
                    if u == 2 and has(3):
                        h = (k + 1) % 2
                        wait(act, qk_mm, b + 4)
                        wait(act, part_out[h], dma_count(b + 1, 2)(h))
                        a.activation(part[h][:, 0, :], mi[0], ACT.Copy).then_inc(a_done, 1)
                    if u == 3 and has(-2):
                        wait(act, num_mm, b - 1)
                        a.activation(c.num[:, ds((b - 2) * TPB, TPB), :], mi[1][:, 0:TPB * E].rearrange("p (j e) -> p j e", e=E),
                                     ACT.Copy).then_inc(num_out, 1)
                    if u == 4 and has(-1):
                        wait(act, pv_done, b * NP)
                        a.activation(ot[(k - 1) % 2][:, 2:4, :].rearrange("p g q -> p (g q)"), po[:, 2 * S:4 * S],
                                     ACT.Copy).then_inc(ot_out, 1)
                    if u == 4 and has(3):
                        h = (k + 1) % 2
                        wait(act, r_done, b + 4)
                        a.activation(part[h][:, 1, :], rest[h][:, :], ACT.Copy).then_inc(b_done, 1)
                    if u == 6 and has(3):
                        wait(act, v_mm, b + 4)
                        wait(act, pv_done, b * NP)
                        a.activation(vp[(k + 3) % NQ][:, :, :, 0:HD].rearrange("p j h d -> p (j h) d"),
                                     mi[0][:, 0:TPB * D].rearrange("p (h d) -> p h d", d=HD), ACT.Copy).then_inc(v_out, 1)
                    if u == 8 and has(-1):
                        wait(act, ont_tr, b)
                        a.activation(ont[(k - 1) % 2][:, :], mi[1][:, 0:S], ACT.Copy).then_inc(ont_out, 1)
                    if u == 9 and has(1):
                        q = (k + 1) % NQ
                        wait(act, mt_tr, b + 2)
                        wait(act, m_in[(q - 2) % NQ], dma_count(b - 1, NQ)(q - 2))
                        a.activation(mt[q % 2][:, :], mi[0].bitcast(BF16)[0:3 * H, 0:S], ACT.Copy).then_inc(mt_out, 1)
                        wait(act, mt_out, b + 2)
                        act.dma_start(qs[q][ROWS:ROWS + 6, :, :], mt[q % 2][:, :].unsqueeze(1)).then_inc(m_in[q], 16)
                    if u == 10 and has(0):
                        wait(act, pv_done, b * NP + 6)
                        wait(act, otr, (b - 1) * TPB)
                        a.activation(ot[k % 2][:, 0:2, :].rearrange("p g q -> p (g q)"), po[:, 0:2 * S], ACT.Copy).then_inc(ot_out, 1)

            run(act, turn)

        @blk.tensor
        def _(pe):
            te = nc.tensor
            pe.wait_ge(zeroed, NZ)

            def turn(b, k, has):
                def scores_by_query(v):
                    n, s, out = b + 1, (k + 1) % NQ, pp[v % 2]
                    if v == 0:
                        wait(pe, q_in[s], dma_count(n, NQ, 6)(s))
                        wait(pe, kb_done, (n + 1) * 2)
                    wait(pe, maxed, n * NP + (v - 1))
                    if v < 4:
                        for w in range(2):
                            te.matmul(out[:, w * S:(w + 1) * S], qs[s][0:ROWS, 2 * v + w, 0:P], kb[s][0:ROWS, 2 * v + w, :, 0:P],
                                      start=(w == 0), stop=False, skip_group_check=True)
                        te.matmul(out, c.identb[:, :], c.mask[:, :, :].rearrange("p a q -> p (a q)"),
                                  start=False, stop=True, skip_group_check=True).then_inc(pre_done, 1)
                    else:
                        te.matmul(out, qs[s][0:ROWS, v - 4, P:S], kb[s][0:ROWS, v - 4, :, :].rearrange("p r q -> p (r q)"),
                                  start=True, stop=False, skip_group_check=True)
                        te.matmul(out.rearrange("p (r q) -> p r q", r=2)[:, :, P:S], c.identb[:, :], c.mask[:, 0:2, :],
                                  start=False, stop=True, skip_group_check=True).then_inc(pre_done, 1)

                def scores_by_key(u):
                    s, out, quad, w = k, pm[u % 2], u // 3, u % 3
                    if u == 0:
                        wait(pe, m_in[s], dma_count(b, NQ)(s))
                    wait(pe, exped, b * NP + (u - 1))
                    if w < 2:
                        for r in range(2):
                            last = te.matmul(out[:, r * S:(r + 1) * S], kb[s][:, 2 * quad + w, r, 0:P], qs[s][:, 2 * quad + w, :],
                                             start=True, stop=True)
                    else:
                        for j in range(4):
                            last = te.matmul(out[:, j * P:(j + 1) * P], kb[s][:, 2 * quad + j // 2, j % 2, P:S],
                                             qs[s][:, 2 * quad + j // 2, P:S], start=True, stop=True)
                    last.then_inc(main_done, 1)

                def times_v(n, s, u):
                    quad, w, src = u // 3, u % 3, pt[u % RING]
                    if u == 0:
                        wait(pe, v_out, n + 1)
                        wait(pe, ot_out, n * 2 - 1)
                    if u == 6:
                        wait(pe, ot_out, n * 2)
                    wait(pe, masked, n * NP + (u + 1))
                    for i in range(2 if w < 2 else 4):
                        j = 2 * w + i if w < 2 else i
                        cols = S if w < 2 else P
                        last = te.matmul(po[32 * j:32 * j + 32, (quad + 1) * S - cols:(quad + 1) * S],
                                         vp[s][:, w // 2, 4 * quad + j, :], src[:, i * cols:(i + 1) * cols],
                                         start=(w < 2), stop=(w == 2), skip_group_check=True)
                    last.then_inc(pv_done, 1)

                def small(u):
                    if u == 0 and has(3):
                        wait(pe, xn_done, (b + 4) * TPB)
                        wait(pe, mt_out, b + 1)
                        if isinstance(b, int):
                            wait(pe, v_out, b + 3)
                        for j in range(TPB):
                            te.transpose(mi[0][:, j * P:(j + 1) * P], xn[(k + 1) % 2][:, j, :], c.ident[:, :]).then_inc(xt_tr, 1)
                    if u == 1 and has(-2):
                        wait(pe, xn2_done, (b - 1) * TPB)
                        for j in range(TPB):
                            te.transpose(mi[1][:, j * P:(j + 1) * P], xn2[k % 2][:, j, :], c.ident[:, :]).then_inc(x2t_tr, 1)
                    if u == 2 and has(3):
                        wait(pe, xt_out, b + 4)
                        te.matmul(mi[0][:, 0:S], c.wq[:, :], xt[(k + 1) % 2][:, :], start=True, stop=True)
                        te.matmul(mi[0][:, S:2 * S], c.wk[:, :], xt[(k + 1) % 2][:, :], start=True, stop=True).then_inc(qk_mm, 1)
                    if u == 3 and has(-2):
                        wait(pe, x2t_out, b - 1)
                        for j in range(TPB):
                            last = te.matmul(mi[1][:, j * E:(j + 1) * E], x2t[k % 2][:, j * P:(j + 1) * P], c.waff_t[:, :],
                                             start=True, stop=True)
                        last.then_inc(num_mm, 1)
                    if u == 5 and has(3):
                        wait(pe, r_done, b + 4)
                        for j in range(TPB):
                            last = te.matmul(mi[0][:, j * D:(j + 1) * D], xt[(k + 1) % 2][:, j * P:(j + 1) * P], c.wv[:, :],
                                             start=True, stop=True)
                        last.then_inc(v_mm, 1)
                    if u in (6, 7) and has(-1):
                        j = u - 6
                        wait(pe, ot_out, b * 2)
                        wait(pe, num_out, b - 1) if j == 0 else wait(pe, v_out, b + 4, B)
                        for quad in range(QUADS):
                            last = te.transpose(mi[1 - j][:, quad * P:(quad + 1) * P], ot[(k - 1) % 2][:, quad, j * P:(j + 1) * P],
                                                c.ident[:, :])
                        last.then_inc(otr, 1)
                    if u == 8 and has(-1):
                        wait(pe, on_done, b * TPB)
                        for j in range(TPB):
                            last = te.transpose(mi[1][:, j * P:(j + 1) * P], on[(k - 1) % 2][:, j, :], c.ident[:, :])
                        last.then_inc(ont_tr, 1)
                    if u == 9 and has(1):
                        wait(pe, mp_done, b + 2)
                        wait(pe, on_done, b * TPB)
                        wait(pe, v_out, b + 4, B)
                        pe.sem_inc(passed, 1)
                        for j in range(TPB):
                            last = te.transpose(mi[0].bitcast(BF16)[0:3 * H, j * P:(j + 1) * P],
                                                mp[(k + 1) % 2][:, j, :, :].rearrange("p t h -> p (t h)"), c.identb[:, :])
                        last.then_inc(mt_tr, 1)
                    if u == 10 and has(-1):
                        wait(pe, ont_out, b)
                        for j in range(TPB):
                            last = te.matmul(mi[1][:, j * D:(j + 1) * D], ont[(k - 1) % 2][:, j * P:(j + 1) * P], c.wproj[:, :],
                                             start=True, stop=True)
                        last.then_inc(proj_mm, 1)

                for u in range(NP):
                    if has(1):
                        for v in QUERY_TILES[u]:
                            scores_by_query(v)
                    if has(0):
                        scores_by_key(u)
                    if u >= LAG and has(0):
                        times_v(b, k, u - LAG)
                    if u < LAG and has(-1):
                        times_v(b - 1, (k - 1) % NQ, NP - LAG + u)
                    small(u)

            run(pe, turn)

        @blk.vector
        def _(dve):
            v = nc.vector
            for k in range(NQ):
                v.memset(qs[k][ROWS:P, :, :], 0.0).then_inc(zeroed, 1)
            dve.wait_ge(zeroed, NZ)
            dve.wait_ge(picked, 5)
            v.tensor_reduce(sel[:, :], pick[:, :, :], axis=AX.X, op=ALU.add).then_inc(selected, 1)
            for k in range(2):
                v.memset(kc[k][ROWS:P, :, :], 1.0).then_inc(selected, 1)
            dve.wait_ge(selected, 3)

            def statistics(n, x, bns, var, bnd, mv, done, keep):
                for j in range(TPB):
                    v.bn_stats(bns[:, j, :], x[:, j, 0:D]).then_inc(bnd, 1)
                for j in range(TPB):
                    wait(dve, bnd, n * TPB + (j + 1))
                    dve.sem_inc(passed, 1)
                    v.bn_aggr(x[:, j, D:D + 2], bns[:, j, :]).then_inc(mv, 1)
                wait(dve, mv, n * TPB + TPB)
                if keep:
                    v.tensor_copy(var[:, :, 1], x[:, :, D + 1])
                v.tensor_scalar(var[:, :, 0] if keep else var[:, :], x[:, :, D + 1], LN_EPS, None, ALU.add).then_inc(done, 1)

            def normalise(out, x, done):
                for j in range(TPB):
                    v.tensor_scalar(out[:, j, :], x[:, j, 0:D], x[:, j, D:D + 1], x[:, j, D + 1:D + 2],
                                    ALU.subtract, ALU.mult).then_inc(done, 1)

            def turn(b, k, has):
                for u in range(NP):
                    if has(1):
                        n, q = b + 1, (k + 1) % 2
                        for w in QUERY_TILES[u]:
                            wait(dve, pre_done, n * NP + (w + 1))
                            if w == 0:
                                wait(dve, mp_done, n - 1)
                            out = mx[q][:, 0, 4 * w:4 * w + 4] if w < 4 else mx[q][:, 1, 2 * w - 8:2 * w - 6]
                            v.tensor_reduce(out, pp[w % 2].rearrange("p (h q) -> p h q", h=4 if w < 4 else 2),
                                            axis=AX.X, op=ALU.max).then_inc(maxed, 1)
                    if u == 0 and has(-2):
                        wait(dve, rstd2, b - 1)
                        wait(dve, x2t_tr, (b - 3) * TPB)
                        normalise(xn2[k % 2], x2[k % 2], xn2_done)
                    if u in (2, 8) and has(2):
                        r = u // 8
                        if r == 0:
                            wait(dve, k_in[k % 2], dma_count(b + 2, 2, 3)(k))
                        v.tensor_scalar(kb[(k + 2) % NQ][:, :, r, :], kc[k % 2][:, :, :], sel[:, r:r + 1], None,
                                        ALU.mult).then_inc(kb_done, 1)
                    if u == 3 and has(3):
                        h = (k + 1) % 2
                        wait(dve, a_done, b + 4)
                        wait(dve, part_done, b + 2)
                        v.tensor_tensor(rest[h][:, :], mi[0], part[h][:, 0, :], ALU.subtract).then_inc(r_done, 1)
                    if u in (6, 7) and has(-1):
                        q, j = (k - 1) % 2, u - 6
                        wait(dve, otr, (b - 1) * TPB + (j + 1))
                        rows = mi[1 - j].rearrange("p (h w) -> p h w", w=32)
                        v.reciprocal(rden[j][:, :], rows[:, :, HD]).then_inc(rd, 1)
                        wait(dve, rd, (b - 1) * TPB + (j + 1))
                        v.tensor_tensor(on[q][:, j, :].rearrange("p (h d) -> p h d", d=HD), rows[:, :, 0:HD],
                                        rden[j][:, :].unsqueeze(2).to_broadcast([P, H, HD]), ALU.mult).then_inc(on_done, 1)
                    if u == 7 and has(4):
                        wait(dve, xa_in[k % 2], dma_count(b + 4, 2)(k))
                        statistics(b + 4, xa[k % 2], bn[k % 2], vare[k % 2], bnd1, mv1, var1, False)
                    if u == 9 and has(4):
                        wait(dve, rstd1, b + 5)
                        wait(dve, xt_tr, (b + 3) * TPB)
                        normalise(xn[k % 2], xa[k % 2], xn_done)
                    if u == 10 and has(-1):
                        q = (k - 1) % 2
                        wait(dve, proj_mm, b)
                        wait(dve, xr_in[q], dma_count(b - 1, 2)(q))
                        wait(dve, row_out[q], dma_count(b - 3, 2)(q))
                        wait(dve, xnorm_done, b - 2)
                        v.tensor_tensor(x2[q][:, :, 0:D], mi[1][:, 0:TPB * D].rearrange("p (j d) -> p j d", d=D), xr[q][:, :, :],
                                        ALU.add).then_inc(x2_done, 1)
                        wait(dve, x2_done, b)
                        statistics(b - 1, x2[q], bn2[q], vare2[q], bnd2, mv2, var2, True)

            run(dve, turn)


def macaron(nc, io, out):
    ctx = ExitStack()
    with ctx:
        m = Mem(nc, ctx)
        c = consts(nc, m)
        io["rows"] = nc.dram_tensor("rows", (T, XW), F32, kind="Internal").ap()
        x1 = nc.dram_tensor("x1", (T, D), F32, kind="Internal").ap()
        preamble(nc, m, io, c)
        token_stats(nc, m, io, c, io["x"])
        route(nc, m, c, "r1")
        experts(nc, m, io, c, "e1", x1)
        attention(nc, m, io, c, x1)
        route(nc, m, c, "r2")
        experts(nc, m, io, c, "e2", out)


_INS = {
    "x": ("L0_attn_batch", (T, D)),
    "wqkv": ("L0_attn_W_qkv", (D, 3 * D)),
    "uqkv": ("L0_attn_u_qkv", (3 * D,)),
    "sqkv": ("L0_attn_sigma_qkv", (1,)),
    "wproj": ("L0_attn_W_proj", (D, D)),
    "uproj": ("L0_attn_u_proj", (D,)),
    "sproj": ("L0_attn_sigma_proj", (1,)),
    "waff": ("L0_ffn_waff", (E, D)),
    "w1": ("L0_ffn_W1", (E, D, F)),
    "b1": ("L0_ffn_b1", (E, F)),
    "w2": ("L0_ffn_W2", (E, F, D)),
    "b2": ("L0_ffn_b2", (E, D)),
    "thr": ("L0_ffn_affinity_threshold", (1,)),
}


def kernel(**inputs):
    import concourse.bacc as _bacc
    from concourse.bass_utils import run_bass_kernel_spmd as _run

    nc = _bacc.Bacc("TRN2", target_bir_lowering=False, num_devices=1)
    arrays, io = {}, {}
    for short, (name, shape) in _INS.items():
        a = np.ascontiguousarray(inputs[name]).reshape(shape)
        arrays[f"in_{short}_dram"] = a
        io[short] = nc.dram_tensor(f"in_{short}_dram", shape, mybir.dt.from_np(a.dtype), kind="ExternalInput").ap()
    out = nc.dram_tensor("out_0_dram", (T, D), F32, kind="ExternalOutput").ap()
    macaron(nc, io, out)
    r = _run(nc, [arrays], core_ids=[0])
    return r.results[0]["out_0_dram"].reshape(B, S, D)
```

```python
import numpy as np
import concourse.bass as bass
from concourse import mybir
from contextlib import ExitStack

F32 = mybir.dt.float32
BF16 = mybir.dt.bfloat16
I32 = mybir.dt.int32
ALU = mybir.AluOpType
ACT = mybir.ActivationFunctionType
AX = mybir.AxisListType

P = 128
D = 128
E, F = 8, 512
FC = F // P
B, S = 32, 256
TPB = S // P
T = B * S
NT = T // P
G = E + 1
NS = NT + G - 1
U = 8
BANK = 512
NSX = NS + U
XW = D + 4
H, HD = 16, 8
MAGIC = 1.5 * 2 ** 23
LN_EPS = 1e-5
TIE = -1e-37


def ds(start, n):
    return bass.ds(start, n)


class Mem:

    def __init__(self, nc, ctx):
        self.nc, self.ctx, self.sems = nc, ctx, []
        ctx.callback(self.clear)

    def clear(self):
        if self.sems:
            for n in range(min(self.sems), max(self.sems) + 1):
                if n in self.sems and n - 1 not in self.sems:
                    end = n
                    while end in self.sems:
                        end += 1
                    self.nc.gpsimd.sem_clear(range(n, end))
            self.nc.all_engine_barrier()

    def sb(self, name, shape, dt=F32):
        return self.ctx.enter_context(self.nc.sbuf_tensor(name, shape, dt))

    def ps(self, name, shape, dt=F32):
        size = int(np.prod(shape[1:]))
        whole = self.ctx.enter_context(self.nc.psum_tensor(name, [P, -(-size // BANK) * BANK], dt))
        out = whole[:, 0:size]
        return out if len(shape) == 2 else out.rearrange("p (a b) -> p a b", a=shape[1])

    def sem(self, name):
        sem = self.ctx.enter_context(self.nc.semaphore(name))
        self.sems.append(sem.num)
        return sem


class Steps:

    def __init__(self, engine, sem):
        self.engine, self.sem, self.n = engine, sem, 0

    def step(self, ins):
        self.n += 1
        ins.then_inc(self.sem, 1)
        self.engine.wait_ge(self.sem, self.n)


def preamble(nc, m, io, c):
    ctx = ExitStack()
    with ctx:
        t = Mem(nc, ctx)
        waff_n = t.sb("waff_n", [E, D])
        b1_chunks = t.sb("b1_chunks", [E * FC, P])
        b1_rows = t.sb("b1_rows", [E, F])
        b1_rest = t.sb("b1_rest", [E, F])
        b1_parts = t.sb("b1_parts", [E, 3, F], BF16)
        gelu_b1 = t.sb("gelu_b1", [P, E * (E * FC + 1)])
        own_rows = t.sb("own_rows", [G, D])
        b2_rows = t.sb("b2_rows", [E, D])
        const_rows = t.sb("const_rows", [G, D])
        rest_rows = t.sb("rest_rows", [G, D])
        const_parts = t.sb("const_parts", [G, 3, D], BF16)
        w_raw, u_row = t.sb("w_raw", [P, 4 * D]), t.sb("u_row", [P, 4 * D])
        sig = t.sb("sig", [P, 2])
        prod = t.sb("prod", [P, 4 * D])
        u2 = t.sb("u2", [P, 4 * D])
        v_bc = [t.sb(f"v_bc{w}", [P, P]) for w in range(2)]
        col = t.sb("col", [P, 16])
        sq = t.sb("sq", [P, E])
        half = t.sb("half", [P, E])
        mhalf = t.sb("mhalf", [P, 2])
        iota_i = t.sb("iota_i", [P, P], I32)
        part_i = t.sb("part_i", [P, 1], I32)
        tile_i = t.sb("tile_i", [P, NT], I32)
        down_i = t.sb("down_i", [P, E], I32)
        pm = [t.ps(f"pre{i}", [P, 512]) for i in range(8)]

        w_in, w_ffn, parts_out = t.sem("w_in"), t.sem("w_ffn"), t.sem("parts_out")
        made, ints = t.sem("made"), t.sem("ints")
        early, filled, small_t = t.sem("early"), t.sem("filled"), t.sem("small_t")
        b1_t, b1_g, k_done = t.sem("b1_t"), t.sem("b1_g"), t.sem("k_done")
        b1_split, const_split = t.sem("b1_split"), t.sem("const_split")
        pows, powask = t.sem("pows"), t.sem("powask")
        ask, told, vstep = t.sem("ask"), t.sem("told"), t.sem("vstep")
        blk = ctx.enter_context(nc.Block())
        N_SMALL = 11
        parts = (slice(0, 3 * D), slice(3 * D, 4 * D))

        @blk.sync
        def _(sp):
            for dst, src in [
                (waff_n[:, :], io["waff"]),
                (b1_chunks[:, :], io["b1"].rearrange("e (c p) -> (e c) p", p=P)),
                (b1_rows[:, :], io["b1"]),
                (b2_rows[:, :], io["b2"]),
                (w_raw[:, parts[0]], io["wqkv"]),
                (w_raw[:, parts[1]], io["wproj"]),
                (u_row[:, parts[0]], io["uqkv"].partition_broadcast(P)),
                (u_row[:, parts[1]], io["uproj"].partition_broadcast(P)),
                (sig[:, 0:1], io["sqkv"].partition_broadcast(P)),
                (sig[:, 1:2], io["sproj"].partition_broadcast(P)),
                (c.thr[:, :], io["thr"].partition_broadcast(P)),
            ]:
                sp.dma_start(dst, src).then_inc(w_in, 16)
            sp.dma_start(c.w2[:, 0:E, :, :], io["w2"].rearrange("e (c p) d -> p e c d", p=P)).then_inc(w_ffn, 16)
            sp.dma_start(c.w1[:, 0:E, :], io["w1"].rearrange("e d f -> d e f")).then_inc(w_ffn, 16)
            sp.wait_ge(filled, 3)
            sp.wait_ge(b1_split, 3)
            for f in range(FC):
                for r in range(3):
                    sp.dma_start(c.b1s[3 * f + r:3 * f + r + 1, 0:E, :],
                                 b1_parts[:, r, f * P:(f + 1) * P].unsqueeze(1)).then_inc(parts_out, 16)
            sp.wait_ge(const_split, 3)
            for r in range(3):
                sp.dma_start(c.cst[r:r + 1, :, :], const_parts[:, r, :].unsqueeze(1)).then_inc(parts_out, 16)
            sp.wait_ge(parts_out, 16 * 3 * (FC + 1))
            sp.wait_ge(w_ffn, 32)

        @blk.gpsimd
        def _(pool):
            g = nc.gpsimd
            for n, eye in enumerate((c.ident, c.identb)):
                g.memset(eye[:, :], 0.0).then_inc(made, 1)
                pool.wait_ge(made, n + 1)
                g.affine_select(out=eye[:, :], in_=eye[:, :], compare_op=ALU.not_equal, fill=1.0,
                                base=0, pattern=[[-1, P]], channel_multiplier=1).then_inc(early, 1)
            g.memset(c.ones[:, :], 1.0).then_inc(early, 1)
            g.memset(half[:, :], 0.5).then_inc(early, 1)
            g.memset(mhalf[:, :], -0.5).then_inc(early, 1)
            g.iota(iota_i[:, :], pattern=[[1, P]], base=0, channel_multiplier=0).then_inc(ints, 1)
            g.iota(part_i[:, :], pattern=[[0, 1]], base=0, channel_multiplier=1).then_inc(ints, 1)
            g.iota(tile_i[:, :], pattern=[[1, NT]], base=1, channel_multiplier=0).then_inc(ints, 1)
            g.iota(down_i[:, :], pattern=[[-1, E]], base=E, channel_multiplier=0).then_inc(ints, 1)
            g.memset(c.onesb[:, :], 1.0).then_inc(made, 1)
            g.memset(c.tri[:, :], 1.0).then_inc(made, 1)
            g.memset(c.tie[:, :, :], 0.0).then_inc(made, 1)
            g.memset(c.mask[:, :, :], 0.0).then_inc(made, 1)
            g.memset(c.w1[:, E, :], 0.0).then_inc(made, 1)
            g.memset(c.w2[:, E, :, :], 0.0).then_inc(made, 1)
            g.memset(c.chunk[:, :, :], 1.0).then_inc(made, 1)
            pool.wait_ge(made, 9)
            g.affine_select(out=c.chunk[:, :, :], in_=c.chunk[:, :, :], compare_op=ALU.is_ge, fill=0.0,
                            base=0, pattern=[[-3, FC], [0, P]], channel_multiplier=1).then_inc(made, 1)
            pool.wait_ge(made, 10)
            g.affine_select(out=c.chunk[:, :, :], in_=c.chunk[:, :, :], compare_op=ALU.is_ge, fill=0.0,
                            base=2, pattern=[[3, FC], [0, P]], channel_multiplier=-1).then_inc(made, 1)
            g.affine_select(out=c.tri[:, :], in_=c.tri[:, :], compare_op=ALU.is_gt, fill=0.0,
                            base=0, pattern=[[1, P]], channel_multiplier=-1).then_inc(made, 1)
            g.affine_select(out=c.tie[:, :, :], in_=c.tie[:, :, :], compare_op=ALU.is_ge, fill=TIE,
                            base=0, pattern=[[-P, TPB], [1, S]], channel_multiplier=-1).then_inc(made, 1)
            g.affine_select(out=c.mask[:, :, :], in_=c.mask[:, :, :], compare_op=ALU.is_ge, fill=-3e38,
                            base=0, pattern=[[0, 4], [-1, P]], channel_multiplier=1).then_inc(made, 1)
            pool.wait_ge(early, 5)
            pool.wait_ge(powask, 1)
            g.tensor_tensor(c.wnorm[:, :], sq[:, :], half[:, :], ALU.pow).then_inc(pows, 1)
            for n in range(2):
                pool.wait_ge(powask, n + 2)
                g.tensor_tensor(col[:, 8 + 2 * n:10 + 2 * n], col[:, 4:6], mhalf[:, :], ALU.pow).then_inc(pows, 1)

        @blk.scalar
        def _(act):
            act.wait_ge(b1_t, 1)
            act.wait_ge(filled, 3)
            nc.scalar.activation(gelu_b1[:, :].rearrange("p (e w) -> p e w", e=E)[:, :, 0:E * FC:E],
                                 pm[0][:, 0:E * FC].rearrange("p (e f) -> p e f", e=E), ACT.Gelu).then_inc(b1_g, 1)

        @blk.tensor
        def _(pe):
            pe.wait_ge(w_in, 16 * N_SMALL)
            pe.wait_ge(early, 5)
            nc.tensor.transpose(pm[0][:, 0:E * FC], b1_chunks[:, :], c.ident[0:E * FC, 0:E * FC]).then_inc(b1_t, 1)
            nc.tensor.transpose(pm[1][:, 0:E], waff_n[:, :], c.ident[0:E, 0:E]).then_inc(small_t, 1)
            pe.wait_ge(ask, 1)
            nc.tensor.matmul(pm[1][:, 16:16 + E], c.ones[:, :], sq[:, :], start=True, stop=True).then_inc(told, 1)
            pe.wait_ge(ask, 2)
            nc.tensor.matmul(pm[4][:, 0:2], c.ones[:, :], col[:, 2:4], start=True, stop=True).then_inc(told, 1)
            pe.wait_ge(ask, 3)
            for w in range(2):
                last = nc.tensor.matmul(pm[5][:, parts[w]], v_bc[w][:, :], w_raw[:, parts[w]], start=True, stop=True)
            last.then_inc(told, 1)
            pe.wait_ge(ask, 4)
            nc.tensor.matmul(pm[4][:, 0:2], c.ones[:, :], col[:, 2:4], start=True, stop=True).then_inc(told, 1)
            pe.wait_ge(b1_g, 1)
            pe.wait_ge(w_ffn, 32)
            for n in range(E * FC):
                last = nc.tensor.matmul(pm[2][0:E, 0:D], gelu_b1[:, n * E:(n + 1) * E], c.w2[:, n // FC, n % FC, :],
                                        start=(n == 0), stop=(n == E * FC - 1))
            last.then_inc(k_done, 1)
            pe.wait_ge(ask, 5)
            nc.tensor.matmul(pm[3][0:G, 0:D], c.ones[0:E, 0:G], b2_rows[:, :], start=True, stop=True).then_inc(told, 1)

        @blk.vector
        def _(dve):
            v = nc.vector
            s = Steps(dve, vstep)
            v.memset(gelu_b1[:, :], 0.0).then_inc(filled, 1)
            v.memset(c.b1s[:, :, :], 0.0).then_inc(filled, 1)
            v.memset(c.cst[:, :, :], 0.0).then_inc(filled, 1)
            dve.wait_ge(ints, 4)
            for dst, src in ((c.iota[:, :], iota_i[:, :]), (c.part[:, :], part_i[:, :]),
                             (c.tile1[:, :], tile_i[:, :]), (c.down[:, :], down_i[:, :])):
                s.step(v.tensor_copy(dst, src))
            dve.wait_ge(w_in, 16 * N_SMALL)
            for r in range(3):
                s.step(v.tensor_copy(b1_parts[:, r, :], b1_rows[:, :] if r == 0 else b1_rest[:, :]))
                b1_split_now = v.tensor_tensor(b1_rest[:, :], b1_rows[:, :] if r == 0 else b1_rest[:, :],
                                               b1_parts[:, r, :], ALU.subtract)
                b1_split_now.then_inc(b1_split, 1)
                dve.wait_ge(b1_split, r + 1)
            dve.wait_ge(small_t, 1)
            s.step(v.tensor_copy(c.waff_t[:, :], pm[1][:, 0:E]))
            v.tensor_tensor(sq[:, :], c.waff_t[:, :], c.waff_t[:, :], ALU.mult).then_inc(ask, 1)
            dve.wait_ge(told, 1)
            v.tensor_copy(sq[:, :], pm[1][:, 16:16 + E]).then_inc(powask, 1)
            dve.wait_ge(pows, 1)
            dve.wait_ge(early, 5)
            s.step(v.tensor_tensor(prod[:, :], w_raw[:, :], u_row[:, :], ALU.mult))
            for w in range(2):
                s.step(v.tensor_reduce(col[:, w:w + 1], prod[:, parts[w]], axis=AX.X, op=ALU.add))
            v.tensor_tensor(col[:, 2:4], col[:, 0:2], col[:, 0:2], ALU.mult).then_inc(ask, 1)
            dve.wait_ge(told, 2)
            v.tensor_copy(col[:, 4:6], pm[4][:, 0:2]).then_inc(powask, 1)
            dve.wait_ge(pows, 2)
            s.step(v.tensor_tensor(col[:, 0:2], col[:, 0:2], col[:, 8:10], ALU.mult))
            s.step(v.tensor_scalar(v_bc[0][:, :], c.ones[:, :], col[:, 0:1], None, ALU.mult))
            v.tensor_scalar(v_bc[1][:, :], c.ones[:, :], col[:, 1:2], None, ALU.mult).then_inc(ask, 1)
            dve.wait_ge(told, 3)
            s.step(v.tensor_copy(u2[:, :], pm[5][:, :]))
            s.step(v.tensor_tensor(prod[:, :], u2[:, :], u2[:, :], ALU.mult))
            s.step(v.tensor_reduce(col[:, 4:5], prod[:, parts[0]], axis=AX.X, op=ALU.add))
            v.tensor_reduce(col[:, 5:6], prod[:, parts[1]], axis=AX.X, op=ALU.add).then_inc(powask, 1)
            dve.wait_ge(powask, 3)
            s.step(v.tensor_tensor(prod[:, :], w_raw[:, :], u2[:, :], ALU.mult))
            for w in range(2):
                s.step(v.tensor_reduce(col[:, 6 + w:7 + w], prod[:, parts[w]], axis=AX.X, op=ALU.add))
            v.tensor_tensor(col[:, 2:4], col[:, 6:8], col[:, 0:2], ALU.mult).then_inc(ask, 1)
            dve.wait_ge(told, 4)
            dve.wait_ge(pows, 3)
            s.step(v.tensor_tensor(col[:, 12:14], pm[4][:, 0:2], col[:, 10:12], ALU.mult))
            s.step(v.reciprocal(col[:, 12:14], col[:, 12:14]))
            s.step(v.tensor_tensor(col[:, 14:16], col[:, 12:14], sig[:, :], ALU.mult))
            for i, out in enumerate((c.wq, c.wk)):
                s.step(v.tensor_scalar(out[:, :].rearrange("p (r d g) -> p r d g", r=2, d=HD),
                                       w_raw[:, i * D:(i + 1) * D].rearrange("p (g r d) -> p r d g", r=2, d=HD),
                                       col[:, 14:15], None, ALU.mult))
            s.step(v.tensor_scalar(c.wv[:, :], w_raw[:, 2 * D:3 * D], col[:, 14:15], None, ALU.mult))
            s.step(v.tensor_scalar(c.wproj[:, :], w_raw[:, parts[1]], col[:, 15:16], None, ALU.mult))
            dve.wait_ge(k_done, 1)
            s.step(v.memset(own_rows[:, :], 0.0))
            s.step(v.tensor_copy(own_rows[0:E, :], pm[2][0:E, 0:D]))
            v.tensor_tensor(b2_rows[:, :], b2_rows[:, :], own_rows[0:E, :], ALU.add).then_inc(ask, 1)
            dve.wait_ge(told, 5)
            s.step(v.tensor_tensor(const_rows[:, :], pm[3][0:G, 0:D], own_rows[:, :], ALU.subtract))
            for r in range(3):
                rows = const_rows if r == 0 else rest_rows
                s.step(v.tensor_copy(const_parts[:, r, :], rows[:, :]))
                v.tensor_tensor(rest_rows[:, :], rows[:, :], const_parts[:, r, :], ALU.subtract).then_inc(const_split, 1)
                dve.wait_ge(const_split, r + 1)


def token_stats(nc, m, io, c, x_dram):
    ctx = ExitStack()
    with ctx:
        t = Mem(nc, ctx)
        TS = 4
        NB = NT // TS
        NX = 4
        x_row = [t.sb(f"ts_x{k}", [P, TS, XW]) for k in range(NX)]
        bn = t.sb("ts_bn", [P, 2, TS, 6])
        vare = t.sb("ts_vare", [P, 2, TS, 2])
        powers = t.sb("ts_powers", [P, TS, 2])
        xn = [t.sb(f"ts_xn{k}", [P, TS, D]) for k in range(2)]
        xn_t = [t.sb(f"ts_xnt{k}", [P, TS * P]) for k in range(2)]
        p_t = [t.ps(f"ts_pt{k}", [P, TS * P]) for k in range(2)]
        p_n = [t.ps(f"ts_pn{k}", [P, TS, E]) for k in range(2)]
        x_in = [t.sem(f"ts_in{k}") for k in range(NX)]
        x_out = [t.sem(f"ts_out{k}") for k in range(NX)]
        pad, bn_done, mv_done, var_done, rstd, xnorm_done, xn_done, tr, tr_out, num, num_out = (
            t.sem(f"ts_{n}") for n in "pad bn mv var rstd xnorm xn tr tro num numo".split())
        passed = t.sem("ts_passed")
        blk = ctx.enter_context(nc.Block())
        x_v = x_dram.rearrange("(b k p) d -> p b k d", k=TS, p=P)
        row_v = io["rows"].rearrange("(b k p) w -> p b k w", k=TS, p=P)

        def wait(eng, s, n):
            if not isinstance(n, int) or n > 0:
                eng.wait_ge(s, n)

        def run(eng, step):
            for k in range(NX):
                step(k, k, k == 0, False)
            with eng.Fori(1, NB // NX - 1) as i:
                for k in range(NX):
                    step(i * NX + k, k, False, False)
            for k in range(NX):
                step(NB - NX + k, k, False, k == NX - 1)

        @blk.sync
        def _(sp):
            def load(b, k, first, last):
                if not isinstance(b, int) or b >= NX:
                    sp.wait_ge(x_out[k], (b - k) * (16 // NX))
                    sp.sem_inc(passed, 1)
                    sp.wait_ge(xn_done, (b - (NX - 1)) * TS)
                    sp.sem_inc(passed, 1)
                    sp.wait_ge(xnorm_done, b - (NX - 1))
                    sp.sem_inc(passed, 1)
                sp.dma_start(x_row[k][:, :, 0:D], x_v[:, ds(b, 1), :, :]).then_inc(x_in[k], 16)

            run(sp, load)

        @blk.gpsimd
        def _(pool):
            g = nc.gpsimd
            g.memset(powers[:, :, 0:1], -0.5).then_inc(pad, 1)
            g.memset(powers[:, :, 1:2], 0.5).then_inc(pad, 1)
            for k in range(NX):
                g.memset(x_row[k][:, :, D + 3:XW], 0.0).then_inc(pad, 1)
            pool.wait_ge(pad, NX + 2)

            def roots(b, k, first, last):
                pool.wait_ge(var_done, b + 1)
                g.tensor_tensor(x_row[k][:, :, D + 1:D + 3], vare[:, k % 2, :, :], powers[:, :, :], ALU.pow).then_inc(rstd, 1)
                pool.wait_ge(rstd, b + 1)
                g.tensor_tensor(c.xnorm[:, ds(b * TS, TS)], x_row[k][:, :, D + 1], x_row[k][:, :, D + 2], ALU.mult).then_inc(xnorm_done, 1)

            run(pool, roots)

        @blk.scalar
        def _(act):
            act.wait_ge(pad, NX + 2)

            def numbers(b, k):
                act.wait_ge(num, b + 1)
                nc.scalar.activation(c.num[:, ds(b * TS, TS), :], p_n[k % 2][:, :, :], ACT.Copy).then_inc(num_out, 1)

            def step(b, k, first, last):
                act.wait_ge(rstd, b + 1)
                act.dma_start(row_v[:, ds(b, 1), :, :], x_row[k][:, :, :]).then_inc(x_out[k], 16)
                act.wait_ge(tr, b * TS + TS)
                nc.scalar.activation(xn_t[k % 2][:, :], p_t[k % 2][:, :], ACT.Copy).then_inc(tr_out, 1)
                if not first:
                    numbers(b - 1, (k - 1) % NX)
                if last:
                    numbers(b, k)

            run(act, step)
            for k in range(NX):
                act.wait_ge(x_out[k], 16 * (NB // NX))

        @blk.vector
        def _(dve):
            v = nc.vector

            def stats(b, k):
                q = k % 2
                dve.wait_ge(x_in[k], b * (16 // NX) + (16 - k * (16 // NX)))
                for j in range(TS):
                    v.bn_stats(bn[:, q, j, :], x_row[k][:, j, 0:D]).then_inc(bn_done, 1)
                dve.wait_ge(bn_done, b * TS + TS)
                dve.sem_inc(passed, 1)
                for j in range(TS):
                    v.bn_aggr(x_row[k][:, j, D:D + 2], bn[:, q, j, :]).then_inc(mv_done, 1)
                dve.wait_ge(mv_done, b * TS + TS)
                v.tensor_copy(vare[:, q, :, 1], x_row[k][:, :, D + 1])
                v.tensor_scalar(vare[:, q, :, 0], x_row[k][:, :, D + 1], LN_EPS, None, ALU.add).then_inc(var_done, 1)

            def norm(b, k):
                dve.wait_ge(rstd, b + 1)
                wait(dve, tr, (b - 1) * TS)
                for j in range(TS):
                    v.tensor_scalar(xn[k % 2][:, j, :], x_row[k][:, j, 0:D], x_row[k][:, j, D:D + 1],
                                    x_row[k][:, j, D + 1:D + 2], ALU.subtract, ALU.mult).then_inc(xn_done, 1)

            def step(b, k, first, last):
                if first:
                    stats(b, k)
                if not last:
                    stats(b + 1, (k + 1) % NX)
                norm(b, k)

            run(dve, step)

        @blk.tensor
        def _(pe):
            def project(b, k):
                q = k % 2
                pe.wait_ge(tr_out, b + 1)
                wait(pe, num_out, b - 1)
                for j in range(TS):
                    last = nc.tensor.matmul(p_n[q][:, j, :], xn_t[q][:, j * P:(j + 1) * P], c.waff_t[:, :],
                                            start=True, stop=True)
                last.then_inc(num, 1)

            def step(b, k, first, last):
                q = k % 2
                for j in range(TS):
                    pe.wait_ge(xn_done, b * TS + (j + 1))
                    nc.tensor.transpose(p_t[q][:, j * P:(j + 1) * P], xn[q][:, j, :], c.ident[:, :]).then_inc(tr, 1)
                if not first:
                    project(b - 1, (k - 1) % NX)
                if last:
                    project(b, k)

            run(pe, step)


def consts(nc, m):
    class C:
        pass
    c = C()
    c.ident, c.ones = m.sb("ident", [P, P]), m.sb("ones", [P, P])
    c.identb, c.onesb, c.tri = (m.sb(n, [P, P], BF16) for n in ("identb", "onesb", "tri"))
    c.tie = m.sb("tie", [P, TPB, S])
    c.mask = m.sb("mask", [P, 4, P], BF16)
    c.iota, c.part, c.tile1, c.down = m.sb("iota", [P, P]), m.sb("part", [P, 1]), m.sb("tile1", [P, NT]), m.sb("down", [P, E])
    c.w1, c.w2 = m.sb("w1", [P, G, F]), m.sb("w2", [P, G, FC, D])
    c.b1s, c.chunk = m.sb("b1s", [P, G, P], BF16), m.sb("chunk", [P, FC, P], BF16)
    c.cst = m.sb("cst", [P, G, D], BF16)
    c.waff_t, c.wnorm, c.thr = m.sb("waff_t", [P, E]), m.sb("wnorm", [P, E]), m.sb("thr", [P, 1])
    c.wq, c.wk, c.wv, c.wproj = (m.sb(n, [P, D]) for n in ("wq", "wk", "wv", "wproj"))
    c.num, c.xnorm = m.sb("num", [P, NT, E]), m.sb("xnorm", [P, NT])
    c.gidx, c.sidx = m.sb("gidx", [P, NSX], I32), m.sb("sidx", [P, NSX], I32)
    c.eid = m.sb("eid", [1, NSX], I32)
    return c


def route(nc, m, c, tag):
    ctx = ExitStack()
    with ctx:
        t = Mem(nc, ctx)

        def sb(name, shape, dt=F32):
            return t.sb(f"{tag}_{name}", shape, dt)

        def sem(name):
            return t.sem(f"{tag}_{name}")

        GT = G * NT
        den = sb("den", [P, NT, E])
        AHEAD = 2 * TPB
        both = sb("both", [P, NT + AHEAD, 2 * E])
        aff, hot = both[:, 0:NT, 0:E], both[:, 0:NT, E:2 * E]
        amax, wmax, weight = sb("amax", [P, NT]), sb("wmax", [P, NT]), sb("weight", [P, NT, E])
        cell = sb("cell", [P, 8])
        batch_s = [sb(f"batch{k}", [P, TPB, 2 * E]) for k in range(2)]
        batch_t = [sb(f"batcht{k}", [P, 2 * S]) for k in range(2)]
        beats = [sb(f"beats{k}", [P, S]) for k in range(2)]
        rank, kept = sb("rank", [P, NT]), sb("kept", [P, NT])
        taken = sb("taken", [P, G, NT], BF16)
        total, upto = sb("total", [P, GT]), sb("upto", [P, GT])
        one_row = sb("one_row", [P, GT])
        ends, count, tiles, tile_end, start, shift = (sb(n, [P, G]) for n in ("ends", "count", "tiles", "tend", "start", "shift"))
        place, slot, row, colp = sb("place", [P, GT]), sb("slot", [P, NT]), sb("row", [P, NT]), sb("colp", [P, NT])
        eid_f = [sb(f"eidf{k}", [P, NSX]) for k in range(2)]
        NR = 4
        at_p = [sb(f"atp{k}", [P, NR, P], BF16) for k in range(2)]
        at_s = [sb(f"ats{k}", [P, NR, NS], BF16) for k in range(2)]
        at_t = [sb(f"att{k}", [P, NR, 2, NS], BF16) for k in range(2)]
        zero = sb("zero", [P, 2 * NS], BF16)
        lo, src, gsrc, away = sb("lo", [P, NS]), sb("src", [P, NS]), sb("gsrc", [P, NS]), sb("away", [P, NS])
        ps_sum = t.ps(f"{tag}_ps_sum", [P, 1])
        ps_t = [t.ps(f"{tag}_ps_t{k}", [P, 2 * S]) for k in range(2)]
        ps_b = [t.ps(f"{tag}_ps_b{k}", [P, TPB, S]) for k in range(2)]
        ps_pre = [t.ps(f"{tag}_ps_pre{k}", [P, 512]) for k in range(2)]
        ps_inv = t.ps(f"{tag}_ps_inv", [P, 2 * NS])

        vs, made = sem("vs"), sem("made")
        sum_ask, sum_got, e_ask, e_got = sem("sum_ask"), sem("sum_got"), sem("e_ask"), sem("e_got")
        hot_done, cut, tr, tr_out, row_b, ranked = (sem(n) for n in ("hot", "cut", "tr", "tro", "rowb", "ranked"))
        taken_done, counted, copied = sem("taken_done"), sem("counted"), sem("copied")
        s_done, onehot, put, inv = (sem(n) for n in ("s_done", "onehot", "put", "inv"))
        blk = ctx.enter_context(nc.Block())
        ROW_CREDIT = 2
        HB = GT // 2

        @blk.gpsimd
        def _(pool):
            nc.gpsimd.memset(both[:, NT:NT + AHEAD, :], 0.0).then_inc(made, 1)
            for k in range(2):
                nc.gpsimd.memset(batch_t[k][:, :], 0.0).then_inc(made, 1)
            nc.gpsimd.memset(zero[:, :], 0.0).then_inc(made, 1)
            nc.gpsimd.memset(one_row[:, :], 1.0).then_inc(made, 1)
            nc.gpsimd.memset(c.gidx[:, NS:NSX], 0).then_inc(made, 1)
            nc.gpsimd.memset(c.sidx[:, NS:NSX], 0).then_inc(made, 1)

        @blk.scalar
        def _(act):
            act.wait_ge(e_ask, 1)
            nc.scalar.activation(cell[:, 2:3], cell[:, 1:2], ACT.Exp, scale=-1.0).then_inc(e_got, 1)
            act.wait_ge(hot_done, 1)
            act.wait_ge(made, 7)
            for b in range(2):
                nc.scalar.activation(batch_s[b][:, :, :], both[:, b * TPB:(b + 1) * TPB, :], ACT.Copy).then_inc(cut, 1)
            with act.Fori(0, B // 2) as i:
                for k in range(2):
                    b = i * 2 + k
                    act.wait_ge(tr, b * 4 + 4)
                    act.wait_ge(row_b, b + 1)
                    nc.scalar.activation(batch_t[k][0:E, :], ps_t[k][0:E, :], ACT.Copy).then_inc(tr_out, 1)
                    nc.scalar.activation(batch_s[k][:, :, :], both[:, ds(b * TPB + 2 * TPB, TPB), :], ACT.Copy).then_inc(cut, 1)

        @blk.tensor
        def _(pe):
            pe.wait_ge(sum_ask, 1)
            nc.tensor.matmul(ps_sum[:, :], c.ones[:, :], cell[:, 0:1], start=True, stop=True).then_inc(sum_got, 1)
            pe.sem_inc(row_b, ROW_CREDIT)

            def as_rows(b, k):
                pe.wait_ge(cut, b + 1)
                for w in range(2):
                    for j in range(TPB):
                        nc.tensor.transpose(ps_t[k][0:E, w * S + j * P:w * S + (j + 1) * P],
                                            batch_s[k][:, j, w * E:(w + 1) * E], c.ident[:, :]).then_inc(tr, 1)

            as_rows(0, 0)
            with pe.Fori(0, B // 2) as i:
                for k in range(2):
                    b = i * 2 + k
                    as_rows(b + 1, (k + 1) % 2)
                    pe.wait_ge(tr_out, b + 1)
                    pe.wait_ge(ranked, b * TPB + TPB)
                    for j in range(TPB):
                        last = nc.tensor.matmul(ps_b[k][:, j, :], batch_t[k][:, S + j * P:S + (j + 1) * P],
                                                batch_t[k][:, 0:S], start=True, stop=True)
                    last.then_inc(row_b, 1)
            pe.wait_ge(taken_done, 2)
            flat = taken[:, :, :].rearrange("p g t -> p (g t)")
            for h in range(2):
                nc.tensor.matmul(ps_pre[h][:, 0:HB], c.onesb[:, :], flat[:, h * HB:(h + 1) * HB], start=True, stop=True).then_inc(counted, 1)
            for h in range(2):
                pe.wait_ge(copied, h + 1)
                nc.tensor.matmul(ps_pre[h][:, 0:HB], c.tri[:, :], flat[:, h * HB:(h + 1) * HB], start=True, stop=True).then_inc(counted, 1)
            nc.tensor.matmul(ps_inv[:, :], zero[:, 0:P], zero[:, :], start=True, stop=False, skip_group_check=True)
            pe.sem_inc(put, 2 * NR)
            with pe.Fori(0, NT // NR // 2) as i:
                for k in range(2):
                    pe.wait_ge(onehot, i * 2 + (k + 1))
                    for r in range(NR):
                        nc.tensor.matmul(ps_inv[:, :], at_p[k][:, r, :], at_t[k][:, r, :, :].rearrange("p a s -> p (a s)"),
                                         start=False, stop=False, skip_group_check=True).then_inc(put, 1)
            nc.tensor.matmul(ps_inv[:, :], zero[:, 0:P], zero[:, :], start=False, stop=True, skip_group_check=True).then_inc(inv, 1)

        @blk.vector
        def _(dve):
            v = nc.vector
            s = Steps(dve, vs)

            def bc(col, shape, axis):
                return col.unsqueeze(axis).to_broadcast(shape)

            full = [P, NT, E]
            s.step(v.tensor_tensor(den[:, :, :], bc(c.xnorm[:, :], full, 2), bc(c.wnorm[:, :], full, 1), ALU.mult))
            s.step(v.tensor_scalar(den[:, :, :], den[:, :, :], float(D) ** 0.5, 1e-9, ALU.mult, ALU.add))
            s.step(v.reciprocal(den[:, :, :], den[:, :, :]))
            s.step(v.tensor_tensor(aff, c.num[:, :, :], den[:, :, :], ALU.mult))
            v.tensor_reduce(cell[:, 0:1], aff, axis=AX.XY, op=ALU.add).then_inc(sum_ask, 1)
            s.step(v.tensor_reduce(amax[:, :], aff, axis=AX.X, op=ALU.max))
            s.step(v.tensor_tensor(weight[:, :, :], aff, bc(amax[:, :], full, 2), ALU.is_equal))
            s.step(v.tensor_tensor(weight[:, :, :], weight[:, :, :], bc(c.down[:, :], full, 1), ALU.mult))
            s.step(v.tensor_reduce(wmax[:, :], weight[:, :, :], axis=AX.X, op=ALU.max))
            v.tensor_tensor(hot, weight[:, :, :], bc(wmax[:, :], full, 2), ALU.is_equal).then_inc(hot_done, 1)
            dve.wait_ge(sum_got, 1)
            v.scalar_tensor_tensor(cell[:, 1:2], ps_sum[:, :], 1.0 / (T * E), c.thr[:, :], ALU.mult, ALU.subtract).then_inc(e_ask, 1)
            dve.wait_ge(e_got, 1)
            s.step(v.tensor_scalar(cell[:, 3:4], cell[:, 2:3], 1.0, None, ALU.add))
            s.step(v.reciprocal(cell[:, 4:5], cell[:, 3:4]))
            s.step(v.tensor_scalar(cell[:, 5:6], cell[:, 4:5], float(S), 4.0, ALU.mult, ALU.max))
            dve.sem_inc(ranked, 2 * TPB)
            with dve.Fori(0, B // 2) as i:
                for k in range(2):
                    b = i * 2 + k
                    dve.wait_ge(row_b, b + (1 + ROW_CREDIT))
                    for j in range(TPB):
                        dve.wait_ge(ranked, b * TPB + (j + 2 * TPB - 1))
                        v.scalar_tensor_tensor(beats[j][:, :], ps_b[k][:, j, :], amax[:, ds(b * TPB + j, 1)],
                                               c.tie[:, j, :], ALU.subtract, ALU.is_gt,
                                               accum_out=rank[:, ds(b * TPB + j, 1)]).then_inc(ranked, 1)
            dve.wait_ge(ranked, NT + 2 * TPB)
            s.step(v.tensor_scalar(kept[:, :], rank[:, :], 1.0, cell[:, 5:6], ALU.add, ALU.is_le))
            v.tensor_tensor(taken[:, 0:E, :].rearrange("p e t -> p t e"), hot, bc(kept[:, :], full, 2), ALU.mult).then_inc(taken_done, 1)
            v.tensor_scalar(taken[:, E, :], kept[:, :], -1.0, 1.0, ALU.mult, ALU.add).then_inc(taken_done, 1)
            dve.wait_ge(made, 7)
            for h in range(2):
                dve.wait_ge(counted, h + 1)
                v.tensor_copy(total[:, h * HB:(h + 1) * HB], ps_pre[h][:, 0:HB]).then_inc(copied, 1)
            dve.wait_ge(copied, 2)
            s.step(v.tensor_tensor_scan(upto[:, :], one_row[:, :], total[:, :], 0.0, ALU.mult, ALU.add))
            s.step(v.tensor_copy(ends[:, :], upto[:, :].rearrange("p (g t) -> p g t", g=G)[:, :, NT - 1]))
            s.step(v.tensor_copy(count[:, :], ends[:, :]))
            s.step(v.tensor_tensor(count[:, 1:G], ends[:, 1:G], ends[:, 0:G - 1], ALU.subtract))
            s.step(v.tensor_scalar(tiles[:, :], count[:, :], 1.0 / P, (P - 1) / P - 0.49609375, ALU.mult, ALU.add))
            s.step(v.tensor_scalar(tiles[:, :], tiles[:, :], MAGIC, None, ALU.add))
            s.step(v.tensor_scalar(tiles[:, :], tiles[:, :], MAGIC, None, ALU.subtract))
            s.step(v.tensor_tensor_scan(tile_end[:, :], one_row[:, 0:G], tiles[:, :], 0.0, ALU.mult, ALU.add))
            s.step(v.tensor_tensor(start[:, :], tile_end[:, :], tiles[:, :], ALU.subtract))
            s.step(v.tensor_tensor(shift[:, :], count[:, :], ends[:, :], ALU.subtract))
            s.step(v.scalar_tensor_tensor(shift[:, :], start[:, :], float(P), shift[:, :], ALU.mult, ALU.add))
            grid = "p (g t) -> p g t"
            s.step(v.tensor_tensor(upto[:, :], upto[:, :], total[:, :], ALU.subtract))
            s.step(v.tensor_tensor(upto[:, :].rearrange(grid, g=G), upto[:, :].rearrange(grid, g=G),
                                   bc(shift[:, :], [P, G, NT], 2), ALU.add))
            for h in range(2):
                dve.wait_ge(counted, h + 3)
                s.step(v.tensor_tensor(place[:, h * HB:(h + 1) * HB], ps_pre[h][:, 0:HB], upto[:, h * HB:(h + 1) * HB], ALU.add))
            s.step(v.tensor_tensor(place[:, :].rearrange(grid, g=G), place[:, :].rearrange(grid, g=G), taken[:, :, :], ALU.mult))
            s.step(v.tensor_reduce(slot[:, :], place[:, :].rearrange("p (g t) -> p t g", g=G), axis=AX.X, op=ALU.add))
            s.step(v.tensor_scalar(row[:, :], slot[:, :], 1.0 / P, -0.49609375, ALU.mult, ALU.add))
            s.step(v.tensor_scalar(row[:, :], row[:, :], MAGIC, None, ALU.add))
            s.step(v.tensor_scalar(row[:, :], row[:, :], MAGIC, None, ALU.subtract))
            s.step(v.scalar_tensor_tensor(colp[:, :], row[:, :], float(-P), slot[:, :], ALU.mult, ALU.add))
            grid = [P, NR, NS]
            with dve.Fori(0, NT // NR // 2) as i:
                for k in range(2):
                    n = i * 2 + k
                    v.tensor_tensor(at_s[k][:, :, :], bc(c.iota[:, 0:NS], grid, 1), bc(row[:, ds(n * NR, NR)], grid, 2),
                                    ALU.is_equal).then_inc(s_done, 1)
                    dve.wait_ge(put, n * NR + NR)
                    v.tensor_tensor(at_p[k][:, :, :], bc(c.iota[:, :], [P, NR, P], 1), bc(colp[:, ds(n * NR, NR)], [P, NR, P], 2),
                                    ALU.is_equal)
                    dve.wait_ge(s_done, n + 1)
                    v.tensor_scalar(at_t[k][:, :, 1, :], at_s[k][:, :, :], c.part[:, :], None, ALU.mult)
                    v.tensor_tensor(at_t[k][:, :, 0, :], at_s[k][:, :, :], bc(c.tile1[:, ds(n * NR, NR)], grid, 2),
                                    ALU.mult).then_inc(onehot, 1)
            s.step(v.tensor_scalar(eid_f[0][:, :], c.iota[:, 0:NSX], tile_end[:, 0:1], None, ALU.is_ge))
            for g in range(1, E):
                s.step(v.scalar_tensor_tensor(eid_f[g % 2][:, :], c.iota[:, 0:NSX], tile_end[:, g:g + 1],
                                              eid_f[(g - 1) % 2][:, :], ALU.is_ge, ALU.add))
            s.step(v.tensor_copy(c.eid[:, :], eid_f[(E - 1) % 2][0:1, :]))
            dve.wait_ge(inv, 1)
            s.step(v.tensor_scalar(lo[:, :], ps_inv[:, NS:2 * NS], float(-P), None, ALU.add))
            s.step(v.scalar_tensor_tensor(src[:, :], ps_inv[:, 0:NS], float(P), lo[:, :], ALU.mult, ALU.add))
            s.step(v.tensor_scalar(gsrc[:, :], src[:, :], 0.0, None, ALU.max))
            s.step(v.tensor_copy(c.gidx[:, 0:NS], gsrc[:, :]))
            s.step(v.tensor_scalar(away[:, :], src[:, :], 0.0, float(4 * T), ALU.is_lt, ALU.mult))
            s.step(v.tensor_tensor(away[:, :], away[:, :], src[:, :], ALU.add))
            s.step(v.tensor_copy(c.sidx[:, 0:NS], away[:, :]))


def experts(nc, m, io, c, tag, y_dram):
    ctx = ExitStack()
    with ctx:
        t = Mem(nc, ctx)

        def sem(name):
            return t.sem(f"{tag}_{name}")

        OWN = 4
        HU = U // 2
        x_row = [t.sb(f"{tag}_x{k}", [P, XW]) for k in range(U)]
        y_row = [t.sb(f"{tag}_y{k}", [P, D]) for k in range(U)]
        gi, si = ([t.sb(f"{tag}_{n}{h}", [P, HU], I32) for h in range(2)] for n in ("gi", "si"))
        xn = [t.sb(f"{tag}_xn{k}", [P, D]) for k in range(2)]
        xn_t = [t.sb(f"{tag}_xnt{k}", [P, P]) for k in range(2)]
        hid_t = [t.sb(f"{tag}_ht{k}", [P, FC, P]) for k in range(2)]
        w1_own = [t.sb(f"{tag}_w1own{k}", [P, F]) for k in range(OWN)]
        ps_x = [t.ps(f"{tag}_ps_x{k}", [P, P]) for k in range(2)]
        ps_h = [t.ps(f"{tag}_ps_h{k}", [P, FC, P]) for k in range(2)]
        ps_y = [t.ps(f"{tag}_ps_y{k}", [P, D]) for k in range(2)]
        x_in = [sem(f"xin{k}") for k in range(U)]
        y_out = [sem(f"yout{k}") for k in range(U)]
        cell = sem("cell")
        xn_done, x_tr, x_tr_out, up, gelu, down, y_done, w1_done = (
            sem(n) for n in ("xn", "xtr", "xtro", "up", "gelu", "down", "y", "w1"))
        passed = sem("passed")
        BOTH = 2
        blk = ctx.enter_context(nc.Block())
        rows = io["rows"]

        def experts_of(eng, j, n):
            _, e = nc.values_load_multi_w_load_instructions(c.eid[0:1, ds(j, n)], engines=[eng.engine], min_val=0, max_val=E)
            return e

        @blk.sync
        def _(sp):
            for k in range(U):
                sp.wait_ge(y_out[k], 16 * (NS // U))

        @blk.gpsimd
        def _(pool):
            g = nc.gpsimd

            def gather(k):
                pool.indirect_dma_start(x_row[k][:, :], None, rows,
                                        bass.IndirectOffsetOnAxis(ap=gi[k // HU][:, k % HU:k % HU + 1], axis=0)).then_inc(x_in[k], 16)

            for h in range(2):
                g.tensor_copy(gi[h][:, :], c.gidx[:, h * HU:(h + 1) * HU]).then_inc(cell, 1)
            pool.wait_ge(cell, 2)
            for k in range(U):
                gather(k)
            with pool.Fori(0, NS // U) as i:
                for h in range(2):
                    for k in range(h * HU, (h + 1) * HU):
                        pool.wait_ge(x_in[k], i * 16 + 16)
                        pool.wait_ge(y_out[k], i * 16)
                    pool.sem_inc(passed, 1)
                    g.tensor_copy(gi[h][:, :], c.gidx[:, ds(i * U + (U + h * HU), HU)]).then_inc(cell, 1)
                    g.tensor_copy(si[h][:, :], c.sidx[:, ds(i * U + h * HU, HU)]).then_inc(cell, 1)
                    pool.wait_ge(cell, i * 4 + (2 * h + 4))
                    pool.sem_inc(passed, 1)
                    for k in range(h * HU, (h + 1) * HU):
                        pool.wait_ge(y_done, i * U + (k + 1))
                        pool.sem_inc(passed, 1)
                        pool.indirect_dma_start(y_dram, bass.IndirectOffsetOnAxis(ap=si[h][:, k % HU:k % HU + 1], axis=0),
                                                y_row[k][:, :], None, bounds_check=T - 1, oob_is_err=False).then_inc(y_out[k], 16)
                        gather(k)
            for k in range(U):
                pool.wait_ge(x_in[k], 16 * (NS // U + 1))

        @blk.scalar
        def _(act):
            a = nc.scalar

            def turn_x(j, k):
                act.wait_ge(x_tr, j + 1)
                act.wait_ge(up, j + 1)
                a.activation(xn_t[k][:, :], ps_x[k][:, :], ACT.Copy).then_inc(x_tr_out, 1)

            def bend(j, k):
                act.wait_ge(up, j + (1 + BOTH))
                act.wait_ge(down, j + 1)
                a.activation(hid_t[k][:, :, :], ps_h[k][:, :, :], ACT.Gelu).then_inc(gelu, 1)

            act.sem_inc(gelu, BOTH)
            turn_x(0, 0)
            turn_x(1, 1)
            bend(0, 0)
            with act.Fori(0, NS // U) as i:
                for k in range(U):
                    j = i * U + k
                    turn_x(j + 2, k % 2)
                    bend(j + 1, (k + 1) % 2)

        @blk.tensor
        def _(pe):
            te = nc.tensor

            def turn_x(j, k):
                pe.wait_ge(xn_done, j + 1)
                if not isinstance(j, int):
                    pe.wait_ge(x_tr_out, j - 1)
                te.transpose(ps_x[k][:, :], xn[k][:, :], c.ident[:, :]).then_inc(x_tr, 1)

            def expand(j, k, s, e):
                pe.wait_ge(x_tr_out, j + 1)
                pe.wait_ge(gelu, j + 1)
                pe.wait_ge(w1_done, j + 1)
                te.matmul(ps_h[k][:, :, :].rearrange("p f s -> p (f s)"), c.b1s[:, ds(e, 1), :].rearrange("p a f -> p (a f)"),
                          c.chunk[:, :, :].rearrange("p f s -> p (f s)"), start=True, stop=False, skip_group_check=True)
                for f in range(FC):
                    last = te.matmul(ps_h[k][:, f, :], w1_own[s][:, f * P:(f + 1) * P], xn_t[k][:, :],
                                     start=False, stop=(f == FC - 1), skip_group_check=True)
                last.then_inc(up, 1)

            def contract(j, k, e):
                pe.wait_ge(gelu, j + (1 + BOTH))
                pe.wait_ge(y_done, j)
                te.matmul(ps_y[k][:, :], c.onesb[:, :], c.cst[:, ds(e, 1), :].rearrange("p a d -> p (a d)"), start=True, stop=False)
                for f in range(FC):
                    last = te.matmul(ps_y[k][:, :], hid_t[k][:, f, :], c.w2[:, ds(e, 1), f, :].rearrange("p a d -> p (a d)"),
                                     start=False, stop=(f == FC - 1))
                last.then_inc(down, 1)

            pe.sem_inc(up, BOTH)
            pe.sem_inc(down, BOTH)
            turn_x(0, 0)
            turn_x(1, 1)
            expand(0, 0, 0, experts_of(pe, 0, 1)[0])
            with pe.Fori(0, NS // U) as i:
                for k in range(U):
                    j = i * U + k
                    own = experts_of(pe, j, 2) if k == 0 else (own[1], *experts_of(pe, j + 1, 1))
                    turn_x(j + 2, k % 2)
                    expand(j + 1, (k + 1) % 2, (k + 1) % OWN, own[1])
                    contract(j, k % 2, own[0])

        @blk.vector
        def _(dve):
            v = nc.vector

            def norm(j, s, turn):
                dve.wait_ge(x_in[s], turn * 16 + 16)
                v.tensor_scalar(xn[s % 2][:, :], x_row[s][:, 0:D], x_row[s][:, D:D + 1], x_row[s][:, D + 1:D + 2],
                                ALU.subtract, ALU.mult).then_inc(xn_done, 1)

            def fetch(j, s, e):
                if not isinstance(j, int):
                    dve.wait_ge(up, j + (1 + BOTH - OWN))
                v.tensor_copy(w1_own[s][:, :], c.w1[:, ds(e, 1), :].rearrange("p a f -> p (a f)")).then_inc(w1_done, 1)

            def finish(j, s, turn):
                dve.wait_ge(down, j + (1 + BOTH))
                dve.wait_ge(y_out[s], turn * 16)
                v.scalar_tensor_tensor(y_row[s][:, :], ps_y[s % 2][:, :], 0.5, x_row[s][:, 0:D], ALU.mult, ALU.add).then_inc(y_done, 1)

            norm(0, 0, 0)
            norm(1, 1, 0)
            e = experts_of(dve, 0, 2)
            fetch(0, 0, e[0])
            fetch(1, 1, e[1])
            dve.wait_ge(x_tr, 1)
            norm(2, 2, 0)
            with dve.Fori(0, NS // U) as i:
                for k in range(U):
                    j = i * U + k
                    if k % HU == 0:
                        e = experts_of(dve, j + 2, HU)
                    dve.wait_ge(x_tr, j + 2)
                    norm(j + 3, (k + 3) % U, i if k + 3 < U else i + 1)
                    fetch(j + 2, (k + 2) % OWN, e[k % HU])
                    finish(j, k, i)


def attention(nc, m, io, c, x_dram):
    ctx = ExitStack()
    with ctx:
        t = Mem(nc, ctx)
        sb = lambda n, s, dt=F32: t.sb(f"at_{n}", s, dt)
        sem = lambda n: t.sem(f"at_{n}")
        two = lambda n, s, dt=F32: [sb(f"{n}{k}", s, dt) for k in range(2)]
        HP = H // 2
        QUADS = H // 4
        NP = 12
        NQ = 4
        RING = 6
        LAG = 4
        ROWS = 96
        QUERY_TILES = [[(1, 4)], [(1, 5)], [(1, 6)], [(1, 7)], [(1, 8)], [(1, 9), (1, 10)], [(1, 11)],
                       [], [(2, 0)], [(2, 1)], [(2, 2)], [(2, 3)]]
        SCALE = HD ** -0.5

        xa, xr, x2 = two("xa", [P, TPB, D + 2]), two("xr", [P, TPB, D]), two("x2", [P, TPB, XW])
        bn, vare = two("bn", [P, TPB, 6]), two("vare", [P, TPB])
        bn2, vare2 = two("bn2", [P, TPB, 6]), two("vare2", [P, TPB, 2])
        xn, xt = two("xn", [P, TPB, D]), two("xt", [P, S])
        xn2, x2t = two("xn2", [P, TPB, D]), two("x2t", [P, S])
        part, rest = two("part", [P, 6, S], BF16), two("rest", [P, 2 * S])
        qs = [sb(f"qs{k}", [P, HP, S], BF16) for k in range(NQ)]
        kb = [sb(f"kb{k}", [P, HP, 2, S], BF16) for k in range(NQ)]
        vp = [sb(f"vp{k}", [P, TPB, H, 32]) for k in range(NQ)]
        pt = [sb(f"pt{k}", [P, 2 * S]) for k in range(RING)]
        ot, on, ont = two("ot", [P, QUADS, S]), two("on", [P, TPB, D]), two("ont", [P, S])
        rden = two("rden", [P, H])
        mx, nr = two("mx", [P, TPB, 2, HP]), two("nr", [P, TPB, H])
        mp, mt = two("mp", [P, TPB, 3, H], BF16), two("mt", [3 * H, S], BF16)
        powers, mhalf, pick, sel = sb("powers", [P, TPB, 2]), sb("mhalf", [P, TPB]), sb("pick", [P, 2, 3]), sb("sel", [P, 2])
        pp = [t.ps(f"at_pp{k}", [P, 2 * S]) for k in range(2)]
        pm = [t.ps(f"at_pm{k}", [P, 2 * S]) for k in range(2)]
        po = t.ps("at_po", [P, QUADS * S])
        mi = [t.ps(f"at_mi{k}", [P, 2 * S]) for k in range(2)]
        qkd = [nc.dram_tensor(f"at_qkd{k}", (6 * P, S), BF16, kind="Internal").ap() for k in range(2)]

        xa_in, xr_in, row_out = ([sem(f"{n}{k}") for k in range(2)] for n in ("xa_in", "xr_in", "row_out"))
        qk_in, m_in = ([sem(f"{n}{k}") for k in range(NQ)] for n in ("qk_in", "m_in"))
        part_out = [sem(f"part_out{k}") for k in range(2)]
        (zeroed, picked, selected, mv1, bnd1, var1, rstd1, xn_done, xt_tr, xt_out, qk_mm, a_done, r_done, b_done, part_done,
         v_mm, v_out, pre_done, maxed, cuts, mp_done, mt_tr, mt_out, main_done, exped, masked, pv_done, ot_out,
         otr, rd, on_done, ont_tr, ont_out, proj_mm, x2_done, bnd2, mv2, var2, rstd2, xn2_done, x2t_tr, x2t_out, num_mm,
         num_out) = (sem(n) for n in (
             "zeroed picked selected mv1 bnd1 var1 rstd1 xn_done xt_tr xt_out qk_mm a_done r_done b_done part_done "
             "v_mm v_out pre_done maxed cuts mp_done mt_tr mt_out main_done exped masked pv_done ot_out "
             "otr rd on_done ont_tr ont_out proj_mm x2_done bnd2 mv2 var2 rstd2 xn2_done x2t_tr x2t_out num_mm "
             "num_out").split())
        xnorm_done, kb_zero = sem("xnorm"), sem("kb_zero")
        passed = sem("passed")
        NZ = NQ * 3 + 2 + 3
        blk = ctx.enter_context(nc.Block())
        x_v = x_dram.rearrange("(b k p) d -> p b k d", k=TPB, p=P)
        row_v = io["rows"].rearrange("(b k p) w -> p b k w", k=TPB, p=P)

        def wait(eng, s, n, most=None):
            if isinstance(n, int):
                n = n if most is None else min(n, most)
                if n <= 0:
                    return
            eng.wait_ge(s, n)

        def dma_count(b, slots, each=1):
            return lambda k: b * (16 * each // slots) + (16 * each - (k % slots) * (16 * each // slots))

        def turns(turn):
            for b in range(-4, NQ):
                turn(b, b % NQ, lambda o, b=b: 0 <= b + o < B)
            yield
            for b in range(B - NQ, B + 2):
                turn(b, b % NQ, lambda o, b=b: 0 <= b + o < B)
            yield

        def run(eng, turn):
            emit = turns(turn)
            next(emit)
            with eng.Fori(1, B // NQ - 1) as i:
                for k in range(NQ):
                    turn(i * NQ + k, k, lambda o: True)
            next(emit)

        @blk.sync
        def _(sp):
            sp.wait_ge(zeroed, NZ)
            def turn(b, k, has):
                if has(4):
                    wait(sp, xn_done, (b + 3) * TPB)
                    sp.dma_start(xa[k % 2][:, :, 0:D], x_v[:, ds(b + 4, 1), :, :]).then_inc(xa_in[k % 2], 16)
                if has(0):
                    wait(sp, x2_done, b - 1)
                    sp.dma_start(xr[k % 2][:, :, :], x_v[:, ds(b, 1), :, :]).then_inc(xr_in[k % 2], 16)
                if has(3):
                    n, q, h = b + 3, (k + 3) % NQ, (k + 1) % 2
                    wait(sp, part_done, n + 1)
                    sp.sem_inc(passed, 1)
                    if isinstance(b, int) and n < NQ:
                        sp.wait_ge(kb_zero, n + 1)
                    wait(sp, main_done, (n - NQ + 1) * NP)
                    sp.sem_inc(passed, 1)
                    wait(sp, qk_in[(q + 2) % NQ], dma_count(n - 2, NQ, 12)(q + 2))
                    for r in range(2):
                        sp.dma_start(qkd[h][6 * 64 * r:6 * 64 * (r + 1), :].rearrange("(t w) n -> w t n", t=6),
                                     part[h][64 * r:64 * r + 64, :, :]).then_inc(part_out[h], 16)
                    wait(sp, part_out[h], dma_count(n, 2, 2)(h))
                    src = qkd[h].rearrange("(a g) n -> a g n", g=HP)
                    for r in range(2):
                        for row, size in ((0, 24), (24, 16), (40, 8)):
                            to, q0, k0 = 48 * r + row, 48 * r, 48 * (r + 1) - size
                            sp.dma_start(kb[q][to:to + size, :, r, :], src[k0:k0 + size, :, :]).then_inc(qk_in[q], 16)
                            sp.dma_start(qs[q][to:to + size, :, :], src[q0:q0 + size, :, :]).then_inc(qk_in[q], 16)
                if has(-2):
                    wait(sp, rstd2, b - 1)
                    sp.dma_start(row_v[:, ds(b - 2, 1), :, :], x2[k % 2][:, :, :]).then_inc(row_out[k % 2], 16)

            run(sp, turn)
            for k in range(2):
                sp.wait_ge(row_out[k], 16 * (B // 2))

        @blk.gpsimd
        def _(pool):
            g = nc.gpsimd
            for k in range(NQ):
                g.memset(qs[k][ROWS:P, :, :], 0.0).then_inc(zeroed, 1)
            pool.wait_ge(zeroed, NQ)
            g.memset(mhalf[:, :], -0.5).then_inc(zeroed, 1)
            g.memset(powers[:, :, 0:1], -0.5).then_inc(zeroed, 1)
            g.memset(powers[:, :, 1:2], 0.5).then_inc(zeroed, 1)
            for k in range(2):
                g.memset(x2[k][:, :, D + 3:XW], 0.0).then_inc(zeroed, 1)
            for k in range(NQ):
                g.memset(vp[k][:, :, :, HD + 1:32], 0.0).then_inc(zeroed, 1)
                g.memset(vp[k][:, :, :, HD:HD + 1], 1.0).then_inc(zeroed, 1)
            g.memset(pick[:, :, :], 0.0).then_inc(picked, 1)
            pool.wait_ge(picked, 1)
            g.affine_select(out=pick[:, :, :], in_=pick[:, :, :], compare_op=ALU.not_equal, fill=-1.0,
                            base=-ROWS, pattern=[[-1, 2], [-2, 3]], channel_multiplier=1).then_inc(picked, 1)

            def turn(b, k, has):
                for u in range(NP):
                    if has(0):
                        wait(pool, exped, b * NP + (u + 1))
                        pool.sem_inc(passed, 1)
                        n = 4 if u % 3 == 2 else 2
                        tile = pt[u % RING][:, :].rearrange("p (h q) -> p h q", h=n)[:, :, 0:P]
                        g.affine_select(out=tile, in_=tile, compare_op=ALU.is_ge, fill=0.0, base=0,
                                        pattern=[[0, n], [1, P]], channel_multiplier=-1).then_inc(masked, 1)
                    if u == 10 and has(-1):
                        n, q = b - 1, (k - 1) % 2
                        wait(pool, var2, n + 1)
                        g.tensor_tensor(x2[q][:, :, D + 1:D + 3], vare2[q][:, :, :], powers[:, :, :], ALU.pow).then_inc(rstd2, 1)
                        wait(pool, rstd2, n + 1)
                        g.tensor_tensor(c.xnorm[:, ds(n * TPB, TPB)], x2[q][:, :, D + 1], x2[q][:, :, D + 2], ALU.mult).then_inc(xnorm_done, 1)
                    if u == 5 and has(3):
                        q = (k + 1) % 2
                        wait(pool, b_done, b + 4)
                        g.tensor_tensor(part[q][:, 2:4, :], rest[q][:, :].rearrange("p (a n) -> p a n", a=2), part[q][:, 1:5:3, :],
                                        ALU.subtract).then_inc(part_done, 1)
                    if u == 6 and has(1):
                        n, q = b + 1, (k + 1) % 2
                        wait(pool, maxed, (n + 1) * NP)
                        pool.sem_inc(passed, 1)
                        flat = mx[q][:, :, :, :].rearrange("p j r g -> p j (r g)")
                        g.tensor_copy(mp[q][:, :, 0, :], flat).then_inc(cuts, 1)
                        wait(pool, cuts, n * 3 + 1)
                        g.tensor_tensor(nr[q][:, :, :], flat, mp[q][:, :, 0, :], ALU.subtract).then_inc(cuts, 1)
                        wait(pool, cuts, n * 3 + 2)
                        pool.sem_inc(passed, 1)
                        g.tensor_copy(mp[q][:, :, 1, :], nr[q][:, :, :]).then_inc(cuts, 1)
                        wait(pool, cuts, n * 3 + 3)
                        g.tensor_tensor(mp[q][:, :, 2, :], nr[q][:, :, :], mp[q][:, :, 1, :], ALU.subtract).then_inc(mp_done, 1)
                    if u == 8 and has(4):
                        wait(pool, var1, b + 5)
                        g.tensor_tensor(xa[k % 2][:, :, D + 1], vare[k % 2][:, :], mhalf[:, :], ALU.pow).then_inc(rstd1, 1)

            run(pool, turn)

        @blk.scalar
        def _(act):
            a = nc.scalar
            act.wait_ge(zeroed, NZ)

            def turn(b, k, has):
                for u in range(NP):
                    if has(0):
                        wait(act, main_done, b * NP + (u + 1))
                        wait(act, pv_done, b * NP + (u + 1 - RING))
                        a.activation(pt[u % RING][:, :], pm[u % 2], ACT.Exp, scale=SCALE).then_inc(exped, 1)
                    if u == 0 and has(3):
                        wait(act, xt_tr, (b + 4) * TPB)
                        a.activation(xt[(k + 1) % 2][:, :], mi[0][:, 0:S], ACT.Copy).then_inc(xt_out, 1)
                    if u == 1 and has(-2):
                        wait(act, x2t_tr, (b - 1) * TPB)
                        a.activation(x2t[k % 2][:, :], mi[1][:, 0:S], ACT.Copy).then_inc(x2t_out, 1)
                    if u == 2 and has(3):
                        h = (k + 1) % 2
                        wait(act, qk_mm, b + 4)
                        wait(act, part_out[h], dma_count(b + 1, 2, 2)(h))
                        a.activation(part[h][:, 0:6:5, :], mi[0].rearrange("p (a n) -> p a n", a=2), ACT.Copy).then_inc(a_done, 1)
                    if u == 3 and has(-2):
                        wait(act, num_mm, b - 1)
                        a.activation(c.num[:, ds((b - 2) * TPB, TPB), :], mi[1][:, 0:TPB * E].rearrange("p (j e) -> p j e", e=E),
                                     ACT.Copy).then_inc(num_out, 1)
                    if u == 4 and has(-1):
                        wait(act, pv_done, b * NP)
                        a.activation(ot[(k - 1) % 2][:, 2:4, :].rearrange("p g q -> p (g q)"), po[:, 2 * S:4 * S],
                                     ACT.Copy).then_inc(ot_out, 1)
                    if u == 4 and has(3):
                        h = (k + 1) % 2
                        wait(act, r_done, b + 4)
                        a.activation(part[h][:, 1:5:3, :], rest[h][:, :].rearrange("p (a n) -> p a n", a=2), ACT.Copy).then_inc(b_done, 1)
                    if u == 5 and has(3):
                        wait(act, v_mm, b + 4)
                        wait(act, pv_done, b * NP)
                        a.activation(vp[(k + 3) % NQ][:, :, :, 0:HD].rearrange("p j h d -> p (j h) d"),
                                     mi[0][:, 0:TPB * D].rearrange("p (h d) -> p h d", d=HD), ACT.Copy).then_inc(v_out, 1)
                    if u == 7 and has(-1):
                        wait(act, ont_tr, b)
                        a.activation(ont[(k - 1) % 2][:, :], mi[1][:, 0:S], ACT.Copy).then_inc(ont_out, 1)
                    if u == 9 and has(1):
                        q = (k + 1) % NQ
                        wait(act, mt_tr, b + 2)
                        wait(act, m_in[(q - 2) % NQ], dma_count(b - 1, NQ)(q - 2))
                        a.activation(mt[q % 2][:, :], mi[0].bitcast(BF16)[0:3 * H, 0:S], ACT.Copy).then_inc(mt_out, 1)
                        wait(act, mt_out, b + 2)
                        act.dma_start(qs[q][ROWS:ROWS + 6, :, :], mt[q % 2][:, :].unsqueeze(1)).then_inc(m_in[q], 16)
                    if u == 10 and has(0):
                        wait(act, pv_done, b * NP + 6)
                        wait(act, otr, (b - 1) * TPB)
                        a.activation(ot[k % 2][:, 0:2, :].rearrange("p g q -> p (g q)"), po[:, 0:2 * S], ACT.Copy).then_inc(ot_out, 1)
                if isinstance(b, int) and b < 0:
                    if b == -NQ:
                        act.wait_ge(selected, 1)
                    a.activation(kb[b + NQ][ROWS:P, :, :, :], sel[ROWS:P, :].unsqueeze(1).unsqueeze(3).to_broadcast([P - ROWS, HP, 2, S]),
                                 ACT.Copy).then_inc(selected, 1)

            run(act, turn)

        @blk.tensor
        def _(pe):
            te = nc.tensor
            pe.wait_ge(zeroed, NZ)

            def turn(b, k, has):
                def scores_by_query(o, v):
                    n, s, out = b + o, (k + o) % NQ, pp[v % 2]
                    if v == 0:
                        wait(pe, qk_in[s], dma_count(n, NQ, 12)(s))
                    wait(pe, maxed, n * NP + (v - 1))
                    if v < 4:
                        for w in range(2):
                            te.matmul(out[:, w * S:(w + 1) * S], qs[s][0:ROWS, 2 * v + w, 0:P], kb[s][0:ROWS, 2 * v + w, :, 0:P],
                                      start=(w == 0), stop=False, skip_group_check=True)
                        te.matmul(out, c.identb[:, :], c.mask[:, :, :].rearrange("p a q -> p (a q)"),
                                  start=False, stop=True, skip_group_check=True).then_inc(pre_done, 1)
                    else:
                        te.matmul(out, qs[s][0:ROWS, v - 4, P:S], kb[s][0:ROWS, v - 4, :, :].rearrange("p r q -> p (r q)"),
                                  start=True, stop=False, skip_group_check=True)
                        te.matmul(out.rearrange("p (r q) -> p r q", r=2)[:, :, P:S], c.identb[:, :], c.mask[:, 0:2, :],
                                  start=False, stop=True, skip_group_check=True).then_inc(pre_done, 1)

                def scores_by_key(u):
                    s, out, quad, w = k, pm[u % 2], u // 3, u % 3
                    if u == 0:
                        wait(pe, m_in[s], dma_count(b, NQ)(s))
                        if isinstance(b, int) and b < NQ:
                            pe.wait_ge(selected, b + 2)
                    wait(pe, exped, b * NP + (u - 1))
                    if w < 2:
                        for r in range(2):
                            last = te.matmul(out[:, r * S:(r + 1) * S], kb[s][:, 2 * quad + w, r, 0:P], qs[s][:, 2 * quad + w, :],
                                             start=True, stop=True)
                    else:
                        for j in range(4):
                            last = te.matmul(out[:, j * P:(j + 1) * P], kb[s][:, 2 * quad + j // 2, j % 2, P:S],
                                             qs[s][:, 2 * quad + j // 2, P:S], start=True, stop=True)
                    last.then_inc(main_done, 1)

                def times_v(n, s, u):
                    quad, w, src = u // 3, u % 3, pt[u % RING]
                    if u == 0:
                        wait(pe, v_out, n + 1)
                        wait(pe, ot_out, n * 2 - 1)
                    if u == 6:
                        wait(pe, ot_out, n * 2)
                    wait(pe, masked, n * NP + (u + 1))
                    for i in range(2 if w < 2 else 4):
                        j = 2 * w + i if w < 2 else i
                        cols = S if w < 2 else P
                        last = te.matmul(po[32 * j:32 * j + 32, (quad + 1) * S - cols:(quad + 1) * S],
                                         vp[s][:, w // 2, 4 * quad + j, :], src[:, i * cols:(i + 1) * cols],
                                         start=(w < 2), stop=(w == 2), skip_group_check=True)
                    last.then_inc(pv_done, 1)

                def small(u):
                    if u == 0 and has(3):
                        wait(pe, xn_done, (b + 4) * TPB)
                        wait(pe, mt_out, b + 1)
                        if isinstance(b, int):
                            wait(pe, v_out, b + 3)
                        for j in range(TPB):
                            te.transpose(mi[0][:, j * P:(j + 1) * P], xn[(k + 1) % 2][:, j, :], c.ident[:, :]).then_inc(xt_tr, 1)
                    if u == 1 and has(-2):
                        wait(pe, xn2_done, (b - 1) * TPB)
                        for j in range(TPB):
                            te.transpose(mi[1][:, j * P:(j + 1) * P], xn2[k % 2][:, j, :], c.ident[:, :]).then_inc(x2t_tr, 1)
                    if u == 2 and has(3):
                        wait(pe, xt_out, b + 4)
                        te.matmul(mi[0][:, 0:S], c.wq[:, :], xt[(k + 1) % 2][:, :], start=True, stop=True)
                        te.matmul(mi[0][:, S:2 * S], c.wk[:, :], xt[(k + 1) % 2][:, :], start=True, stop=True).then_inc(qk_mm, 1)
                    if u == 3 and has(-2):
                        wait(pe, x2t_out, b - 1)
                        for j in range(TPB):
                            last = te.matmul(mi[1][:, j * E:(j + 1) * E], x2t[k % 2][:, j * P:(j + 1) * P], c.waff_t[:, :],
                                             start=True, stop=True)
                        last.then_inc(num_mm, 1)
                    if u == 4 and has(3):
                        wait(pe, r_done, b + 4)
                        for j in range(TPB):
                            last = te.matmul(mi[0][:, j * D:(j + 1) * D], xt[(k + 1) % 2][:, j * P:(j + 1) * P], c.wv[:, :],
                                             start=True, stop=True)
                        last.then_inc(v_mm, 1)
                    if u in (5, 6) and has(-1):
                        j = u - 5
                        wait(pe, ot_out, b * 2)
                        wait(pe, num_out, b - 1) if j == 0 else wait(pe, v_out, b + 4, B)
                        for quad in range(QUADS):
                            last = te.transpose(mi[1 - j][:, quad * P:(quad + 1) * P], ot[(k - 1) % 2][:, quad, j * P:(j + 1) * P],
                                                c.ident[:, :])
                        last.then_inc(otr, 1)
                    if u == 7 and has(-1):
                        wait(pe, on_done, b * TPB)
                        for j in range(TPB):
                            last = te.transpose(mi[1][:, j * P:(j + 1) * P], on[(k - 1) % 2][:, j, :], c.ident[:, :])
                        last.then_inc(ont_tr, 1)
                    if u == 9 and has(1):
                        wait(pe, mp_done, b + 2)
                        wait(pe, on_done, b * TPB)
                        wait(pe, v_out, b + 4, B)
                        pe.sem_inc(passed, 1)
                        for j in range(TPB):
                            last = te.transpose(mi[0].bitcast(BF16)[0:3 * H, j * P:(j + 1) * P],
                                                mp[(k + 1) % 2][:, j, :, :].rearrange("p t h -> p (t h)"), c.identb[:, :])
                        last.then_inc(mt_tr, 1)
                    if u == 8 and has(-1):
                        wait(pe, ont_out, b)
                        for j in range(TPB):
                            last = te.matmul(mi[1][:, j * D:(j + 1) * D], ont[(k - 1) % 2][:, j * P:(j + 1) * P], c.wproj[:, :],
                                             start=True, stop=True)
                        last.then_inc(proj_mm, 1)

                for u in range(NP):
                    for o, v in QUERY_TILES[u]:
                        if has(o):
                            scores_by_query(o, v)
                    if has(0):
                        scores_by_key(u)
                    if u >= LAG and has(0):
                        times_v(b, k, u - LAG)
                    if u < LAG and has(-1):
                        times_v(b - 1, (k - 1) % NQ, NP - LAG + u)
                    small(u)

            run(pe, turn)

        @blk.vector
        def _(dve):
            v = nc.vector
            dve.wait_ge(picked, 2)
            v.tensor_reduce(sel[:, :], pick[:, :, :], axis=AX.X, op=ALU.add).then_inc(selected, 1)

            def statistics(n, x, bns, var, bnd, mv, done, keep):
                for j in range(TPB):
                    v.bn_stats(bns[:, j, :], x[:, j, 0:D]).then_inc(bnd, 1)
                for j in range(TPB):
                    wait(dve, bnd, n * TPB + (j + 1))
                    dve.sem_inc(passed, 1)
                    v.bn_aggr(x[:, j, D:D + 2], bns[:, j, :]).then_inc(mv, 1)
                wait(dve, mv, n * TPB + TPB)
                if keep:
                    v.tensor_copy(var[:, :, 1], x[:, :, D + 1])
                v.tensor_scalar(var[:, :, 0] if keep else var[:, :], x[:, :, D + 1], LN_EPS, None, ALU.add).then_inc(done, 1)

            def normalise(out, x, done):
                for j in range(TPB):
                    v.tensor_scalar(out[:, j, :], x[:, j, 0:D], x[:, j, D:D + 1], x[:, j, D + 1:D + 2],
                                    ALU.subtract, ALU.mult).then_inc(done, 1)

            def turn(b, k, has):
                if isinstance(b, int) and b < 0:
                    v.memset(kb[b + NQ][0:ROWS, :, :, :].bitcast(F32), 0.0).then_inc(kb_zero, 1)
                for u in range(NP):
                    for o, w in QUERY_TILES[u]:
                        if has(o):
                            n, q = b + o, (k + o) % 2
                            wait(dve, pre_done, n * NP + (w + 1))
                            if w == 0:
                                wait(dve, mp_done, n - 1)
                            if w < 4:
                                out = mx[q][:, 0, :, 2 * w:2 * w + 2].rearrange("p r g -> p g r")
                                src = pp[w % 2].rearrange("p (g r q) -> p g r q", g=2, r=2)
                            else:
                                out, src = mx[q][:, 1, :, w - 4], pp[w % 2].rearrange("p (r q) -> p r q", r=2)
                            v.tensor_reduce(out, src, axis=AX.X, op=ALU.max).then_inc(maxed, 1)
                    if u == 0 and has(-2):
                        wait(dve, rstd2, b - 1)
                        wait(dve, x2t_tr, (b - 3) * TPB)
                        normalise(xn2[k % 2], x2[k % 2], xn2_done)
                    if u == 3 and has(3):
                        h = (k + 1) % 2
                        wait(dve, a_done, b + 4)
                        wait(dve, part_done, b + 2)
                        v.tensor_tensor(rest[h][:, :].rearrange("p (a n) -> p a n", a=2), mi[0].rearrange("p (a n) -> p a n", a=2), part[h][:, 0:6:5, :],
                                        ALU.subtract).then_inc(r_done, 1)
                    if u in (5, 6) and has(-1):
                        q, j = (k - 1) % 2, u - 5
                        wait(dve, otr, (b - 1) * TPB + (j + 1))
                        rows = mi[1 - j].rearrange("p (h w) -> p h w", w=32)
                        v.reciprocal(rden[j][:, :], rows[:, :, HD]).then_inc(rd, 1)
                        wait(dve, rd, (b - 1) * TPB + (j + 1))
                        v.tensor_tensor(on[q][:, j, :].rearrange("p (h d) -> p h d", d=HD), rows[:, :, 0:HD],
                                        rden[j][:, :].unsqueeze(2).to_broadcast([P, H, HD]), ALU.mult).then_inc(on_done, 1)
                    if u == 7 and has(4):
                        wait(dve, xa_in[k % 2], dma_count(b + 4, 2)(k))
                        statistics(b + 4, xa[k % 2], bn[k % 2], vare[k % 2], bnd1, mv1, var1, False)
                    if u == 10 and has(4):
                        wait(dve, rstd1, b + 5)
                        wait(dve, xt_tr, (b + 3) * TPB)
                        normalise(xn[k % 2], xa[k % 2], xn_done)
                    if u == 9 and has(-1):
                        q = (k - 1) % 2
                        wait(dve, proj_mm, b)
                        wait(dve, xr_in[q], dma_count(b - 1, 2)(q))
                        wait(dve, row_out[q], dma_count(b - 3, 2)(q))
                        wait(dve, xnorm_done, b - 2)
                        v.tensor_tensor(x2[q][:, :, 0:D], mi[1][:, 0:TPB * D].rearrange("p (j d) -> p j d", d=D), xr[q][:, :, :],
                                        ALU.add).then_inc(x2_done, 1)
                        wait(dve, x2_done, b)
                        statistics(b - 1, x2[q], bn2[q], vare2[q], bnd2, mv2, var2, True)

            run(dve, turn)


def macaron(nc, io, out):
    ctx = ExitStack()
    with ctx:
        m = Mem(nc, ctx)
        c = consts(nc, m)
        io["rows"] = nc.dram_tensor("rows", (T, XW), F32, kind="Internal").ap()
        x1 = nc.dram_tensor("x1", (T, D), F32, kind="Internal").ap()
        preamble(nc, m, io, c)
        token_stats(nc, m, io, c, io["x"])
        route(nc, m, c, "r1")
        experts(nc, m, io, c, "e1", x1)
        attention(nc, m, io, c, x1)
        route(nc, m, c, "r2")
        experts(nc, m, io, c, "e2", out)


_INS = {
    "x": ("L0_attn_batch", (T, D)),
    "wqkv": ("L0_attn_W_qkv", (D, 3 * D)),
    "uqkv": ("L0_attn_u_qkv", (3 * D,)),
    "sqkv": ("L0_attn_sigma_qkv", (1,)),
    "wproj": ("L0_attn_W_proj", (D, D)),
    "uproj": ("L0_attn_u_proj", (D,)),
    "sproj": ("L0_attn_sigma_proj", (1,)),
    "waff": ("L0_ffn_waff", (E, D)),
    "w1": ("L0_ffn_W1", (E, D, F)),
    "b1": ("L0_ffn_b1", (E, F)),
    "w2": ("L0_ffn_W2", (E, F, D)),
    "b2": ("L0_ffn_b2", (E, D)),
    "thr": ("L0_ffn_affinity_threshold", (1,)),
}


def kernel(**inputs):
    import concourse.bacc as _bacc
    from concourse.bass_utils import run_bass_kernel_spmd as _run

    nc = _bacc.Bacc("TRN2", target_bir_lowering=False, num_devices=1)
    arrays, io = {}, {}
    for short, (name, shape) in _INS.items():
        a = np.ascontiguousarray(inputs[name]).reshape(shape)
        arrays[f"in_{short}_dram"] = a
        io[short] = nc.dram_tensor(f"in_{short}_dram", shape, mybir.dt.from_np(a.dtype), kind="ExternalInput").ap()
    out = nc.dram_tensor("out_0_dram", (T, D), F32, kind="ExternalOutput").ap()
    macaron(nc, io, out)
    r = _run(nc, [arrays], core_ids=[0])
    return r.results[0]["out_0_dram"].reshape(B, S, D)
```
